# Optimizing a Trainium2 kernel written in Bass

```python
import numpy as np
import jax
import jax.numpy as jnp

def _softmax(x, axis=-1):
    return jax.nn.softmax(x, axis=axis)

def _gelu(x):
    return jax.nn.gelu(x, approximate=True)

def _silu(x):
    return jax.nn.silu(x)

def _sigmoid(x):
    return jax.nn.sigmoid(x)

def _layernorm(x, axis=-1, eps=1e-05):
    m = jnp.mean(x, axis=axis, keepdims=True)
    v = jnp.var(x, axis=axis, keepdims=True)
    return (x - m) / jnp.sqrt(v + eps)

def _scatter_add(tgt, idx, src, axis=0):
    return tgt.at[idx].add(src)

def _segment_sum(src, seg, n):
    return jax.ops.segment_sum(src, seg, n)
kernel_name = 'mk_vit_tower_d1_tok_img768_r4_b78b77'

def setup_inputs(seed: int=0):
    np.random.seed(seed)
    _w = jnp.asarray

    def _rec_inputs():
        import jax
        import jax.numpy as jnp
        _rk = jax.random.key(seed)
        x = -0.000147625 + 0.999875 * jax.random.normal(jax.random.fold_in(_rk, 1), (64, 12, 224, 224), jnp.float32)
        return x
    x = _rec_inputs()

    def _L0_tok_setup():
        import jax, jax.numpy as jnp
        import numpy as np
        IMG = 224
        PATCH = 16
        EMBED = 192
        C = 12
        B = 64
        key = jax.random.key(seed)
        k1, k2 = jax.random.split(key)
        x = jax.random.normal(k1, (B, C, IMG, IMG), dtype=jnp.float32)
        channel_weights = jax.random.normal(k2, (C, EMBED), dtype=jnp.float32)
        return {'x': x, 'channel_weights': channel_weights}
    _L0_tok_all = _L0_tok_setup()
    _L0_tok_in = {k: v for k, v in _L0_tok_all.items() if k in ('channel_weights',)}
    del _L0_tok_all

    def _L0_attn_setup():
        import jax, jax.numpy as jnp
        import numpy as np
        import math
        D_MODEL = 192
        N_HEADS = 12
        B, L = (2, 512)
        ALPHA = 0.3
        key = jax.random.key(seed)
        ks = jax.random.split(key, 7)
        s = 0.02
        return {'x': jax.random.normal(ks[0], (B, L, D_MODEL), dtype=jnp.float32), 'Wqkv_w': jax.random.normal(ks[1], (D_MODEL, 3 * D_MODEL), dtype=jnp.float32) * s, 'Wqkv_b': jax.random.normal(ks[2], (3 * D_MODEL,), dtype=jnp.float32) * s, 'sel_w': jax.random.normal(ks[3], (D_MODEL, 2), dtype=jnp.float32) * s, 'sel_b': jax.random.normal(ks[4], (2,), dtype=jnp.float32) * s, 'out_w': jax.random.normal(ks[5], (D_MODEL, D_MODEL), dtype=jnp.float32) * s, 'out_b': jax.random.normal(ks[6], (D_MODEL,), dtype=jnp.float32) * s, 'temperature': jnp.ones((1,), dtype=jnp.float32) * (math.sqrt(D_MODEL) * ALPHA)}
    _L0_attn_all = _L0_attn_setup()
    _L0_attn_in = {k: v for k, v in _L0_attn_all.items() if k in ('Wqkv_w', 'Wqkv_b', 'sel_w', 'sel_b', 'out_w', 'out_b', 'temperature')}
    del _L0_attn_all

    def _L0_ffn_setup():
        import jax, jax.numpy as jnp
        import numpy as np
        B, S, D_IN, D_HID, D_OUT = (32, 128, 192, 768, 192)
        key = jax.random.key(seed)
        k1, k2, k3, k4 = jax.random.split(key, 4)
        init_k = float(np.sqrt(1.0 / D_IN))
        init_k2 = float(np.sqrt(1.0 / D_HID))
        x = jax.random.normal(k1, (B, S, D_IN), dtype=jnp.float32)
        in_weight = jax.random.uniform(k2, (D_HID, D_IN), dtype=jnp.float32, minval=-init_k, maxval=init_k)
        in_bias = jax.random.uniform(k3, (D_HID,), dtype=jnp.float32, minval=-init_k, maxval=init_k)
        out_weight = jax.random.uniform(k4, (D_HID, D_OUT), dtype=jnp.float32, minval=-init_k2, maxval=init_k2)
        return {'x': x, 'in_weight': in_weight, 'in_bias': in_bias, 'out_weight': out_weight}
    _L0_ffn_all = _L0_ffn_setup()
    _L0_ffn_in = {k: v for k, v in _L0_ffn_all.items() if k in ('in_weight', 'in_bias', 'out_weight')}
    del _L0_ffn_all
    return {'x': x, 'L0_tok_channel_weights': _L0_tok_in['channel_weights'], 'L0_attn_Wqkv_w': _L0_attn_in['Wqkv_w'], 'L0_attn_Wqkv_b': _L0_attn_in['Wqkv_b'], 'L0_attn_sel_w': _L0_attn_in['sel_w'], 'L0_attn_sel_b': _L0_attn_in['sel_b'], 'L0_attn_out_w': _L0_attn_in['out_w'], 'L0_attn_out_b': _L0_attn_in['out_b'], 'L0_attn_temperature': _L0_attn_in['temperature'], 'L0_ffn_in_weight': _L0_ffn_in['in_weight'], 'L0_ffn_in_bias': _L0_ffn_in['in_bias'], 'L0_ffn_out_weight': _L0_ffn_in['out_weight']}

def reference(x, L0_tok_channel_weights, L0_attn_Wqkv_w, L0_attn_Wqkv_b, L0_attn_sel_w, L0_attn_sel_b, L0_attn_out_w, L0_attn_out_b, L0_attn_temperature, L0_ffn_in_weight, L0_ffn_in_bias, L0_ffn_out_weight):
    import jax
    import jax.numpy as jnp

    def _L0_tok_ref(x, channel_weights):
        import jax, jax.numpy as jnp
        import numpy as np
        IMG = 224
        PATCH = 16
        EMBED = 192
        C = 12
        B = 64
        Bb, Cc, H, W = x.shape
        K = PATCH
        n = H // K
        pooled = x.reshape(Bb, Cc, n, K, n, K).sum(axis=(3, 5))
        out = jnp.einsum('bcij,ce->bije', pooled, channel_weights)
        return out.reshape(Bb, n * n, EMBED)

    def _L0_attn_ref(x, Wqkv_w, Wqkv_b, sel_w, sel_b, out_w, out_b, temperature):
        import jax, jax.numpy as jnp
        import numpy as np
        import math
        D_MODEL = 192
        N_HEADS = 12
        B, L = (2, 512)
        ALPHA = 0.3
        b, l, d = x.shape
        h = N_HEADS
        hd = d // h
        qkv = (x @ Wqkv_w + Wqkv_b).reshape(b, l, 3, h, hd)
        q, k_, v = (qkv[:, :, 0], qkv[:, :, 1], qkv[:, :, 2])
        scale = 1.0 / math.sqrt(hd)
        scores = jnp.einsum('bthd,bshd->bhts', q, k_ * scale)
        causal_mask = jnp.triu(jnp.full((l, l), -10000.0, dtype=scores.dtype), 1)
        attn = jax.nn.softmax(scores + causal_mask, axis=-1)
        ctx = jnp.einsum('bhts,bshd->bthd', attn, v).reshape(b, l, d)
        attn_output = ctx @ out_w + out_b
        selection = jax.nn.softmax((x @ sel_w + sel_b) / temperature, axis=-1)[..., 1:]
        k_sel = int(math.ceil(math.sqrt(l)))
        _, idx = jax.lax.top_k(selection[..., 0], k_sel)
        gated = attn_output * selection
        src = jnp.take_along_axis(gated, idx[..., None], axis=1)
        y = jax.vmap(lambda xb, ib, sb: xb.at[ib].add(sb))(x, idx, src)
        return y

    def _L0_ffn_ref(x, in_weight, in_bias, out_weight):
        import jax, jax.numpy as jnp
        import numpy as np
        B, S, D_IN, D_HID, D_OUT = (32, 128, 192, 768, 192)
        lead = x.shape[:-1]
        xt = x.reshape(-1, in_weight.shape[1])
        h = jax.nn.gelu(jnp.einsum('td,hd->th', xt, in_weight) + in_bias, approximate=False)
        out = jnp.einsum('th,ho->to', h, out_weight)
        return out.reshape(*lead, out_weight.shape[1])
    h = _L0_tok_ref(x, L0_tok_channel_weights)
    h = h + _L0_attn_ref(_layernorm(h, axis=-1), L0_attn_Wqkv_w, L0_attn_Wqkv_b, L0_attn_sel_w, L0_attn_sel_b, L0_attn_out_w, L0_attn_out_b, L0_attn_temperature)
    h = h + _L0_ffn_ref(_layernorm(h, axis=-1), L0_ffn_in_weight, L0_ffn_in_bias, L0_ffn_out_weight)
    return h

_drawn_inputs = setup_inputs


def setup_inputs(seed=0):
    import zlib

    import numpy as np

    out = dict(_drawn_inputs(seed))
    spreads = {}
    factors = {'L0_attn_Wqkv_w': 35.547,
     'L0_attn_Wqkv_b': 64.0,
     'L0_attn_sel_w': 34.818,
     'L0_attn_sel_b': 64.0,
     'L0_attn_out_w': 34.98,
     'L0_attn_out_b': 64.0,
     'L0_ffn_in_weight': 8.0,
     'L0_ffn_in_bias': 23.657,
     'L0_ffn_out_weight': 8.0}
    for name, (base, spread) in spreads.items():
        noise = np.random.default_rng([zlib.crc32(name.encode()), seed]).standard_normal(out[name].shape)
        drawn = base * np.exp(spread * noise) if base else spread * noise
        out[name] = jnp.asarray(drawn.astype(out[name].dtype))
    for name, factor in factors.items():
        out[name] = (out[name] * factor).astype(out[name].dtype)
    return out
```

```python
import numpy as np
import concourse.bass as bass
from concourse import mybir
from contextlib import ExitStack

B, C, IMG, PATCH, D, HEADS, HID = 64, 12, 224, 16, 192, 12, 768
N = IMG // PATCH
T = N * N
HD = D // HEADS
KSEL = int(np.ceil(np.sqrt(T)))
GB = 4
NG = B // GB
BC = GB * C
SLOTS = GB * KSEL
HALF = T // 2
GT = GB * T
Z1 = BC
NW_IN = 1 + 2 * GB + 8 + 12
ZR = 64
PR = ZR
FR = PR + BC
W1 = C + 1
PAIRS = 8
PART_OF = [0, 0, 0, 1, 1, 1, 2, 2]
WPART_OF = [0, 1, 2, 0, 1, 2, 0, 1]
SK = PAIRS * W1
DH = D // 2
HP = HEADS // 2
ROWS = 2 * SLOTS
HT = HID // 128
FT = 7
FP = T // FT
OT = GB * FP
QR = 4
QB = QR * IMG
NQ = GB * C * IMG // QR // 128
TQ = 3
XT = NQ // TQ
NX = 4
EPS = 1e-5
NEG = -10000.0

COLS = {}
_at = 0
for _name, _n in [("ident", 128), ("same", FR), ("tmk", FR + GB * 2 * W1), ("tmm", FR + GB * 2 * W1),
                  ("tw", GB * 2 * W1), ("bm2", SLOTS), ("bmzy", SLOTS), ("e4", SLOTS), ("bmt", GB),
                  ("r1", 1), ("iota14", KSEL), ("iota", T), ("tpos", 2), ("e13", 1), ("mh", 1),
                  ("mm", 1), ("ml", 1), ("bsel", GB), ("ones", T), ("f0", T)]:
    COLS[_name] = (_at, _at + _n)
    _at += _n
NCOLS = _at


def constants():
    k = np.zeros((128, NCOLS), np.float32)

    def col(name):
        a, b = COLS[name]
        return k[:, a:b]

    col("ident")[:] = np.eye(128)
    for b in range(GB):
        z, p = slice(b * C, b * C + C), slice(PR + b * C, PR + b * C + C)
        s = slice(b * KSEL, b * KSEL + KSEL)
        v = FR + b * 2 * W1
        col("same")[p, p] = 1
        for c in range(C):
            col("tmk")[b * C + c, v + W1 + c] = 1
            col("tmk")[PR + b * C + c, v + W1 + c] = 1
            col("tw")[PR + b * C + c, b * 2 * W1 + c] = 1
        col("tmk")[Z1, v + C] = 1
        col("tmm")[p, v + 2 * W1 - 1] = 1
        col("bm2")[z, s] = 1
        col("bm2")[ZR + b * C:ZR + b * C + C, s] = 1
        col("bmzy")[z, s] = 1
        col("bmzy")[p, s] = 1
        col("e4")[b, s] = 1
        col("bmt")[s, b] = 1
        col("r1")[s, 0] = np.arange(1, KSEL + 1)
        col("bsel")[z, b] = 1
    col("tmk")[:FR, :FR] = np.eye(FR)
    col("bm2")[[Z1, ZR + Z1]] = 1
    col("bmzy")[Z1] = 1
    col("bsel")[Z1] = 1
    col("iota14")[:] = np.arange(1, KSEL + 1)
    col("iota")[:] = np.arange(T)
    col("tpos")[:, 0] = np.arange(128)
    col("tpos")[:, 1] = HALF + np.arange(128)
    for n in range(PAIRS):
        col("e13")[n * W1 + C] = 1
        col(["mh", "mm", "ml"][WPART_OF[n]])[n * W1:n * W1 + W1] = 1
    col("ones")[:] = 1
    col("f0")[Z1] = 1
    return k


class Steps:

    def __init__(self, sem, names):
        self.sem, self.names = sem, names.split()

    def at(self, group, name):
        return group * len(self.names) + (self.names.index(name) + 1)


def program(nc, x, cw, wqkv, bqkv, selw, selb, ow, ob, temp, w1t, b1, w2, consts, e48, e13r, out):
    f32, bf16 = mybir.dt.float32, mybir.dt.bfloat16
    ALU, ACT, AX = mybir.AluOpType, mybir.ActivationFunctionType, mybir.AxisListType

    xg = x.rearrange("(g b) c h w -> g (b c h w)", b=GB).rearrange("g (p q) -> g p q", p=128)
    og = out.rearrange("(g b) (t i) e -> g (b t) (i e)", b=GB, i=FT)
    scratch = nc.dram_tensor("patch_sums", (NG, 128, NQ * N), f32, kind="Internal").ap()
    sums_in = scratch.rearrange("g p q -> g (p q)").rearrange("g (r q) -> g r q", r=BC)

    with ExitStack() as ctx:
        def sb(name, shape, dt=f32):
            return ctx.enter_context(nc.sbuf_tensor(name, shape, dt))

        def ps(name):
            return ctx.enter_context(nc.psum_tensor(name, [128, 512], f32))

        def sem(name):
            return ctx.enter_context(nc.semaphore(name))

        K = sb("K", [128, NCOLS])

        def kc(name, rows=128):
            a, b = COLS[name]
            return K[0:rows, a:b]

        WR, BW, WcR = sb("WR", [FR, D]), sb("BW", [FR, D]), sb("WcR", [FR, D])
        WS, WcS = sb("WS", [SK, D]), sb("WcS", [SK, D])
        mean_r, mean_s = sb("mean_r", [FR, 1]), sb("mean_s", [SK, 1])
        WT4, WST = sb("WT4", [DH + 1, 2, FR]), sb("WST", [DH + 1, 2, SK])
        Wsel = sb("Wsel", [DH + 1, 2, 2])
        W1T = sb("W1T", [DH + 1, 2, HID])
        W2 = sb("W2", [128, HT, D])
        OB = sb("OB", [SLOTS, D])
        temp_sb = sb("temp_sb", [ZR, 1])
        A4 = sb("A4", [ZR, HEADS, ZR])
        B2 = sb("B2", [128, HP, D])
        CF = sb("CF", [FR, FR])
        TMR = sb("TMR", [FR, FR + GB * 2 * W1])
        selM2, selM = sb("selM2", [ZR, 2]), sb("selM", [ZR, 2, GB])
        sel_raw, sel_d = sb("sel_raw", [ZR, 2]), sb("sel_d", [ZR, 1])
        M1S, RS = sb("M1S", [SK, HID], bf16), sb("RS", [SK, D], bf16)
        identb = sb("identb", [128, 128], bf16)

        X = sb("X", [128, NX, TQ * QB])
        R = sb("R", [128, 2, NQ * N])
        Praw = sb("Praw", [FR, 2, NQ * 128 * N // BC])
        Pt = sb("Pt", [FR, 2, T])
        FM = [sb(f"FM{i}", [FR, T]) for i in range(2)]
        V = sb("V", [FR, T])
        sc = {n: sb(n, [FR, T]) for n in ("ve", "rstd", "t1", "t2", "s2", "s3", "r2", "al")}
        WT = sb("WT", [FR, T])
        Dm, Ex2 = sb("Dm", [GB, 2, T]), sb("Ex2", [GB, 2, T])
        den = sb("den", [GB, T])
        sel, sl1, sl2 = sb("sel", [GB, T + 4]), sb("sl1", [GB, T + 4]), sb("sl2", [GB, T + 4])
        m8a, m8b = sb("m8a", [GB, 8]), sb("m8b", [GB, 8])
        mask, cum, srow = sb("mask", [GB, T]), sb("cum", [GB, T]), sb("srow", [GB, T])
        Sg = [sb(f"S{i}", [HALF, 2, 2, SLOTS]) for i in range(2)]
        keep = sb("keep", [HALF, 2, GB])
        ST = [sb(f"ST{i}", [SLOTS, GB, T]) for i in range(4)]
        F = [sb(f"F{i}", [HALF, 2, FR]) for i in range(2)]
        v26, d1, d2 = (sb(n, [HALF, 4 * GB, W1]) for n in ("v26", "d1", "d2"))
        SP = sb("SP", [HALF, 4 * GB, PAIRS, W1], bf16)
        Stk1 = [sb(f"Stk1_{i}", [SK, GT], bf16) for i in range(2)]
        Stk2 = [sb(f"Stk2_{i}", [SK, GT], bf16) for i in range(4)]
        act_sb = [sb(f"act{i}", [128, HT, GT]) for i in range(2)]
        spare = [t[:, :, :].rearrange("p h t -> p (h t)") for t in act_sb]
        Wqkv = spare[0][0:DH + 1, 0:6 * D].rearrange("p (k n) -> p k n", k=2)
        Wo = spare[0][0:HD, 6 * D:(6 + HEADS) * D].rearrange("p (h e) -> p h e", h=HEADS)
        MqT, MkT, MvT = (spare[1][0:HD, n * HEADS * ZR:(n + 1) * HEADS * ZR].rearrange("p (h c) -> p h c", h=HEADS) for n in range(3))
        M1f, M1r = (spare[1][0:SK, n * HID:(n + 1) * HID] for n in (3, 4))
        M1h = spare[1][0:SK, 5 * HID:5 * HID + HID // 2].bitcast(bf16)
        ZY = sb("ZY", [FR, SLOTS])
        RM = sb("RM", [ROWS, T])
        UB = sb("UB", [ZR, HP, 2, SLOTS])
        Sm = sb("Sm", [ROWS, HP, T])
        mx, nm, rsum, rinv = (sb(n, [ROWS, HP]) for n in ("mx", "nm", "rsum", "rinv"))
        ET = sb("ET", [HALF, 2 * HP, ROWS])
        GN = sb("GN", [ROWS, HP, ZR])
        G2 = sb("G2", [128, HP, SLOTS])
        dmin, dexp, dden, dsel = sb("dmin", [SLOTS, 2]), sb("dexp", [SLOTS, 2]), sb("dden", [SLOTS, 1]), sb("dsel", [SLOTS, 1])
        AO, h1, xh = sb("AO", [SLOTS, D]), sb("h1", [SLOTS, D]), sb("xh", [SLOTS, D])
        bst, mv, vrs, rst = sb("bst", [SLOTS, 6]), sb("mv", [SLOTS, 2]), sb("vrs", [SLOTS, 1]), sb("rst", [SLOTS, 1])
        mhalf, rden, rdden = sb("mhalf", [FR, T]), sb("rden", [GB, T]), sb("rdden", [SLOTS, 1])
        XH = sb("XH", [DH + 1, 2, SLOTS])
        actS = sb("actS", [128, HT, SLOTS])
        OS = [sb(f"OS{i}", [SLOTS, D]) for i in range(2)]
        obuf = [sb(f"obuf{i}", [OT, FT, D]) for i in range(2)]

        psF = [ps("psF0"), ps("psF1")]
        psO, psA, psB = ps("psO"), ps("psA"), ps("psB")
        psS = ctx.enter_context(nc.psum_tensor("psS", [128, 3, 512], f32))

        w_in, w_zero = sem("weights_loaded"), sem("weights_zeroed")
        x_in = [sem(f"x_loaded{k}") for k in range(NX)]
        sums_out = [sem(f"sums_stored{k}") for k in range(2)]
        sums_back = [sem(f"sums_loaded{k}") for k in range(2)]
        y_out = [sem(f"out_stored{k}") for k in range(2)]
        passed = sem("waits_passed")
        tiles = [f"x{k}" for k in range(XT)]
        pool_L = Steps(sem("pool_halved_x"), " ".join(tiles))
        dve_L = Steps(sem("dve_summed_x"), " ".join(tiles))
        pool_A = Steps(sem("pool_norm_steps"), "q01 q23 p rstd r2")
        pe_A = Steps(sem("pe_norm_steps"), "cp var lg tm st tr1 tr2")
        dve_A = Steps(sem("dve_norm_steps"), "v ve t1 z t2 s2 s3 d al w den rden sel m8a mr1 m8b fx mr2 mk cs sr S S2 kp ST v26 H d1 M d2 L k1")
        act_A = Steps(sem("act_norm_steps"), "e F k2")
        pool_S = Steps(sem("pool_chosen_steps"), "rs")
        pe_S = Steps(sem("pe_chosen_steps"), "ga u sc et g gt at xt f1 f2")
        dve_S = Steps(sem("dve_chosen_steps"), "zy rm ub0 ub1 sm mx nm ri gn g0 g1 dm ao dn rn sv h1 bs ba vr xh XH os")
        act_S = Steps(sem("act_chosen_steps"), "e0 e1 e2 e3 e4 e5 t0 t1 t2 se ge")
        ffn = [f"n{k}" for k in range(2 * HT)]
        outs = [f"o{k}" for k in range(FT)]
        pe_F1 = Steps(sem("pe_ffn1"), " ".join(ffn))
        act_F1 = Steps(sem("act_gelu"), " ".join(ffn))
        pe_F2 = Steps(sem("pe_ffn2"), " ".join(outs))
        act_F2 = Steps(sem("act_out"), " ".join(outs))
        pe_W = Steps(sem("pe_weights"), "wt ws c sel q k v a4 b2 m1")
        splits = "h r1 ah m r2 am l al"
        dve_W = Steps(sem("dve_weights"), "wr0 ws0 wt0 ini idb mr mr2 wcr tmr bw0 bw1 ms ms2 wcs rf wt ws cf raw sd sd2 s1 s0 sm1 sm0 q k v a4 b2 m1 "
                      + " ".join(f"{n}{t}" for t in "MR" for n in splits.split()))
        block = ctx.enter_context(nc.Block())

        def periods(engine, body):
            for p in range(4):
                body(p, p, 0)
            with engine.Fori(0, 3) as i:
                for k in range(4, 8):
                    body(i * 4 + k, k % 4, i + k // 4)
            for p in range(16, NG + 3):
                body(p, p % 4, p // 4)

        def by_itself(engine):
            engine.sem_inc(passed, 1)

        def active(p, lag):
            return not isinstance(p, int) or 0 <= p - lag < NG

        def exists(group):
            return not isinstance(group, int) or group >= 0

        def landed(group, par):
            return (group - par) * 8 + 16

        def tile_of(ap, i):
            return ap.rearrange("p (m i) -> p i m", i=FT)[:, i, :]

        @block.sync
        def _(sp):
            sp.dma_start(K[:, :], consts).then_inc(w_in, 16)
            sp.wait_ge(dve_W.sem, dve_W.at(0, "wt0"))
            n = 1
            for b in range(GB):
                sp.dma_start(WR[b * C:b * C + C, :], cw).then_inc(w_in, 16)
                sp.dma_start(WR[PR + b * C:PR + b * C + C, :], cw).then_inc(w_in, 16)
                n += 2
            for k in range(PAIRS):
                sp.dma_start(WS[k * W1:k * W1 + C, :], cw).then_inc(w_in, 16)
                n += 1
            for dst, src in [
                    (Wqkv[0:DH, :, :], wqkv.rearrange("(k d) n -> d k n", k=2)), (Wqkv[DH:DH + 1, 0, :], bqkv),
                    (Wsel[0:DH, :, :], selw.rearrange("(k d) n -> d k n", k=2)), (Wsel[DH:DH + 1, 0, :], selb),
                    (Wo[:, :, :], ow.rearrange("(h d) e -> d h e", h=HEADS)),
                    (W1T[0:DH, :, :], w1t.rearrange("(k d) n -> d k n", k=2)), (W1T[DH:DH + 1, 0, :], b1),
                    (W2[:, :, :], w2.rearrange("(h p) e -> p h e", h=HT)),
                    (OB[:, :], ob.to_broadcast([SLOTS, D])),
                    (temp_sb[:, :], temp.to_broadcast([ZR, 1])),
                    (WT4[DH:DH + 1, 0, :], e48), (WST[DH:DH + 1, 0, :], e13r)]:
                sp.dma_start(dst, src).then_inc(w_in, 16)
                n += 1
            assert n == NW_IN, n

            def body(p, u, q):
                for k in range(XT):
                    if active(p, 0):
                        if exists(p if k >= NX else p - 1):
                            sp.wait_ge(dve_L.sem, dve_L.at(p if k >= NX else p - 1, f"x{(k - NX) % XT}"))
                        sp.dma_start(X[:, (XT * u + k) % NX, :], xg[bass.ds(p, 1), :, k * TQ * QB:(k + 1) * TQ * QB]
                                     .rearrange("o p q -> (o p) q")).then_inc(x_in[(XT * u + k) % NX], 16)
                    if k == NX - 1 and active(p, 1):
                        sp.wait_ge(dve_L.sem, dve_L.at(p - 1, f"x{XT - 1}"))
                        sp.dma_start(scratch[bass.ds(p - 1, 1)].rearrange("o p q -> (o p) q"),
                                     R[:, (u - 1) % 2, :]).then_inc(sums_out[(u - 1) % 2], 16)
                    if k == NX and active(p, 1):
                        g, r = p - 1, (u - 1) % 2
                        sp.wait_ge(sums_out[r], landed(g, r))
                        if exists(g - 2):
                            sp.wait_ge(pool_A.sem, pool_A.at(g - 2, "q23"))
                        sp.dma_start(Praw[PR:FR, r, :], sums_in[bass.ds(g, 1)].rearrange("o p q -> (o p) q")
                                     ).then_inc(sums_back[r], 16)

            periods(nc.sync, body)
            for r in range(2):
                sp.wait_ge(sums_out[r], landed(NG - 2 + r, r))
                sp.wait_ge(y_out[r], landed(NG - 2 + r, r))

        @block.gpsimd
        def _(pool):
            def body(p, u, q):
                for k in range(XT):
                    if active(p, 0):
                        b = (XT * u + k) % NX
                        pool.wait_ge(x_in[b], (q * XT + ((XT * u + k) // NX + 1)) * 16)
                        v = X[:, b, :].rearrange("p (q r w) -> p q r w", q=TQ, r=QR)
                        if k >= 2:
                            before(p, k)
                        pool.tensor_tensor(v[:, :, 0:2, :], v[:, :, 0:2, :], v[:, :, 2:4, :], ALU.add).then_inc(pool_L.sem, 1)
                    if 1 <= k <= 4 and active(p, 0):
                        pool.wait_ge(pool_L.sem, pool_L.at(p, f"x{k}"))
                    if k == 1 and active(p, 1):
                        sum_quarters(p - 1, (u - 1) % 2)
                    if k == 2 and active(p, 1):
                        root(p - 1, "ve", "rstd")
                    if k == 3 and active(p, 1):
                        root(p - 1, "s3", "r2")
                    if k == 4 and active(p, 2):
                        pool.wait_ge(dve_S.sem, dve_S.at(p - 2, "vr"))
                        pool.tensor_tensor(rst[:, :], vrs[:, :], mhalf[0:SLOTS, 0:1], ALU.pow).then_inc(pool_S.sem, 1)

            def before(p, k):
                if k <= 4 and active(p, 1):
                    pool.wait_ge(pool_A.sem, pool_A.at(p - 1, ["p", "rstd", "r2"][k - 2]))
                if k == 5 and active(p, 2):
                    pool.wait_ge(pool_S.sem, pool_S.at(p - 2, "rs"))

            def root(g, of, to):
                pool.wait_ge(dve_A.sem, dve_A.at(g, of))
                pool.tensor_tensor(sc[to][PR:FR, :], sc[of][PR:FR, :], mhalf[PR:FR, :], ALU.pow).then_inc(pool_A.sem, 1)

            def sum_quarters(g, r):
                pool.wait_ge(sums_back[r], landed(g, r))
                raw = Praw[PR:FR, r, :].rearrange("p (i q j) -> p q i j", i=N, q=4)
                t = Pt[PR:FR, :, :].rearrange("p k (i j) -> p k i j", i=N)
                pool.tensor_tensor(t[:, 0], raw[:, 0], raw[:, 1], ALU.add).then_inc(pool_A.sem, 1)
                pool.tensor_tensor(t[:, 1], raw[:, 2], raw[:, 3], ALU.add).then_inc(pool_A.sem, 1)
                pool.wait_ge(pool_A.sem, pool_A.at(g, "q23"))
                if exists(g - 2):
                    pool.wait_ge(pe_A.sem, pe_A.at(g - 2, "tm"))
                if exists(g - 2):
                    pool.wait_ge(dve_A.sem, dve_A.at(g - 2, "w"))
                pool.wait_ge(dve_W.sem, dve_W.at(0, "ini"))
                pool.tensor_tensor(FM[r][PR:FR, :], Pt[PR:FR, 0, :], Pt[PR:FR, 1, :], ALU.add).then_inc(pool_A.sem, 1)

            periods(nc.gpsimd, body)

        @block.tensor
        def _(pe):
            def weights():
                pe.wait_ge(dve_W.sem, dve_W.at(0, "wcs"))
                for k in range(2):
                    mm = pe.transpose(psA[0:DH, k * FR:k * FR + FR], WcR[:, k * DH:k * DH + DH], kc("ident")[0:FR, 0:FR])
                mm.then_inc(pe_W.sem, 1)
                for k in range(2):
                    mm = pe.transpose(psB[0:DH, k * SK:k * SK + SK], WcS[:, k * DH:k * DH + DH], kc("ident")[0:SK, 0:SK])
                mm.then_inc(pe_W.sem, 1)
                pe.wait_ge(dve_W.sem, dve_W.at(0, "ws"))
                for k in range(2):
                    mm = pe.matmul(psO[0:FR, 0:FR], WT4[0:DH, k, :], WT4[0:DH, k, :], start=(k == 0), stop=(k == 1))
                mm.then_inc(pe_W.sem, 1)

                def bias_first(k):
                    return slice(0, DH + 1) if k == 0 else slice(0, DH)

                for k in range(2):
                    mm = pe.matmul(psF[0][0:ZR, 0:2], WT4[bias_first(k), k, 0:ZR], Wsel[bias_first(k), k, :],
                                   start=(k == 0), stop=(k == 1))
                mm.then_inc(pe_W.sem, 1)
                pe.wait_ge(dve_W.sem, dve_W.at(0, "raw"))
                banks = [(psS[:, 0], psS[:, 1]), (psS[:, 2], psA[:, :]), (psB[:, :], psF[1][:, :])]
                for m in range(3):
                    for h in range(HEADS):
                        to = banks[m][h // HP][0:HD, (h % HP) * ZR:(h % HP) * ZR + ZR]
                        for k in range(2):
                            mm = pe.matmul(to, Wqkv[bias_first(k), k, m * D + h * HD:m * D + h * HD + HD],
                                           WT4[bias_first(k), k, 0:ZR], start=(k == 0), stop=(k == 1))
                    mm.then_inc(pe_W.sem, 1)
                pe.wait_ge(dve_W.sem, dve_W.at(0, "v"))
                for h in range(HEADS):
                    mm = pe.matmul((psA if h < HP else psB)[0:ZR, (h % HP) * ZR:(h % HP) * ZR + ZR],
                                   MqT[:, h, :], MkT[:, h, :], start=True, stop=True)
                mm.then_inc(pe_W.sem, 1)
                for h in range(HEADS):
                    j = h % HP
                    r = ZR * (h // HP)
                    mm = pe.matmul(psS[r:r + ZR, j // 2, (j % 2) * D:(j % 2) * D + D], MvT[:, h, :], Wo[:, h, :],
                                   start=True, stop=True)
                mm.then_inc(pe_W.sem, 1)
                pe.wait_ge(dve_W.sem, dve_W.at(0, "b2"))
                for n in range(2):
                    for k in range(2):
                        mm = pe.matmul((psA, psB)[n][0:SK, 0:HID // 2], WST[bias_first(k), k, :],
                                       W1T[bias_first(k), k, n * HID // 2:(n + 1) * HID // 2], start=(k == 0), stop=(k == 1))
                mm.then_inc(pe_W.sem, 1)

            def step_A(g, u, name):
                r = u % 2
                fm, h2 = FM[r], FR + GB * 2 * W1
                if name == "cp":
                    pe.wait_ge(pool_A.sem, pool_A.at(g, "p"))
                    if exists(g - 1):
                        pe.wait_ge(dve_A.sem, dve_A.at(g - 1, "k1"))
                    mm = pe.matmul(psA[0:FR, 0:T], CF[:, :], fm[:, :], start=True, stop=True)
                elif name == "var":
                    pe.wait_ge(dve_A.sem, dve_A.at(g, "v"))
                    mm = pe.matmul(psA[0:FR, T:2 * T], kc("same", FR), V[:, :], start=True, stop=True)
                elif name == "lg":
                    pe.wait_ge(dve_A.sem, dve_A.at(g, "s2"))
                    by_itself(pe)
                    for k in range(2):
                        mm = pe.matmul(psA[0:GB, k * T:k * T + T], selM[:, k, :], fm[0:ZR, :], start=True, stop=True)
                elif name == "tm":
                    pe.wait_ge(dve_A.sem, dve_A.at(g, "w"))
                    if exists(g - 1):
                        pe.wait_ge(act_A.sem, act_A.at(g - 1, "k2"))
                    for k in range(2):
                        pe.matmul(psB[0:HALF, k * h2:(k + 1) * h2], fm[:, k * HALF:(k + 1) * HALF], TMR[:, :],
                                  start=True, stop=False)
                        mm = pe.matmul(psB[0:HALF, k * h2 + FR:(k + 1) * h2], WT[:, k * HALF:(k + 1) * HALF],
                                       kc("tw", FR), start=False, stop=True)
                elif name == "st":
                    pe.wait_ge(dve_A.sem, dve_A.at(g, "sr"))
                    for k in range(2):
                        pe.matmul(psA[0:HALF, 400 + k * GB:400 + (k + 1) * GB], srow[:, k * HALF:(k + 1) * HALF],
                                  kc("ident")[0:GB, 0:GB], start=True, stop=True)
                    mm = pe.matmul(psA[0:SLOTS, 0:T], kc("e4", GB), srow[:, :], start=True, stop=True)
                else:
                    k = int(name[2]) - 1
                    pe.wait_ge(dve_A.sem, dve_A.at(g, "L"))
                    if k:
                        pe.wait_ge(act_A.sem, act_A.at(g, "F"))
                    to = (psA, psB)[k][:, :].bitcast(bf16)
                    for n in range(2 * GB):
                        c0 = (n % GB) * T + (n // GB) * HALF
                        mm = pe.transpose(to[0:SK, c0:c0 + HALF], SP[:, 2 * n + k, :, :].rearrange("p n c -> p (n c)"), identb[0:HALF, 0:HALF])
                mm.then_inc(pe_A.sem, 1)

            def step_S(g, u, name):
                r = u % 2
                if name == "ga":
                    pe.wait_ge(dve_A.sem, dve_A.at(g, "S2"))
                    pe.wait_ge(act_A.sem, act_A.at(g, "F"))
                    if exists(g - 1):
                        pe.wait_ge(dve_S.sem, dve_S.at(g - 1, "os"))
                    for k in range(2):
                        pe.matmul(psS[0:FR, 0, 0:SLOTS], F[r][:, k, :], Sg[r][:, k, 0, :],
                                  start=(k == 0), stop=(k == 1))
                    for k in range(2):
                        mm = pe.matmul(psS[0:ROWS, 0, ZR:ZR + 1],
                                       Sg[r][:, k, :, :].rearrange("p d s -> p (d s)"),
                                       kc("tpos", HALF)[:, k:k + 1], start=(k == 0), stop=(k == 1))
                elif name == "u":
                    pe.wait_ge(dve_S.sem, dve_S.at(g, "zy"))
                    by_itself(pe)
                    for h in range(HEADS):
                        mm = pe.matmul(psS[0:ZR, 1 + h // HP, (h % HP) * SLOTS:(h % HP + 1) * SLOTS], A4[:, h, :],
                                       ZY[0:ZR, :], start=True, stop=True)
                elif name == "sc":
                    pe.wait_ge(dve_S.sem, dve_S.at(g, "ub1"))
                    for j in range(HP):
                        mm = pe.matmul(psS[0:ROWS, j // 2, (j % 2) * T:(j % 2 + 1) * T],
                                       UB[:, j, :, :].rearrange("p k s -> p (k s)"), FM[r][0:ZR, :], start=True, stop=True)
                elif name == "et":
                    pe.wait_ge(act_S.sem, act_S.at(g, "e5"))
                    for n in range(2 * HP):
                        k, j = n // HP, n % HP
                        mm = pe.transpose(psS[0:HALF, n // 4, (n % 4) * ROWS:(n % 4 + 1) * ROWS],
                                          Sm[:, j, k * HALF:(k + 1) * HALF], kc("ident")[0:ROWS, 0:ROWS])
                elif name == "g":
                    pe.wait_ge(act_S.sem, act_S.at(g, "t2"))
                    for j in range(HP):
                        for k in range(2):
                            mm = pe.matmul(psS[0:ROWS, 0, j * ZR:(j + 1) * ZR], ET[:, k * HP + j, :], F[r][:, k, 0:ZR],
                                           start=(k == 0), stop=(k == 1))
                elif name == "gt":
                    pe.wait_ge(dve_S.sem, dve_S.at(g, "gn"))
                    by_itself(pe)
                    for j in range(HP):
                        mm = pe.transpose(psS[0:ZR, 1 + j // 3, (j % 3) * ROWS:(j % 3 + 1) * ROWS],
                                          GN[:, j, :], kc("ident")[0:ROWS, 0:ROWS])
                elif name == "at":
                    pe.wait_ge(dve_S.sem, dve_S.at(g, "g1"))
                    for j in range(HP):
                        pe.matmul(psS[0:SLOTS, 0, 0:D], G2[:, j, :], B2[:, j, :], start=(j == 0), stop=(j == HP - 1))
                    pe.matmul(psS[0:SLOTS, 0, D:2 * D], ZY[:, :], BW[:, :], start=True, stop=True)
                    mm = pe.matmul(psS[0:SLOTS, 0, 2 * D:2 * D + 2], ZY[0:ZR, :], selM2[:, :], start=True, stop=True)
                elif name == "xt":
                    pe.wait_ge(dve_S.sem, dve_S.at(g, "xh"))
                    by_itself(pe)
                    for k in range(2):
                        mm = pe.transpose(psS[0:DH, 1, k * SLOTS:(k + 1) * SLOTS], xh[:, k * DH:(k + 1) * DH],
                                          kc("ident")[0:SLOTS, 0:SLOTS])
                elif name == "f1":
                    pe.wait_ge(dve_S.sem, dve_S.at(g, "XH"))
                    for h in range(HT):
                        for k in range(2):
                            rows = slice(0, DH + 1) if k == 0 else slice(0, DH)
                            mm = pe.matmul(psS[:, 2, h * SLOTS:(h + 1) * SLOTS], W1T[rows, k, h * 128:(h + 1) * 128],
                                           XH[rows, k, :], start=(k == 0), stop=(k == 1))
                elif name == "f2":
                    pe.wait_ge(act_S.sem, act_S.at(g, "ge"))
                    for h in range(HT):
                        mm = pe.matmul(psS[0:SLOTS, 0, 0:D], actS[:, h, :], W2[:, h, :], start=(h == 0), stop=(h == HT - 1))
                mm.then_inc(pe_S.sem, 1)

            def step_F1(g, u, n):
                if n == 0:
                    pe.wait_ge(dve_A.sem, dve_A.at(g, "k1"))
                if exists(g if n >= 2 else g - 1):
                    pe.wait_ge(act_F1.sem, act_F1.at(g if n >= 2 else g - 1, f"n{(n - 2) % (2 * HT)}"))
                pe.matmul(psF[n % 2][:, 0:GT // 2], M1S[:, (n // 2) * 128:(n // 2 + 1) * 128],
                          Stk1[u % 2][:, (n % 2) * (GT // 2):(n % 2 + 1) * (GT // 2)], start=True, stop=True).then_inc(pe_F1.sem, 1)

            def step_F2(g, u, n):
                i, m = n // 8, n % 8
                to = psO[0:OT, 0:D]
                if m == 0:
                    pe.wait_ge(act_F1.sem, act_F1.at(g, f"n{2 * HT - 1}"))
                    if exists(g if i else g - 1):
                        pe.wait_ge(act_F2.sem, act_F2.at(g if i else g - 1, f"o{(i - 1) % FT}"))
                if m < HT:
                    pe.matmul(to, tile_of(act_sb[u % 2][:, m, :], i), W2[:, m, :], start=(m == 0), stop=False)
                elif m == HT:
                    pe.wait_ge(act_A.sem, act_A.at(g, "k2"))
                    pe.matmul(to, tile_of(Stk2[u][:, :], i), RS[:, :], start=False, stop=False)
                else:
                    pe.wait_ge(dve_S.sem, dve_S.at(g, "os"))
                    pe.matmul(to, tile_of(ST[u][:, :, :].rearrange("p b t -> p (b t)"), i), OS[u % 2][:, :],
                              start=False, stop=True).then_inc(pe_F2.sem, 1)

            plan_A = {3: ["cp"], 4: ["var"], 6: ["lg"], 8: ["tm"], 9: ["st"], 11: ["tr1", "tr2"]}
            plan_S = {0: "ga", 1: "u", 2: "sc", 4: "et", 5: "g", 6: "gt", 7: "at", 9: "xt", 10: "f1", 11: "f2"}
            n_F2 = 8 * FT

            def body(p, u, q):
                done = 0
                for s in range(2 * HT):
                    if s in plan_S and active(p, 2):
                        step_S(p - 2, (u - 2) % 4, plan_S[s])
                    for part in range(2):
                        upto = n_F2 * (2 * s + part + 1) // (4 * HT)
                        while done < upto:
                            if active(p, 3):
                                step_F2(p - 3, (u - 3) % 4, done)
                            done += 1
                        if part == 0:
                            for name in plan_A.get(s, []):
                                if active(p, 1):
                                    step_A(p - 1, (u - 1) % 4, name)
                            if active(p, 2):
                                step_F1(p - 2, (u - 2) % 4, s)

            pe.wait_ge(w_in, NW_IN * 16)
            weights()
            pe.wait_ge(dve_W.sem, dve_W.at(0, "alR"))
            periods(nc.tensor, body)

        @block.scalar
        def _(act):
            def step_A(g, u, name):
                if name == "e":
                    act.wait_ge(dve_A.sem, dve_A.at(g, "d"))
                    act.activation(Ex2[:, :, :], Dm[:, :, :], ACT.Exp).then_inc(act_A.sem, 1)
                elif name == "F":
                    act.wait_ge(pe_A.sem, pe_A.at(g, "tm"))
                    if exists(g - 2):
                        act.wait_ge(pe_S.sem, pe_S.at(g - 2, "g"))
                    act.activation(F[u % 2][:, :, :], psB[0:HALF, 0:2 * (FR + GB * 2 * W1)]
                                   .rearrange("p (k c) -> p k c", k=2)[:, :, 0:FR], ACT.Copy).then_inc(act_A.sem, 1)
                else:
                    act.wait_ge(pe_A.sem, pe_A.at(g, "tr2"))
                    act.activation(Stk2[u][:, :], psB[:, :].bitcast(bf16)[0:SK, 0:GT], ACT.Copy).then_inc(act_A.sem, 1)

            def step_S(g, u, name):
                if name == "exp":
                    act.wait_ge(dve_S.sem, dve_S.at(g, "nm"))
                    for j in range(HP):
                        act.activation(Sm[:, j, :], Sm[:, j, :], ACT.Exp, bias=nm[:, j:j + 1],
                                       accum_out=rsum[:, j:j + 1]).then_inc(act_S.sem, 1)
                elif name == "t":
                    act.wait_ge(pe_S.sem, pe_S.at(g, "et"))
                    if exists(g - 1):
                        act.wait_ge(pe_S.sem, pe_S.at(g - 1, "g"))
                    for n in range(3):
                        act.activation(ET[:, 4 * n:4 * n + 4, :], psS[0:HALF, n, 0:4 * ROWS]
                                       .rearrange("p (k s) -> p k s", k=4), ACT.Copy).then_inc(act_S.sem, 1)
                elif name == "se":
                    act.wait_ge(dve_S.sem, dve_S.at(g, "dm"))
                    act.activation(dexp[:, :], dmin[:, :], ACT.Exp).then_inc(act_S.sem, 1)
                else:
                    act.wait_ge(pe_S.sem, pe_S.at(g, "f1"))
                    if exists(g - 1):
                        act.wait_ge(pe_S.sem, pe_S.at(g - 1, "f2"))
                    act.activation(actS[:, :, :], psS[:, 2, 0:HT * SLOTS].rearrange("p (h s) -> p h s", h=HT),
                                   ACT.Gelu).then_inc(act_S.sem, 1)

            def step_F1(g, u, n):
                act.wait_ge(pe_F1.sem, pe_F1.at(g, f"n{n}"))
                act.activation(act_sb[u % 2][:, n // 2, (n % 2) * (GT // 2):(n % 2 + 1) * (GT // 2)],
                               psF[n % 2][:, 0:GT // 2], ACT.Gelu).then_inc(act_F1.sem, 1)

            def step_F2(g, u, i):
                act.wait_ge(pe_F2.sem, pe_F2.at(g, f"o{i}"))
                if i == 3:
                    if exists(g - 1):
                        act.wait_ge(y_out[(u - 1) % 2], landed(g - 1, (u - 1) % 2))
                act.activation(obuf[u % 2][:, i, :], psO[0:OT, 0:D], ACT.Copy).then_inc(act_F2.sem, 1)
                if i == FT - 1:
                    act.wait_ge(act_F2.sem, act_F2.at(g, f"o{i}"))
                    act.dma_start(og[bass.ds(g, 1)].rearrange("o p q -> (o p) q"),
                                  obuf[u % 2][:, :, :].rearrange("p i e -> p (i e)")).then_inc(y_out[u % 2], 16)

            plan_A = {6: ["e"], 8: ["F"], 11: ["k2"]}
            plan_S = {3: "exp", 4: "t", 7: "se", 10: "ge"}

            def body(p, u, q):
                done = 0
                for s in range(2 * HT):
                    if s in plan_S and active(p, 2):
                        step_S(p - 2, (u - 2) % 4, plan_S[s])
                    for part in range(2):
                        upto = 8 * FT * (2 * s + part + 1) // (4 * HT) // 8
                        while done < upto:
                            if active(p, 3):
                                step_F2(p - 3, (u - 3) % 4, done)
                            done += 1
                        if part == 0:
                            for name in plan_A.get(s, []):
                                if active(p, 1):
                                    step_A(p - 1, (u - 1) % 4, name)
                            if active(p, 2):
                                step_F1(p - 2, (u - 2) % 4, s)

            periods(nc.scalar, body)

        @block.vector
        def _(dve):
            def weights():


                dve.memset(WR[:, :], 0.0).then_inc(dve_W.sem, 1)
                dve.memset(WS[:, :], 0.0).then_inc(dve_W.sem, 1)
                dve.memset(XH[:, :, :], 1.0).then_inc(dve_W.sem, 1)
                dve.wait_ge(w_in, NW_IN * 16)
                for t in FM:
                    dve.tensor_copy(t[0:ZR, :], kc("f0", ZR))
                dve.memset(V[:, :], 0.0)
                dve.memset(WT[:, :], 0.0)
                dve.memset(sel[:, :], -7.0)
                dve.memset(mhalf[:, :], -0.5)
                dve.memset(m8b[:, :], -7.0).then_inc(dve_W.sem, 1)
                dve.tensor_copy(identb[:, :], kc("ident")).then_inc(dve_W.sem, 1)
                dve.tensor_reduce(mean_r[:, :], WR[:, :], AX.X, ALU.add).then_inc(dve_W.sem, 1)
                dve.wait_ge(dve_W.sem, dve_W.at(0, "mr"))
                dve.tensor_scalar(mean_r[:, :], mean_r[:, :], 1.0 / D, None, ALU.mult).then_inc(dve_W.sem, 1)
                dve.wait_ge(dve_W.sem, dve_W.at(0, "mr2"))
                dve.tensor_scalar(WcR[:, :], WR[:, :], mean_r[:, 0:1], None, ALU.subtract).then_inc(dve_W.sem, 1)
                dve.scalar_tensor_tensor(out=TMR[:, :], in0=kc("tmm", FR), scalar=mean_r[:, 0:1], in1=kc("tmk", FR),
                                           op0=ALU.mult, op1=ALU.add).then_inc(dve_W.sem, 1)
                dve.wait_ge(dve_W.sem, dve_W.at(0, "wcr"))
                dve.tensor_copy(BW[0:ZR, :], WcR[0:ZR, :]).then_inc(dve_W.sem, 1)
                dve.tensor_copy(BW[PR:FR, :], WR[PR:FR, :]).then_inc(dve_W.sem, 1)
                dve.tensor_reduce(mean_s[:, :], WS[:, :], AX.X, ALU.add).then_inc(dve_W.sem, 1)
                dve.wait_ge(dve_W.sem, dve_W.at(0, "ms"))
                dve.tensor_scalar(mean_s[:, :], mean_s[:, :], 1.0 / D, None, ALU.mult).then_inc(dve_W.sem, 1)
                dve.wait_ge(dve_W.sem, dve_W.at(0, "ms2"))
                dve.tensor_scalar(WcS[:, :], WS[:, :], mean_s[:, 0:1], None, ALU.subtract).then_inc(dve_W.sem, 1)
                dve.wait_ge(dve_W.sem, dve_W.at(0, "wcs"))
                dve.tensor_scalar(WS[:, :], WcS[:, :], kc("e13", SK), None, ALU.add).then_inc(dve_W.sem, 1)
                dve.wait_ge(pe_W.sem, pe_W.at(0, "ws"))
                dve.tensor_copy(WT4[0:DH, :, :], psA[0:DH, 0:2 * FR].rearrange("p (k c) -> p k c", k=2)).then_inc(dve_W.sem, 1)
                dve.tensor_copy(WST[0:DH, :, :], psB[0:DH, 0:2 * SK].rearrange("p (k c) -> p k c", k=2)).then_inc(dve_W.sem, 1)
                dve.wait_ge(pe_W.sem, pe_W.at(0, "c"))
                dve.scalar_tensor_tensor(out=CF[:, :], in0=psO[0:FR, 0:FR], scalar=1.0 / D, in1=kc("same", FR),
                                           op0=ALU.mult, op1=ALU.mult).then_inc(dve_W.sem, 1)
                dve.wait_ge(pe_W.sem, pe_W.at(0, "sel"))
                dve.tensor_copy(sel_raw[:, :], psF[0][0:ZR, 0:2]).then_inc(dve_W.sem, 1)
                dve.wait_ge(dve_W.sem, dve_W.at(0, "raw"))
                dve.tensor_tensor(sel_d[:, :], sel_raw[:, 1:2], sel_raw[:, 0:1], ALU.subtract).then_inc(dve_W.sem, 1)
                dve.wait_ge(dve_W.sem, dve_W.at(0, "sd"))
                dve.reciprocal(temp_sb[:, :], temp_sb[:, :]).then_inc(dve_W.sem, 1)
                dve.wait_ge(dve_W.sem, dve_W.at(0, "sd2"))
                dve.tensor_tensor(selM2[:, 1:2], sel_d[:, :], temp_sb[:, :], ALU.mult).then_inc(dve_W.sem, 1)
                dve.wait_ge(dve_W.sem, dve_W.at(0, "s1"))
                dve.tensor_scalar(selM2[:, 0:1], selM2[:, 1:2], -1.0, None, ALU.mult).then_inc(dve_W.sem, 1)
                dve.wait_ge(dve_W.sem, dve_W.at(0, "s0"))
                for k in (1, 0):
                    dve.tensor_scalar(selM[:, k, :], kc("bsel", ZR), selM2[:, k:k + 1], None, ALU.mult).then_inc(dve_W.sem, 1)
                banks = [(psS[:, 0], psS[:, 1]), (psS[:, 2], psA[:, :]), (psB[:, :], psF[1][:, :])]
                for m, (name, to) in enumerate([("q", MqT), ("k", MkT), ("v", MvT)]):
                    dve.wait_ge(pe_W.sem, pe_W.at(0, name))
                    for k in range(2):
                        ins = dve.tensor_copy(to[:, k * HP:(k + 1) * HP, :],
                                              banks[m][k][0:HD, 0:HP * ZR].rearrange("p (h c) -> p h c", h=HP))
                    ins.then_inc(dve_W.sem, 1)
                dve.wait_ge(pe_W.sem, pe_W.at(0, "a4"))
                for k in range(2):
                    ins = dve.tensor_scalar(A4[:, k * HP:(k + 1) * HP, :], (psA, psB)[k][0:ZR, 0:HP * ZR]
                                            .rearrange("p (h c) -> p h c", h=HP), float(HD) ** -0.5, None, ALU.mult)
                ins.then_inc(dve_W.sem, 1)
                dve.wait_ge(pe_W.sem, pe_W.at(0, "b2"))
                dve.tensor_copy(B2[:, :, :].rearrange("p (k j) e -> p k (j e)", k=3), psS[:, :, 0:2 * D]).then_inc(dve_W.sem, 1)
                dve.wait_ge(pe_W.sem, pe_W.at(0, "m1"))
                for k in range(2):
                    ins = dve.tensor_copy(M1f[:, k * HID // 2:(k + 1) * HID // 2], (psA, psB)[k][0:SK, 0:HID // 2])
                ins.then_inc(dve_W.sem, 1)
                dve.wait_ge(dve_W.sem, dve_W.at(0, "m1"))
                for t, f, to, n in (("M", M1f, M1S, HID), ("R", WS, RS, D)):
                    part, rest = M1h[:, 0:n], M1r[:, 0:n]
                    dve.tensor_copy(part, f[:, :]).then_inc(dve_W.sem, 1)
                    dve.wait_ge(dve_W.sem, dve_W.at(0, "h" + t))
                    dve.tensor_tensor(rest, f[:, :], part, ALU.subtract).then_inc(dve_W.sem, 1)
                    dve.tensor_scalar(to[:, :], part, kc("mh", SK), None, ALU.mult).then_inc(dve_W.sem, 1)
                    dve.wait_ge(dve_W.sem, dve_W.at(0, "ah" + t))
                    dve.tensor_copy(part, rest).then_inc(dve_W.sem, 1)
                    dve.wait_ge(dve_W.sem, dve_W.at(0, "m" + t))
                    dve.tensor_tensor(rest, rest, part, ALU.subtract).then_inc(dve_W.sem, 1)
                    dve.scalar_tensor_tensor(out=to[:, :], in0=part, scalar=kc("mm", SK), in1=to[:, :],
                                               op0=ALU.mult, op1=ALU.add).then_inc(dve_W.sem, 1)
                    dve.wait_ge(dve_W.sem, dve_W.at(0, "am" + t))
                    dve.tensor_copy(part, rest).then_inc(dve_W.sem, 1)
                    dve.wait_ge(dve_W.sem, dve_W.at(0, "l" + t))
                    dve.scalar_tensor_tensor(out=to[:, :], in0=part, scalar=kc("ml", SK), in1=to[:, :],
                                               op0=ALU.mult, op1=ALU.add).then_inc(dve_W.sem, 1)
                    dve.wait_ge(dve_W.sem, dve_W.at(0, "al" + t))

            def sum_tile(g, u, k):
                dve.wait_ge(pool_L.sem, pool_L.at(g, f"x{k}"))
                if k == 0:
                    if exists(g - 2):
                        dve.wait_ge(sums_out[u % 2], landed(g - 2, u % 2))
                v = X[:, (XT * u + k) % NX, :].rearrange("p (q r j l) -> p q j r l", q=TQ, r=QR, j=N)
                dve.tensor_reduce(R[:, u % 2, k * TQ * N:(k + 1) * TQ * N].rearrange("p (q j) -> p q j", q=TQ),
                                  v[:, :, :, 0:2, :], AX.XY, ALU.add).then_inc(dve_L.sem, 1)

            def stage_A(g, u, part):
                r = u % 2
                fm = FM[r]
                p = slice(PR, FR)



                if part == "v":
                    dve.wait_ge(pe_A.sem, pe_A.at(g, "cp"))
                    dve.tensor_tensor(V[p, :], psA[p, 0:T], fm[p, :], ALU.mult).then_inc(dve_A.sem, 1)
                elif part == "ve":
                    dve.wait_ge(pe_A.sem, pe_A.at(g, "var"))
                    var = psA[p, T:2 * T]
                    dve.tensor_scalar(sc["ve"][p, :], var, EPS, None, ALU.add).then_inc(dve_A.sem, 1)
                elif part == "scale":
                    dve.wait_ge(pool_A.sem, pool_A.at(g, "rstd"))
                    dve.tensor_scalar(sc["t1"][p, :], sc["rstd"][p, :], 1.0, None, ALU.add).then_inc(dve_A.sem, 1)
                    if exists(g - 2):
                        dve.wait_ge(pe_S.sem, pe_S.at(g - 2, "sc"))
                    dve.tensor_tensor(fm[0:BC, :], fm[p, :], sc["rstd"][p, :], ALU.mult).then_inc(dve_A.sem, 1)
                    dve.wait_ge(dve_A.sem, dve_A.at(g, "t1"))
                    dve.tensor_tensor(sc["t2"][p, :], sc["t1"][p, :], sc["t1"][p, :], ALU.mult).then_inc(dve_A.sem, 1)
                    dve.wait_ge(dve_A.sem, dve_A.at(g, "t2"))
                    dve.tensor_tensor(sc["s2"][p, :], sc["t2"][p, :], psA[p, T:2 * T], ALU.mult).then_inc(dve_A.sem, 1)
                    dve.wait_ge(dve_A.sem, dve_A.at(g, "s2"))
                    dve.tensor_scalar(sc["s3"][p, :], sc["s2"][p, :], EPS, None, ALU.add).then_inc(dve_A.sem, 1)
                elif part == "w":
                    dve.wait_ge(pool_A.sem, pool_A.at(g, "r2"))
                    dve.tensor_tensor(sc["al"][p, :], sc["t1"][p, :], sc["r2"][p, :], ALU.mult).then_inc(dve_A.sem, 1)
                    dve.wait_ge(dve_A.sem, dve_A.at(g, "al"))
                    if exists(g - 1):
                        dve.wait_ge(pe_A.sem, pe_A.at(g - 1, "tm"))
                    dve.tensor_tensor(WT[p, :], fm[p, :], sc["al"][p, :], ALU.mult).then_inc(dve_A.sem, 1)
                elif part == "d":
                    dve.wait_ge(pe_A.sem, pe_A.at(g, "lg"))
                    dve.tensor_scalar(Dm[:, :, :], psA[0:GB, 0:2 * T].rearrange("p (k t) -> p k t", k=2), 0.0, None, ALU.min).then_inc(dve_A.sem, 1)
                elif part == "top":
                    dve.wait_ge(act_A.sem, act_A.at(g, "e"))
                    dve.tensor_tensor(den[:, :], Ex2[:, 0, :], Ex2[:, 1, :], ALU.add).then_inc(dve_A.sem, 1)
                    dve.wait_ge(dve_A.sem, dve_A.at(g, "den"))
                    dve.reciprocal(rden[:, :], den[:, :]).then_inc(dve_A.sem, 1)
                    dve.wait_ge(dve_A.sem, dve_A.at(g, "rden"))
                    dve.tensor_tensor(sel[:, 0:T], Ex2[:, 1, :], rden[:, :], ALU.mult).then_inc(dve_A.sem, 1)
                    dve.wait_ge(dve_A.sem, dve_A.at(g, "sel"))
                    by_itself(dve)
                    dve.max(m8a[:, :], sel[:, :]).then_inc(dve_A.sem, 1)
                    dve.wait_ge(dve_A.sem, dve_A.at(g, "m8a"))
                    by_itself(dve)
                    dve.match_replace(sl1[:, :], m8a[:, :], sel[:, :], -1.0).then_inc(dve_A.sem, 1)
                    dve.wait_ge(dve_A.sem, dve_A.at(g, "mr1"))
                    by_itself(dve)
                    dve.max(m8b[:, :], sl1[:, :]).then_inc(dve_A.sem, 1)
                    dve.wait_ge(dve_A.sem, dve_A.at(g, "m8b"))
                    dve.memset(m8b[:, KSEL - 8:8], -7.0).then_inc(dve_A.sem, 1)
                    dve.wait_ge(dve_A.sem, dve_A.at(g, "fx"))
                    by_itself(dve)
                    dve.match_replace(sl2[:, :], m8b[:, :], sl1[:, :], -1.0).then_inc(dve_A.sem, 1)
                    dve.wait_ge(dve_A.sem, dve_A.at(g, "mr2"))
                    dve.tensor_scalar(mask[:, :], sl2[:, 0:T], 0.0, None, ALU.is_lt).then_inc(dve_A.sem, 1)
                    dve.wait_ge(dve_A.sem, dve_A.at(g, "mk"))
                    dve.tensor_tensor_scan(cum[:, :], kc("ones", GB), mask[:, :], 0.0, ALU.mult, ALU.add).then_inc(dve_A.sem, 1)
                    dve.wait_ge(dve_A.sem, dve_A.at(g, "cs"))
                    dve.tensor_tensor(srow[:, :], cum[:, :], mask[:, :], ALU.mult).then_inc(dve_A.sem, 1)
                elif part == "slots":
                    dve.wait_ge(pe_A.sem, pe_A.at(g, "st"))
                    col = psA[0:HALF, 400:400 + 2 * GB]
                    if exists(g - 2):
                        dve.wait_ge(pe_S.sem, pe_S.at(g - 2, "ga"))
                    for d in range(2):
                        dve.tensor_tensor(Sg[r][:, :, d, :].rearrange("p k (b s) -> p k b s", b=GB),
                                            col.rearrange("p (k b) -> p k b", k=2).unsqueeze(3).broadcast_to([HALF, 2, GB, KSEL]),
                                            kc("iota14", HALF).unsqueeze(1).unsqueeze(1).broadcast_to([HALF, 2, GB, KSEL]),
                                            ALU.is_equal).then_inc(dve_A.sem, 1)
                    dve.tensor_scalar(keep[:, :, :].rearrange("p k b -> p (k b)"), col, 0.0, None, ALU.is_equal).then_inc(dve_A.sem, 1)
                    dve.scalar_tensor_tensor(out=ST[u][:, :, :], in0=psA[0:SLOTS, 0:T].unsqueeze(1).broadcast_to([SLOTS, GB, T]),
                                               scalar=kc("r1", SLOTS), in1=kc("bmt", SLOTS).unsqueeze(2).broadcast_to([SLOTS, GB, T]),
                                               op0=ALU.is_equal, op1=ALU.mult).then_inc(dve_A.sem, 1)
                elif part == "parts":
                    dve.wait_ge(act_A.sem, act_A.at(g, "F"))
                    dve.wait_ge(dve_A.sem, dve_A.at(g, "kp"))
                    h2 = FR + GB * 2 * W1
                    dve.tensor_tensor(v26[:, :, :].rearrange("p (k b s) c -> p k b (s c)", k=2, b=GB),
                                        psB[0:HALF, 0:2 * h2].rearrange("p (k c) -> p k c", k=2)[:, :, FR:h2]
                                        .rearrange("p k (b c) -> p k b c", b=GB),
                                        keep[:, :, :].unsqueeze(3).broadcast_to([HALF, 2, GB, 2 * W1]), ALU.mult).then_inc(dve_A.sem, 1)
                    if exists(g - 1):
                        dve.wait_ge(pe_A.sem, pe_A.at(g - 1, "tr2"))
                    dve.wait_ge(dve_A.sem, dve_A.at(g, "v26"))

                    def part_of(src, n0, n1):
                        return dve.tensor_copy(SP[:, :, n0:n1, :],
                                               src[:, :, :].unsqueeze(2).broadcast_to([HALF, 4 * GB, n1 - n0, W1]))

                    part_of(v26, 0, 3).then_inc(dve_A.sem, 1)
                    dve.wait_ge(dve_A.sem, dve_A.at(g, "H"))
                    dve.tensor_tensor(d1[:, :, :], v26[:, :, :], SP[:, :, 0, :], ALU.subtract).then_inc(dve_A.sem, 1)
                    dve.wait_ge(dve_A.sem, dve_A.at(g, "d1"))
                    part_of(d1, 3, 6).then_inc(dve_A.sem, 1)
                    dve.wait_ge(dve_A.sem, dve_A.at(g, "M"))
                    dve.tensor_tensor(d2[:, :, :], d1[:, :, :], SP[:, :, 3, :], ALU.subtract).then_inc(dve_A.sem, 1)
                    dve.wait_ge(dve_A.sem, dve_A.at(g, "d2"))
                    part_of(d2, 6, 8).then_inc(dve_A.sem, 1)
                else:
                    dve.wait_ge(pe_A.sem, pe_A.at(g, "tr1"))
                    if exists(g - 2):
                        dve.wait_ge(pe_F1.sem, pe_F1.at(g - 2, f"n{2 * HT - 1}"))
                    dve.tensor_copy(Stk1[r][:, :], psA[:, :].bitcast(bf16)[0:SK, 0:GT]).then_inc(dve_A.sem, 1)

            def stage_S(g, u, part):


                r = u % 2
                if part == "ga":
                    dve.wait_ge(pe_S.sem, pe_S.at(g, "ga"))
                    dve.tensor_tensor(ZY[:, :], psS[0:FR, 0, 0:SLOTS], kc("bmzy", FR), ALU.mult).then_inc(dve_S.sem, 1)
                    dve.tensor_scalar(RM[:, :], kc("iota", ROWS), psS[0:ROWS, 0, ZR:ZR + 1], NEG, ALU.is_gt, ALU.mult).then_inc(dve_S.sem, 1)
                elif part == "u":
                    dve.wait_ge(pe_S.sem, pe_S.at(g, "u"))
                    for k in range(2):
                        dve.tensor_tensor(UB[:, :, k, :], psS[0:ZR, 1 + k, 0:HP * SLOTS].rearrange("p (j s) -> p j s", j=HP),
                                            kc("bm2", ZR).unsqueeze(1).broadcast_to([ZR, HP, SLOTS]), ALU.mult).then_inc(dve_S.sem, 1)
                elif part == "sc":
                    dve.wait_ge(pe_S.sem, pe_S.at(g, "sc"))
                    dve.wait_ge(dve_S.sem, dve_S.at(g, "rm"))
                    dve.tensor_tensor(Sm[:, :, :].rearrange("p (k j) t -> p k j t", k=3),
                                        psS[0:ROWS, :, 0:2 * T].rearrange("p k (j t) -> p k j t", j=2),
                                        RM[:, :].unsqueeze(1).unsqueeze(1).broadcast_to([ROWS, 3, 2, T]), ALU.add).then_inc(dve_S.sem, 1)
                    dve.wait_ge(dve_S.sem, dve_S.at(g, "sm"))
                    dve.tensor_reduce(mx[:, :], Sm[:, :, :], AX.X, ALU.max).then_inc(dve_S.sem, 1)
                    dve.wait_ge(dve_S.sem, dve_S.at(g, "mx"))
                    dve.tensor_scalar(nm[:, :], mx[:, :], -1.0, None, ALU.mult).then_inc(dve_S.sem, 1)
                elif part == "g":
                    dve.wait_ge(act_S.sem, act_S.at(g, "e5"))
                    dve.reciprocal(rinv[:, :], rsum[:, :]).then_inc(dve_S.sem, 1)
                    dve.wait_ge(pe_S.sem, pe_S.at(g, "g"))
                    dve.wait_ge(dve_S.sem, dve_S.at(g, "ri"))
                    dve.tensor_tensor(GN[:, :, :], psS[0:ROWS, 0, 0:HP * ZR].rearrange("p (j c) -> p j c", j=HP),
                                        rinv[:, :].unsqueeze(2).broadcast_to([ROWS, HP, ZR]), ALU.mult).then_inc(dve_S.sem, 1)
                elif part == "gt":
                    dve.wait_ge(pe_S.sem, pe_S.at(g, "gt"))
                    for k in range(2):
                        dve.tensor_tensor(G2[ZR * k:ZR * k + ZR, :, :].rearrange("p (i j) s -> p i j s", i=2),
                                            psS[0:ZR, 1:3, 0:3 * ROWS].rearrange("p i (j s) -> p i j s", j=3)[:, :, :, SLOTS * k:SLOTS * (k + 1)],
                                            kc("bm2", ZR).unsqueeze(1).unsqueeze(1).broadcast_to([ZR, 2, 3, SLOTS]), ALU.mult).then_inc(dve_S.sem, 1)
                elif part == "at":
                    dve.wait_ge(pe_S.sem, pe_S.at(g, "at"))
                    dve.tensor_scalar(dmin[:, :], psS[0:SLOTS, 0, 2 * D:2 * D + 2], 0.0, None, ALU.min).then_inc(dve_S.sem, 1)
                    dve.tensor_tensor(AO[:, :], psS[0:SLOTS, 0, 0:D], OB[:, :], ALU.add).then_inc(dve_S.sem, 1)
                elif part == "norm":
                    dve.wait_ge(act_S.sem, act_S.at(g, "se"))
                    dve.tensor_tensor(dden[:, :], dexp[:, 0:1], dexp[:, 1:2], ALU.add).then_inc(dve_S.sem, 1)
                    dve.wait_ge(dve_S.sem, dve_S.at(g, "dn"))
                    dve.reciprocal(rdden[:, :], dden[:, :]).then_inc(dve_S.sem, 1)
                    dve.wait_ge(dve_S.sem, dve_S.at(g, "rn"))
                    dve.tensor_tensor(dsel[:, :], dexp[:, 1:2], rdden[:, :], ALU.mult).then_inc(dve_S.sem, 1)
                    dve.wait_ge(dve_S.sem, dve_S.at(g, "sv"))
                    dve.scalar_tensor_tensor(out=h1[:, :], in0=AO[:, :], scalar=dsel[:, 0:1], in1=psS[0:SLOTS, 0, D:2 * D],
                                               op0=ALU.mult, op1=ALU.add).then_inc(dve_S.sem, 1)
                    dve.wait_ge(dve_S.sem, dve_S.at(g, "h1"))
                    dve.bn_stats(bst[:, :], h1[:, :]).then_inc(dve_S.sem, 1)
                    dve.wait_ge(dve_S.sem, dve_S.at(g, "bs"))
                    by_itself(dve)
                    dve.bn_aggr(mv[:, :], bst[:, :]).then_inc(dve_S.sem, 1)
                    dve.wait_ge(dve_S.sem, dve_S.at(g, "ba"))
                    dve.tensor_scalar(vrs[:, :], mv[:, 1:2], EPS, None, ALU.add).then_inc(dve_S.sem, 1)
                elif part == "xh":
                    dve.wait_ge(pool_S.sem, pool_S.at(g, "rs"))
                    dve.tensor_scalar(xh[:, :], h1[:, :], mv[:, 0:1], rst[:, 0:1], ALU.subtract, ALU.mult).then_inc(dve_S.sem, 1)
                elif part == "xt":
                    dve.wait_ge(pe_S.sem, pe_S.at(g, "xt"))
                    dve.tensor_copy(XH[0:DH, :, :], psS[0:DH, 1, 0:2 * SLOTS].rearrange("p (k s) -> p k s", k=2)).then_inc(dve_S.sem, 1)
                else:
                    dve.wait_ge(pe_S.sem, pe_S.at(g, "f2"))
                    dve.tensor_tensor(OS[r][:, :], psS[0:SLOTS, 0, 0:D], h1[:, :], ALU.add).then_inc(dve_S.sem, 1)

            plan_A = {3: ["v"], 4: ["ve"], 5: ["scale"], 6: ["d"], 7: ["w", "top"], 9: ["slots"], 10: ["parts"], 11: ["k1"]}
            plan_S = {0: "ga", 1: "u", 2: "sc", 5: "g", 6: "gt", 7: "at", 8: "norm", 9: "xh", 10: "xt", 11: "f2"}
            plan_L = {1: 0, 2: 1, 4: 2, 6: 3, 8: 4, 10: 5, 11: 6}

            def body(p, u, q):
                for s in range(2 * HT):
                    if s in plan_S and active(p, 2):
                        stage_S(p - 2, (u - 2) % 4, plan_S[s])
                    if s in plan_L and active(p, 0):
                        sum_tile(p, u, plan_L[s])
                    for part in plan_A.get(s, []):
                        if active(p, 1):
                            stage_A(p - 1, (u - 1) % 4, part)

            weights()
            periods(nc.vector, body)


def kernel(x, L0_tok_channel_weights, L0_attn_Wqkv_w, L0_attn_Wqkv_b, L0_attn_sel_w, L0_attn_sel_b, L0_attn_out_w,
           L0_attn_out_b, L0_attn_temperature, L0_ffn_in_weight, L0_ffn_in_bias, L0_ffn_out_weight):
    import concourse.bacc as bacc
    from concourse.bass_utils import run_bass_kernel_spmd as run

    e48, e13r = np.zeros((1, FR), np.float32), np.zeros((1, SK), np.float32)
    e48[0, Z1] = 1
    e13r[0, C::W1] = 1
    arrays = {
        "x": x, "cw": L0_tok_channel_weights, "wqkv": L0_attn_Wqkv_w, "bqkv": np.reshape(L0_attn_Wqkv_b, (1, -1)),
        "selw": L0_attn_sel_w, "selb": np.reshape(L0_attn_sel_b, (1, -1)), "ow": L0_attn_out_w,
        "ob": np.reshape(L0_attn_out_b, (1, -1)), "temp": np.reshape(L0_attn_temperature, (1, 1)),
        "w1t": np.transpose(L0_ffn_in_weight), "b1": np.reshape(L0_ffn_in_bias, (1, -1)), "w2": L0_ffn_out_weight,
        "consts": constants(), "e48": e48, "e13r": e13r,
    }
    arrays = {f"in_{k}": np.ascontiguousarray(v) for k, v in arrays.items()}
    nc = bacc.Bacc("TRN2", target_bir_lowering=False, num_devices=1)
    args = [nc.dram_tensor(k, v.shape, mybir.dt.from_np(v.dtype), kind="ExternalInput").ap() for k, v in arrays.items()]
    args.append(nc.dram_tensor("out_0", (B, T, D), mybir.dt.float32, kind="ExternalOutput").ap())
    program(nc, *args)
    return run(nc, [arrays], core_ids=[0]).results[0]["out_0"]
```

```python
import numpy as np
import concourse.bass as bass
from concourse import mybir
from contextlib import ExitStack

B, C, IMG, PATCH, D, HEADS, HID = 64, 12, 224, 16, 192, 12, 768
N = IMG // PATCH
T = N * N
HD = D // HEADS
KSEL = int(np.ceil(np.sqrt(T)))
GB = 4
NG = B // GB
BC = GB * C
SLOTS = GB * KSEL
HALF = T // 2
GT = GB * T
Z1 = BC
NW_IN = 1 + 2 * GB + 8 + 12
ZR = 64
PR = ZR
FR = PR + BC
AUX = 3
PF = BC + 1
TMC = 2 * BC + GB * AUX
FC = PR + TMC
W1 = C + 1
PAIRS = 8
PART_OF = [0, 0, 0, 1, 1, 1, 2, 2]
WPART_OF = [0, 1, 2, 0, 1, 2, 0, 1]
SK = PAIRS * W1
DH = D // 2
HP = HEADS // 2
ROWS = 2 * SLOTS
HT = HID // 128
FT = 7
FP = T // FT
OT = GB * FP
QR = 4
QB = QR * IMG
NQ = GB * C * IMG // QR // 128
TQ = 3
XT = NQ // TQ
NX = 4
EPS = 1e-5
NEG = -10000.0

COLS = {}
_at = 0
for _name, _n in [("ident", 128), ("same", BC), ("mexp", GB), ("bm2", SLOTS), ("bmzy", SLOTS), ("e4", SLOTS), ("bmt", GB),
                  ("r1", 1), ("iota14", KSEL), ("iota", T), ("tpos", 2), ("e13", 1), ("mh", 1),
                  ("mm", 1), ("ml", 1), ("bsel", GB), ("ones", T), ("f0", T)]:
    COLS[_name] = (_at, _at + _n)
    _at += _n
NCOLS = _at


def constants():
    k = np.zeros((128, NCOLS), np.float32)

    def col(name):
        a, b = COLS[name]
        return k[:, a:b]

    col("ident")[:] = np.eye(128)
    for b in range(GB):
        z, p = slice(b * C, b * C + C), slice(PR + b * C, PR + b * C + C)
        s = slice(b * KSEL, b * KSEL + KSEL)
        col("same")[z, z] = 1
        col("bm2")[z, s] = 1
        col("bmzy")[z, s] = 1
        col("bmzy")[p, s] = 1
        col("e4")[b, s] = 1
        col("bmt")[s, b] = 1
        col("r1")[s, 0] = np.arange(1, KSEL + 1)
        col("bsel")[z, b] = 1
    col("bm2")[Z1] = 1
    col("bmzy")[Z1] = 1
    col("iota14")[:] = np.arange(1, KSEL + 1)
    col("iota")[:] = np.arange(T)
    col("tpos")[:, 0] = np.arange(128)
    col("tpos")[:, 1] = HALF + np.arange(128)
    for n in range(PAIRS):
        col("e13")[n * W1 + C] = 1
        col(["mh", "mm", "ml"][WPART_OF[n]])[n * W1:n * W1 + W1] = 1
    col("ones")[:] = 1
    col("f0")[Z1] = 1
    return k


class Steps:

    def __init__(self, sem, names):
        self.sem, self.names = sem, names.split()

    def at(self, group, name):
        return group * len(self.names) + (self.names.index(name) + 1)


def program(nc, x, cw, wqkv, bqkv, selw, selb, ow, ob, temp, w1t, b1, w2, consts, e48, e13r, out):
    f32, bf16, i32 = mybir.dt.float32, mybir.dt.bfloat16, mybir.dt.int32
    ALU, ACT, AX = mybir.AluOpType, mybir.ActivationFunctionType, mybir.AxisListType

    xg = x.rearrange("(g b) c h w -> g (b c h w)", b=GB).rearrange("g (p q) -> g p q", p=128)
    og = out.rearrange("(g b) (t i) e -> g (b t) (i e)", b=GB, i=FT)
    scratch = nc.dram_tensor("patch_sums", (NG, 128, NQ * N), f32, kind="Internal").ap()
    sums_in = scratch.rearrange("g p q -> g (p q)").rearrange("g (r q) -> g r q", r=BC)

    with ExitStack() as ctx:
        def sb(name, shape, dt=f32):
            return ctx.enter_context(nc.sbuf_tensor(name, shape, dt))

        def ps(name):
            return ctx.enter_context(nc.psum_tensor(name, [128, 512], f32))

        def sem(name):
            return ctx.enter_context(nc.semaphore(name))

        K = sb("K", [128, NCOLS])

        def kc(name, rows=128):
            a, b = COLS[name]
            return K[0:rows, a:b]

        WR, BW, WcR = sb("WR", [FR, D]), sb("BW", [FR, D]), sb("WcR", [FR, D])
        WS, WcS = sb("WS", [SK, D]), sb("WcS", [SK, D])
        mean_r, mean_s = sb("mean_r", [FR, 1]), sb("mean_s", [SK, 1])
        WT4, WST = sb("WT4", [DH + 1, 2, FR]), sb("WST", [DH + 1, 2, SK])
        Wsel = sb("Wsel", [DH + 1, 2, 2])
        W1T = sb("W1T", [DH + 1, 2, HID])
        W2 = sb("W2", [128, HT, D])
        OB = sb("OB", [SLOTS, D])
        temp_sb = sb("temp_sb", [ZR, 1])
        A4 = sb("A4", [ZR, HEADS, ZR])
        B2 = sb("B2", [128, HP, D])
        TMR = sb("TMR", [PF, TMC])
        selM2 = sb("selM2", [ZR, 2])
        sel_raw, sel_d = sb("sel_raw", [ZR, 2]), sb("sel_d", [ZR, 1])
        M1S, RS = sb("M1S", [SK, HID], bf16), sb("RS", [SK, D], bf16)
        identb = sb("identb", [128, 128], bf16)

        X = sb("X", [128, NX, TQ * QB])
        R = sb("R", [128, 2, NQ * N])
        Praw = sb("Praw", [BC, 2, NQ * 128 * N // BC])
        Pt = sb("Pt", [BC, 2, T])
        P = [sb(f"P{i}", [PF, T]) for i in range(2)]
        FM = [sb(f"FM{i}", [ZR, T]) for i in range(2)]
        prod = sb("prod", [HALF, 2, BC])
        sc = {n: sb(n, [HALF, 2 * GB]) for n in ("var", "ve", "hv", "rstd", "ya", "yb", "lr", "L", "t1", "t2", "s2", "s3", "hv2", "r2", "al",
                                                 "den", "rden", "kw", "ky")}
        selT = sb("selT", [HALF, 2 * GB])
        Dm, Ex2 = sb("Dm", [HALF, 2, 2 * GB]), sb("Ex2", [HALF, 2, 2 * GB])
        sel, sl1, sl2 = sb("sel", [GB, T + 4]), sb("sl1", [GB, T + 4]), sb("sl2", [GB, T + 4])
        m8a, m8b = sb("m8a", [GB, 8]), sb("m8b", [GB, 8])
        mask, cum, srow = sb("mask", [GB, T]), sb("cum", [GB, T]), sb("srow", [GB, T])
        Sg = [sb(f"S{i}", [HALF, 2, 2, SLOTS]) for i in range(2)]
        keep = sb("keep", [HALF, 2 * GB])
        ST = [sb(f"ST{i}", [SLOTS, GB, T]) for i in range(4)]
        F = [sb(f"F{i}", [HALF, 2, FC]) for i in range(2)]
        v26, d1, d2 = (sb(n, [HALF, 4 * GB, W1]) for n in ("v26", "d1", "d2"))
        SP = sb("SP", [HALF, 4 * GB, PAIRS, W1], bf16)
        Stk1 = [sb(f"Stk1_{i}", [SK, GT], bf16) for i in range(2)]
        Stk2 = [sb(f"Stk2_{i}", [SK, GT], bf16) for i in range(4)]
        act_sb = [sb(f"act{i}", [128, HT, GT]) for i in range(2)]
        spare = [t[:, :, :].rearrange("p h t -> p (h t)") for t in act_sb]
        Wqkv = spare[0][0:DH + 1, 0:6 * D].rearrange("p (k n) -> p k n", k=2)
        Wo = spare[0][0:HD, 6 * D:(6 + HEADS) * D].rearrange("p (h e) -> p h e", h=HEADS)
        MqT, MkT, MvT = (spare[1][0:HD, n * HEADS * ZR:(n + 1) * HEADS * ZR].rearrange("p (h c) -> p h c", h=HEADS) for n in range(3))
        M1f, M1r = (spare[1][0:SK, n * HID:(n + 1) * HID] for n in (3, 4))
        M1h = spare[1][0:SK, 5 * HID:5 * HID + HID // 2].bitcast(bf16)
        ZY = sb("ZY", [FR, SLOTS])
        RM = sb("RM", [ROWS, T])
        UB = sb("UB", [ZR, HP, 2, SLOTS])
        Sm = sb("Sm", [ROWS, HP, T])
        mx, nm, rsum, rinv = (sb(n, [ROWS, HP]) for n in ("mx", "nm", "rsum", "rinv"))
        ET = sb("ET", [HALF, 2 * HP, ROWS])
        GN = sb("GN", [ROWS, HP, ZR])
        G2 = sb("G2", [128, HP, SLOTS])
        dmin, dexp, dden, dsel = sb("dmin", [SLOTS, 2]), sb("dexp", [SLOTS, 2]), sb("dden", [SLOTS, 1]), sb("dsel", [SLOTS, 1])
        AO, h1, xh = sb("AO", [SLOTS, D]), sb("h1", [SLOTS, D]), sb("xh", [SLOTS, D])
        bst, mv, vrs, rst = sb("bst", [SLOTS, 6]), sb("mv", [SLOTS, 2]), sb("vrs", [SLOTS, 1]), sb("rst", [SLOTS, 1])
        rdden, hvs, yas, ybs = (sb(n, [SLOTS, 1]) for n in ("rdden", "hvs", "yas", "ybs"))
        XH = sb("XH", [DH + 1, 2, SLOTS])
        actS = sb("actS", [128, HT, SLOTS])
        OS = [sb(f"OS{i}", [SLOTS, D]) for i in range(2)]
        obuf = [sb(f"obuf{i}", [OT, FT, D]) for i in range(2)]

        psF = [ps("psF0"), ps("psF1")]
        psO, psA, psB = ps("psO"), ps("psA"), ps("psB")
        psS = ctx.enter_context(nc.psum_tensor("psS", [128, 3, 512], f32))

        w_in, w_zero = sem("weights_loaded"), sem("weights_zeroed")
        x_in = [sem(f"x_loaded{k}") for k in range(NX)]
        sums_out = [sem(f"sums_stored{k}") for k in range(2)]
        sums_back = [sem(f"sums_loaded{k}") for k in range(2)]
        y_out = [sem(f"out_stored{k}") for k in range(2)]
        passed = sem("waits_passed")
        tiles = [f"x{k}" for k in range(XT)]
        pool_L = Steps(sem("pool_halved_x"), " ".join(tiles))
        dve_L = Steps(sem("dve_summed_x"), " ".join(tiles))
        pool_A = Steps(sem("pool_token_sums"), "q01 q23 p")
        pe_A = Steps(sem("pe_norm_steps"), "tm zt sl st tr1 tr2")
        root = "h0 g0 " + " ".join(f"{n}{k}" for k in range(3) for n in "aby")
        dve_A = Steps(sem("dve_norm_steps"), "cp pr var ve " + " ".join("r" + n for n in root.split()) + " z lr L D1 D0 t1 t2 s2 s3 "
                      + " ".join("q" + n for n in root.split()) + " al den rden sel row m8a mr1 m8b fx mr2 mk cs sr S S2 kp ST "
                      "kw ky w y one mean H d1 M d2 L3 k1")
        act_A = Steps(sem("act_norm_steps"), "e fm k2")
        pe_S = Steps(sem("pe_chosen_steps"), "ga u sc et g gt at xt f1 f2")
        dve_S = Steps(sem("dve_chosen_steps"), "zy rm ub0 ub1 sm mx nm ri gn g0 g1 dm ao dn rn sv h1 bs ba vr " + " ".join("r" + n for n in root.split()) + " xh XH os")
        act_S = Steps(sem("act_chosen_steps"), "e0 e1 e2 e3 e4 e5 t0 t1 t2 se ge")
        ffn = [f"n{k}" for k in range(2 * HT)]
        outs = [f"o{k}" for k in range(FT)]
        pe_F1 = Steps(sem("pe_ffn1"), " ".join(ffn))
        act_F1 = Steps(sem("act_gelu"), " ".join(ffn))
        pe_F2 = Steps(sem("pe_ffn2"), " ".join(outs))
        act_F2 = Steps(sem("act_out"), " ".join(outs))
        pe_W = Steps(sem("pe_weights"), "wt ws c sel q k v a4 b2 m1")
        splits = "h r1 ah m r2 am l al"
        dve_W = Steps(sem("dve_weights"), "wr0 ws0 wt0 ini idb mr mr2 wcr bw0 bw1 ms ms2 wcs rf wt ws cf cf2 raw sd sd2 s1 s0 tp tz tmm tmd tmb q k v a4 b2 m1 "
                      + " ".join(f"{n}{t}" for t in "MR" for n in splits.split()))
        block = ctx.enter_context(nc.Block())

        def periods(engine, body):
            for p in range(4):
                body(p, p, 0)
            with engine.Fori(0, 3) as i:
                for k in range(4, 8):
                    body(i * 4 + k, k % 4, i + k // 4)
            for p in range(16, NG + 3):
                body(p, p % 4, p // 4)

        def by_itself(engine):
            engine.sem_inc(passed, 1)

        def active(p, lag):
            return not isinstance(p, int) or 0 <= p - lag < NG

        def exists(group):
            return not isinstance(group, int) or group >= 0

        def landed(group, par):
            return (group - par) * 8 + 16

        def tile_of(ap, i):
            return ap.rearrange("p (m i) -> p i m", i=FT)[:, i, :]

        @block.sync
        def _(sp):
            sp.dma_start(K[:, :], consts).then_inc(w_in, 16)
            sp.wait_ge(dve_W.sem, dve_W.at(0, "wt0"))
            n = 1
            for b in range(GB):
                sp.dma_start(WR[b * C:b * C + C, :], cw).then_inc(w_in, 16)
                sp.dma_start(WR[PR + b * C:PR + b * C + C, :], cw).then_inc(w_in, 16)
                n += 2
            for k in range(PAIRS):
                sp.dma_start(WS[k * W1:k * W1 + C, :], cw).then_inc(w_in, 16)
                n += 1
            for dst, src in [
                    (Wqkv[0:DH, :, :], wqkv.rearrange("(k d) n -> d k n", k=2)), (Wqkv[DH:DH + 1, 0, :], bqkv),
                    (Wsel[0:DH, :, :], selw.rearrange("(k d) n -> d k n", k=2)), (Wsel[DH:DH + 1, 0, :], selb),
                    (Wo[:, :, :], ow.rearrange("(h d) e -> d h e", h=HEADS)),
                    (W1T[0:DH, :, :], w1t.rearrange("(k d) n -> d k n", k=2)), (W1T[DH:DH + 1, 0, :], b1),
                    (W2[:, :, :], w2.rearrange("(h p) e -> p h e", h=HT)),
                    (OB[:, :], ob.to_broadcast([SLOTS, D])),
                    (temp_sb[:, :], temp.to_broadcast([ZR, 1])),
                    (WT4[DH:DH + 1, 0, :], e48), (WST[DH:DH + 1, 0, :], e13r)]:
                sp.dma_start(dst, src).then_inc(w_in, 16)
                n += 1
            assert n == NW_IN, n

            def body(p, u, q):
                for k in range(XT):
                    if active(p, 0):
                        if exists(p if k >= NX else p - 1):
                            sp.wait_ge(dve_L.sem, dve_L.at(p if k >= NX else p - 1, f"x{(k - NX) % XT}"))
                        sp.dma_start(X[:, (XT * u + k) % NX, :], xg[bass.ds(p, 1), :, k * TQ * QB:(k + 1) * TQ * QB]
                                     .rearrange("o p q -> (o p) q")).then_inc(x_in[(XT * u + k) % NX], 16)
                    if k == NX - 1 and active(p, 1):
                        sp.wait_ge(dve_L.sem, dve_L.at(p - 1, f"x{XT - 1}"))
                        sp.dma_start(scratch[bass.ds(p - 1, 1)].rearrange("o p q -> (o p) q"),
                                     R[:, (u - 1) % 2, :]).then_inc(sums_out[(u - 1) % 2], 16)
                    if k == NX and active(p, 1):
                        g, r = p - 1, (u - 1) % 2
                        sp.wait_ge(sums_out[r], landed(g, r))
                        if exists(g - 2):
                            sp.wait_ge(pool_A.sem, pool_A.at(g - 2, "q23"))
                        sp.dma_start(Praw[:, r, :], sums_in[bass.ds(g, 1)].rearrange("o p q -> (o p) q")
                                     ).then_inc(sums_back[r], 16)

            periods(nc.sync, body)
            for r in range(2):
                sp.wait_ge(sums_out[r], landed(NG - 2 + r, r))
                sp.wait_ge(y_out[r], landed(NG - 2 + r, r))

        @block.gpsimd
        def _(pool):
            def body(p, u, q):
                for k in range(XT):
                    if active(p, 0):
                        b = (XT * u + k) % NX
                        pool.wait_ge(x_in[b], (q * XT + ((XT * u + k) // NX + 1)) * 16)
                        v = X[:, b, :].rearrange("p (q r w) -> p q r w", q=TQ, r=QR)
                        if k == 2 and active(p, 1):
                            pool.wait_ge(pool_A.sem, pool_A.at(p - 1, "p"))
                        pool.tensor_tensor(v[:, :, 0:2, :], v[:, :, 0:2, :], v[:, :, 2:4, :], ALU.add).then_inc(pool_L.sem, 1)
                    if k == 1 and active(p, 0):
                        pool.wait_ge(pool_L.sem, pool_L.at(p, f"x{k}"))
                    if k == 1 and active(p, 1):
                        sum_quarters(p - 1, (u - 1) % 2)

            def sum_quarters(g, r):
                pool.wait_ge(sums_back[r], landed(g, r))
                raw = Praw[:, r, :].rearrange("p (i q j) -> p q i j", i=N, q=4)
                t = Pt[:, :, :].rearrange("p k (i j) -> p k i j", i=N)
                pool.tensor_tensor(t[:, 0], raw[:, 0], raw[:, 1], ALU.add).then_inc(pool_A.sem, 1)
                pool.tensor_tensor(t[:, 1], raw[:, 2], raw[:, 3], ALU.add).then_inc(pool_A.sem, 1)
                pool.wait_ge(pool_A.sem, pool_A.at(g, "q23"))
                if exists(g - 2):
                    pool.wait_ge(pe_A.sem, pe_A.at(g - 2, "tm"))
                pool.wait_ge(dve_W.sem, dve_W.at(0, "ini"))
                pool.tensor_tensor(P[r][0:BC, :], Pt[:, 0, :], Pt[:, 1, :], ALU.add).then_inc(pool_A.sem, 1)

            periods(nc.gpsimd, body)

        @block.tensor
        def _(pe):
            def weights():
                pe.wait_ge(dve_W.sem, dve_W.at(0, "wcs"))
                for k in range(2):
                    mm = pe.transpose(psA[0:DH, k * FR:k * FR + FR], WcR[:, k * DH:k * DH + DH], kc("ident")[0:FR, 0:FR])
                mm.then_inc(pe_W.sem, 1)
                for k in range(2):
                    mm = pe.transpose(psB[0:DH, k * SK:k * SK + SK], WcS[:, k * DH:k * DH + DH], kc("ident")[0:SK, 0:SK])
                mm.then_inc(pe_W.sem, 1)
                pe.wait_ge(dve_W.sem, dve_W.at(0, "ws"))
                for k in range(2):
                    mm = pe.matmul(psO[0:BC, 0:BC], WT4[0:DH, k, 0:BC], WT4[0:DH, k, 0:BC], start=(k == 0), stop=(k == 1))
                mm.then_inc(pe_W.sem, 1)

                def bias_first(k):
                    return slice(0, DH + 1) if k == 0 else slice(0, DH)

                for k in range(2):
                    mm = pe.matmul(psF[0][0:ZR, 0:2], WT4[bias_first(k), k, 0:ZR], Wsel[bias_first(k), k, :],
                                   start=(k == 0), stop=(k == 1))
                mm.then_inc(pe_W.sem, 1)
                pe.wait_ge(dve_W.sem, dve_W.at(0, "raw"))
                banks = [(psS[:, 0], psS[:, 1]), (psS[:, 2], psA[:, :]), (psB[:, :], psF[1][:, :])]
                for m in range(3):
                    for h in range(HEADS):
                        to = banks[m][h // HP][0:HD, (h % HP) * ZR:(h % HP) * ZR + ZR]
                        for k in range(2):
                            mm = pe.matmul(to, Wqkv[bias_first(k), k, m * D + h * HD:m * D + h * HD + HD],
                                           WT4[bias_first(k), k, 0:ZR], start=(k == 0), stop=(k == 1))
                    mm.then_inc(pe_W.sem, 1)
                pe.wait_ge(dve_W.sem, dve_W.at(0, "v"))
                for h in range(HEADS):
                    mm = pe.matmul((psA if h < HP else psB)[0:ZR, (h % HP) * ZR:(h % HP) * ZR + ZR],
                                   MqT[:, h, :], MkT[:, h, :], start=True, stop=True)
                mm.then_inc(pe_W.sem, 1)
                for h in range(HEADS):
                    j = h % HP
                    r = ZR * (h // HP)
                    mm = pe.matmul(psS[r:r + ZR, j // 2, (j % 2) * D:(j % 2) * D + D], MvT[:, h, :], Wo[:, h, :],
                                   start=True, stop=True)
                mm.then_inc(pe_W.sem, 1)
                pe.wait_ge(dve_W.sem, dve_W.at(0, "b2"))
                for n in range(2):
                    for k in range(2):
                        mm = pe.matmul((psA, psB)[n][0:SK, 0:HID // 2], WST[bias_first(k), k, :],
                                       W1T[bias_first(k), k, n * HID // 2:(n + 1) * HID // 2], start=(k == 0), stop=(k == 1))
                mm.then_inc(pe_W.sem, 1)

            def step_A(g, u, name):
                r = u % 2
                if name == "tm":
                    pe.wait_ge(pool_A.sem, pool_A.at(g, "p"))
                    if exists(g - 1):
                        pe.wait_ge(act_A.sem, act_A.at(g - 1, "k2"))
                    for k in range(2):
                        mm = pe.matmul(psB[0:HALF, k * TMC:(k + 1) * TMC], P[r][:, k * HALF:(k + 1) * HALF], TMR[:, :],
                                       start=True, stop=True)
                elif name == "zt":
                    pe.wait_ge(dve_A.sem, dve_A.at(g, "L"))
                    by_itself(pe)
                    for k in range(2):
                        mm = pe.transpose(psB[0:ZR, k * HALF:(k + 1) * HALF], F[r][:, k, 0:ZR], kc("ident")[0:HALF, 0:HALF])
                elif name == "sl":
                    pe.wait_ge(dve_A.sem, dve_A.at(g, "sel"))
                    if exists(g - 1):
                        pe.wait_ge(dve_A.sem, dve_A.at(g - 1, "k1"))
                    for k in range(2):
                        mm = pe.transpose(psA[0:GB, k * HALF:(k + 1) * HALF], selT[:, k * GB:(k + 1) * GB], kc("ident")[0:HALF, 0:HALF])
                elif name == "st":
                    pe.wait_ge(dve_A.sem, dve_A.at(g, "sr"))
                    for k in range(2):
                        pe.matmul(psA[0:HALF, 400 + k * GB:400 + (k + 1) * GB], srow[:, k * HALF:(k + 1) * HALF],
                                  kc("ident")[0:GB, 0:GB], start=True, stop=True)
                    mm = pe.matmul(psA[0:SLOTS, 0:T], kc("e4", GB), srow[:, :], start=True, stop=True)
                else:
                    k = int(name[2]) - 1
                    pe.wait_ge(dve_A.sem, dve_A.at(g, "L3"))
                    if k:
                        pe.wait_ge(act_A.sem, act_A.at(g, "fm"))
                    to = (psA, psB)[k][:, :].bitcast(bf16)
                    for n in range(2 * GB):
                        c0 = (n % GB) * T + (n // GB) * HALF
                        mm = pe.transpose(to[0:SK, c0:c0 + HALF], SP[:, 2 * n + k, :, :].rearrange("p n c -> p (n c)"),
                                          identb[0:HALF, 0:HALF])
                mm.then_inc(pe_A.sem, 1)

            def step_S(g, u, name):
                r = u % 2
                if name == "ga":
                    pe.wait_ge(dve_A.sem, dve_A.at(g, "S2"))
                    if exists(g - 1):
                        pe.wait_ge(dve_S.sem, dve_S.at(g - 1, "os"))
                    for k in range(2):
                        pe.matmul(psS[0:FR, 0, 0:SLOTS], F[r][:, k, 0:FR], Sg[r][:, k, 0, :],
                                  start=(k == 0), stop=(k == 1))
                    for k in range(2):
                        mm = pe.matmul(psS[0:ROWS, 0, ZR:ZR + 1],
                                       Sg[r][:, k, :, :].rearrange("p d s -> p (d s)"),
                                       kc("tpos", HALF)[:, k:k + 1], start=(k == 0), stop=(k == 1))
                elif name == "u":
                    pe.wait_ge(dve_S.sem, dve_S.at(g, "zy"))
                    by_itself(pe)
                    for h in range(HEADS):
                        mm = pe.matmul(psS[0:ZR, 1 + h // HP, (h % HP) * SLOTS:(h % HP + 1) * SLOTS], A4[:, h, :],
                                       ZY[0:ZR, :], start=True, stop=True)
                elif name == "sc":
                    pe.wait_ge(act_A.sem, act_A.at(g, "fm"))
                    pe.wait_ge(dve_S.sem, dve_S.at(g, "ub1"))
                    for j in range(HP):
                        mm = pe.matmul(psS[0:ROWS, j // 2, (j % 2) * T:(j % 2 + 1) * T],
                                       UB[:, j, :, :].rearrange("p k s -> p (k s)"), FM[r][:, :], start=True, stop=True)
                elif name == "et":
                    pe.wait_ge(act_S.sem, act_S.at(g, "e5"))
                    for n in range(2 * HP):
                        k, j = n // HP, n % HP
                        mm = pe.transpose(psS[0:HALF, n // 4, (n % 4) * ROWS:(n % 4 + 1) * ROWS],
                                          Sm[:, j, k * HALF:(k + 1) * HALF], kc("ident")[0:ROWS, 0:ROWS])
                elif name == "g":
                    pe.wait_ge(act_S.sem, act_S.at(g, "t2"))
                    for j in range(HP):
                        for k in range(2):
                            mm = pe.matmul(psS[0:ROWS, 0, j * ZR:(j + 1) * ZR], ET[:, k * HP + j, :], F[r][:, k, 0:ZR],
                                           start=(k == 0), stop=(k == 1))
                elif name == "gt":
                    pe.wait_ge(dve_S.sem, dve_S.at(g, "gn"))
                    by_itself(pe)
                    for j in range(HP):
                        mm = pe.transpose(psS[0:ZR, 1 + j // 3, (j % 3) * ROWS:(j % 3 + 1) * ROWS],
                                          GN[:, j, :], kc("ident")[0:ROWS, 0:ROWS])
                elif name == "at":
                    pe.wait_ge(dve_S.sem, dve_S.at(g, "g1"))
                    for j in range(HP):
                        pe.matmul(psS[0:SLOTS, 0, 0:D], G2[:, j, :], B2[:, j, :], start=(j == 0), stop=(j == HP - 1))
                    pe.matmul(psS[0:SLOTS, 0, D:2 * D], ZY[:, :], BW[:, :], start=True, stop=True)
                    mm = pe.matmul(psS[0:SLOTS, 0, 2 * D:2 * D + 2], ZY[0:ZR, :], selM2[:, :], start=True, stop=True)
                elif name == "xt":
                    pe.wait_ge(dve_S.sem, dve_S.at(g, "xh"))
                    by_itself(pe)
                    for k in range(2):
                        mm = pe.transpose(psS[0:DH, 1, k * SLOTS:(k + 1) * SLOTS], xh[:, k * DH:(k + 1) * DH],
                                          kc("ident")[0:SLOTS, 0:SLOTS])
                elif name == "f1":
                    pe.wait_ge(dve_S.sem, dve_S.at(g, "XH"))
                    for h in range(HT):
                        for k in range(2):
                            rows = slice(0, DH + 1) if k == 0 else slice(0, DH)
                            mm = pe.matmul(psS[:, 2, h * SLOTS:(h + 1) * SLOTS], W1T[rows, k, h * 128:(h + 1) * 128],
                                           XH[rows, k, :], start=(k == 0), stop=(k == 1))
                elif name == "f2":
                    pe.wait_ge(act_S.sem, act_S.at(g, "ge"))
                    for h in range(HT):
                        mm = pe.matmul(psS[0:SLOTS, 0, 0:D], actS[:, h, :], W2[:, h, :], start=(h == 0), stop=(h == HT - 1))
                mm.then_inc(pe_S.sem, 1)

            def step_F1(g, u, n):
                if n == 0:
                    pe.wait_ge(dve_A.sem, dve_A.at(g, "k1"))
                if exists(g if n >= 2 else g - 1):
                    pe.wait_ge(act_F1.sem, act_F1.at(g if n >= 2 else g - 1, f"n{(n - 2) % (2 * HT)}"))
                pe.matmul(psF[n % 2][:, 0:GT // 2], M1S[:, (n // 2) * 128:(n // 2 + 1) * 128],
                          Stk1[u % 2][:, (n % 2) * (GT // 2):(n % 2 + 1) * (GT // 2)], start=True, stop=True).then_inc(pe_F1.sem, 1)

            def step_F2(g, u, n):
                i, m = n // 8, n % 8
                to = psO[0:OT, 0:D]
                if m == 0:
                    pe.wait_ge(act_F1.sem, act_F1.at(g, f"n{2 * HT - 1}"))
                    if exists(g if i else g - 1):
                        pe.wait_ge(act_F2.sem, act_F2.at(g if i else g - 1, f"o{(i - 1) % FT}"))
                if m < HT:
                    pe.matmul(to, tile_of(act_sb[u % 2][:, m, :], i), W2[:, m, :], start=(m == 0), stop=False)
                elif m == HT:
                    pe.wait_ge(act_A.sem, act_A.at(g, "k2"))
                    pe.matmul(to, tile_of(Stk2[u][:, :], i), RS[:, :], start=False, stop=False)
                else:
                    pe.wait_ge(dve_S.sem, dve_S.at(g, "os"))
                    pe.matmul(to, tile_of(ST[u][:, :, :].rearrange("p b t -> p (b t)"), i), OS[u % 2][:, :],
                              start=False, stop=True).then_inc(pe_F2.sem, 1)

            plan_A = {3: ["tm"], 5: ["zt"], 6: ["sl"], 9: ["st"], 11: ["tr1", "tr2"]}
            plan_S = {0: "ga", 1: "u", 2: "sc", 4: "et", 5: "g", 6: "gt", 7: "at", 9: "xt", 10: "f1", 11: "f2"}
            n_F2 = 8 * FT

            def body(p, u, q):
                done = 0
                for s in range(2 * HT):
                    if s in plan_S and active(p, 2):
                        step_S(p - 2, (u - 2) % 4, plan_S[s])
                    for part in range(2):
                        upto = n_F2 * (2 * s + part + 1) // (4 * HT)
                        while done < upto:
                            if active(p, 3):
                                step_F2(p - 3, (u - 3) % 4, done)
                            done += 1
                        if part == 0:
                            for name in plan_A.get(s, []):
                                if active(p, 1):
                                    step_A(p - 1, (u - 1) % 4, name)
                            if active(p, 2):
                                step_F1(p - 2, (u - 2) % 4, s)

            pe.wait_ge(w_in, NW_IN * 16)
            weights()
            pe.wait_ge(dve_W.sem, dve_W.at(0, "alR"))
            periods(nc.tensor, body)

        @block.scalar
        def _(act):
            def step_A(g, u, name):
                if name == "e":
                    act.wait_ge(dve_A.sem, dve_A.at(g, "D0"))
                    act.activation(Ex2[:, :, :], Dm[:, :, :], ACT.Exp).then_inc(act_A.sem, 1)
                elif name == "fm":
                    act.wait_ge(pe_A.sem, pe_A.at(g, "zt"))
                    if exists(g - 2):
                        act.wait_ge(pe_S.sem, pe_S.at(g - 2, "sc"))
                    act.activation(FM[u % 2][:, :], psB[0:ZR, 0:T], ACT.Copy).then_inc(act_A.sem, 1)
                else:
                    act.wait_ge(pe_A.sem, pe_A.at(g, "tr2"))
                    act.activation(Stk2[u][:, :], psB[:, :].bitcast(bf16)[0:SK, 0:GT], ACT.Copy).then_inc(act_A.sem, 1)

            def step_S(g, u, name):
                if name == "exp":
                    act.wait_ge(dve_S.sem, dve_S.at(g, "nm"))
                    for j in range(HP):
                        act.activation(Sm[:, j, :], Sm[:, j, :], ACT.Exp, bias=nm[:, j:j + 1],
                                       accum_out=rsum[:, j:j + 1]).then_inc(act_S.sem, 1)
                elif name == "t":
                    act.wait_ge(pe_S.sem, pe_S.at(g, "et"))
                    if exists(g - 1):
                        act.wait_ge(pe_S.sem, pe_S.at(g - 1, "g"))
                    for n in range(3):
                        act.activation(ET[:, 4 * n:4 * n + 4, :], psS[0:HALF, n, 0:4 * ROWS]
                                       .rearrange("p (k s) -> p k s", k=4), ACT.Copy).then_inc(act_S.sem, 1)
                elif name == "se":
                    act.wait_ge(dve_S.sem, dve_S.at(g, "dm"))
                    act.activation(dexp[:, :], dmin[:, :], ACT.Exp).then_inc(act_S.sem, 1)
                else:
                    act.wait_ge(pe_S.sem, pe_S.at(g, "f1"))
                    if exists(g - 1):
                        act.wait_ge(pe_S.sem, pe_S.at(g - 1, "f2"))
                    act.activation(actS[:, :, :], psS[:, 2, 0:HT * SLOTS].rearrange("p (h s) -> p h s", h=HT),
                                   ACT.Gelu).then_inc(act_S.sem, 1)

            def step_F1(g, u, n):
                act.wait_ge(pe_F1.sem, pe_F1.at(g, f"n{n}"))
                act.activation(act_sb[u % 2][:, n // 2, (n % 2) * (GT // 2):(n % 2 + 1) * (GT // 2)],
                               psF[n % 2][:, 0:GT // 2], ACT.Gelu).then_inc(act_F1.sem, 1)

            def step_F2(g, u, i):
                act.wait_ge(pe_F2.sem, pe_F2.at(g, f"o{i}"))
                if i == 3:
                    if exists(g - 1):
                        act.wait_ge(y_out[(u - 1) % 2], landed(g - 1, (u - 1) % 2))
                act.activation(obuf[u % 2][:, i, :], psO[0:OT, 0:D], ACT.Copy).then_inc(act_F2.sem, 1)
                if i == FT - 1:
                    act.wait_ge(act_F2.sem, act_F2.at(g, f"o{i}"))
                    act.dma_start(og[bass.ds(g, 1)].rearrange("o p q -> (o p) q"),
                                  obuf[u % 2][:, :, :].rearrange("p i e -> p (i e)")).then_inc(y_out[u % 2], 16)

            plan_A = {5: ["e", "fm"], 11: ["k2"]}
            plan_S = {3: "exp", 4: "t", 7: "se", 10: "ge"}

            def body(p, u, q):
                done = 0
                for s in range(2 * HT):
                    if s in plan_S and active(p, 2):
                        step_S(p - 2, (u - 2) % 4, plan_S[s])
                    for part in range(2):
                        upto = 8 * FT * (2 * s + part + 1) // (4 * HT) // 8
                        while done < upto:
                            if active(p, 3):
                                step_F2(p - 3, (u - 3) % 4, done)
                            done += 1
                        if part == 0:
                            for name in plan_A.get(s, []):
                                if active(p, 1):
                                    step_A(p - 1, (u - 1) % 4, name)
                            if active(p, 2):
                                step_F1(p - 2, (u - 2) % 4, s)

            periods(nc.scalar, body)

        @block.vector
        def _(dve):
            def weights():


                dve.memset(WR[:, :], 0.0).then_inc(dve_W.sem, 1)
                dve.memset(WS[:, :], 0.0).then_inc(dve_W.sem, 1)
                dve.memset(XH[:, :, :], 1.0).then_inc(dve_W.sem, 1)
                dve.wait_ge(w_in, NW_IN * 16)
                for t in P:
                    dve.tensor_copy(t[:, :], kc("f0", PF))
                for t in F:
                    dve.memset(t[:, :, 0:Z1], 0.0)
                    dve.memset(t[:, :, Z1 + 1:PR], 0.0)
                    dve.memset(t[:, :, Z1:Z1 + 1], 1.0)
                dve.memset(sel[:, :], -7.0)
                dve.memset(m8b[:, :], -7.0).then_inc(dve_W.sem, 1)
                dve.tensor_copy(identb[:, :], kc("ident")).then_inc(dve_W.sem, 1)
                dve.tensor_reduce(mean_r[:, :], WR[:, :], AX.X, ALU.add).then_inc(dve_W.sem, 1)
                dve.wait_ge(dve_W.sem, dve_W.at(0, "mr"))
                dve.tensor_scalar(mean_r[:, :], mean_r[:, :], 1.0 / D, None, ALU.mult).then_inc(dve_W.sem, 1)
                dve.wait_ge(dve_W.sem, dve_W.at(0, "mr2"))
                dve.tensor_scalar(WcR[:, :], WR[:, :], mean_r[:, 0:1], None, ALU.subtract).then_inc(dve_W.sem, 1)
                dve.wait_ge(dve_W.sem, dve_W.at(0, "wcr"))
                dve.tensor_copy(BW[0:ZR, :], WcR[0:ZR, :]).then_inc(dve_W.sem, 1)
                dve.tensor_copy(BW[PR:FR, :], WR[PR:FR, :]).then_inc(dve_W.sem, 1)
                dve.tensor_reduce(mean_s[:, :], WS[:, :], AX.X, ALU.add).then_inc(dve_W.sem, 1)
                dve.wait_ge(dve_W.sem, dve_W.at(0, "ms"))
                dve.tensor_scalar(mean_s[:, :], mean_s[:, :], 1.0 / D, None, ALU.mult).then_inc(dve_W.sem, 1)
                dve.wait_ge(dve_W.sem, dve_W.at(0, "ms2"))
                dve.tensor_scalar(WcS[:, :], WS[:, :], mean_s[:, 0:1], None, ALU.subtract).then_inc(dve_W.sem, 1)
                dve.wait_ge(dve_W.sem, dve_W.at(0, "wcs"))
                dve.tensor_scalar(WS[:, :], WcS[:, :], kc("e13", SK), None, ALU.add).then_inc(dve_W.sem, 1)
                dve.wait_ge(pe_W.sem, pe_W.at(0, "ws"))
                dve.tensor_copy(WT4[0:DH, :, :], psA[0:DH, 0:2 * FR].rearrange("p (k c) -> p k c", k=2)).then_inc(dve_W.sem, 1)
                dve.tensor_copy(WST[0:DH, :, :], psB[0:DH, 0:2 * SK].rearrange("p (k c) -> p k c", k=2)).then_inc(dve_W.sem, 1)
                dve.wait_ge(pe_W.sem, pe_W.at(0, "c"))
                dve.memset(TMR[:, :], 0.0).then_inc(dve_W.sem, 1)
                dve.wait_ge(dve_W.sem, dve_W.at(0, "cf"))
                dve.scalar_tensor_tensor(out=TMR[0:BC, BC:2 * BC], in0=psO[0:BC, 0:BC], scalar=1.0 / D, in1=kc("same", BC),
                                         op0=ALU.mult, op1=ALU.mult).then_inc(dve_W.sem, 1)
                dve.wait_ge(pe_W.sem, pe_W.at(0, "sel"))
                dve.tensor_copy(sel_raw[:, :], psF[0][0:ZR, 0:2]).then_inc(dve_W.sem, 1)
                dve.wait_ge(dve_W.sem, dve_W.at(0, "raw"))
                dve.tensor_tensor(sel_d[:, :], sel_raw[:, 1:2], sel_raw[:, 0:1], ALU.subtract).then_inc(dve_W.sem, 1)
                dve.wait_ge(dve_W.sem, dve_W.at(0, "sd"))
                dve.reciprocal(temp_sb[:, :], temp_sb[:, :]).then_inc(dve_W.sem, 1)
                dve.wait_ge(dve_W.sem, dve_W.at(0, "sd2"))
                dve.tensor_tensor(selM2[:, 1:2], sel_d[:, :], temp_sb[:, :], ALU.mult).then_inc(dve_W.sem, 1)
                dve.wait_ge(dve_W.sem, dve_W.at(0, "s1"))
                dve.tensor_scalar(selM2[:, 0:1], selM2[:, 1:2], -1.0, None, ALU.mult).then_inc(dve_W.sem, 1)
                dve.wait_ge(dve_W.sem, dve_W.at(0, "s0"))
                dve.tensor_copy(TMR[0:BC, 0:BC], kc("ident")[0:BC, 0:BC]).then_inc(dve_W.sem, 1)
                aux = TMR[:, 2 * BC:TMC].rearrange("p (b c) -> p b c", c=AUX)
                dve.tensor_copy(aux[:, :, 2], kc("f0", PF)[:, 0:GB]).then_inc(dve_W.sem, 1)
                dve.tensor_scalar(aux[0:BC, :, 0], kc("bsel", BC), mean_r[0:BC, 0:1], None, ALU.mult).then_inc(dve_W.sem, 1)
                dve.tensor_scalar(aux[0:BC, :, 1], kc("bsel", BC), selM2[0:BC, 1:2], None, ALU.mult).then_inc(dve_W.sem, 1)
                dve.wait_ge(dve_W.sem, dve_W.at(0, "tz"))
                dve.tensor_scalar(aux[:, :, 2], aux[:, :, 2], selM2[0:PF, 1:2], None, ALU.mult).then_inc(dve_W.sem, 1)
                banks = [(psS[:, 0], psS[:, 1]), (psS[:, 2], psA[:, :]), (psB[:, :], psF[1][:, :])]
                for m, (name, to) in enumerate([("q", MqT), ("k", MkT), ("v", MvT)]):
                    dve.wait_ge(pe_W.sem, pe_W.at(0, name))
                    for k in range(2):
                        ins = dve.tensor_copy(to[:, k * HP:(k + 1) * HP, :],
                                              banks[m][k][0:HD, 0:HP * ZR].rearrange("p (h c) -> p h c", h=HP))
                    ins.then_inc(dve_W.sem, 1)
                dve.wait_ge(pe_W.sem, pe_W.at(0, "a4"))
                for k in range(2):
                    ins = dve.tensor_scalar(A4[:, k * HP:(k + 1) * HP, :], (psA, psB)[k][0:ZR, 0:HP * ZR]
                                            .rearrange("p (h c) -> p h c", h=HP), float(HD) ** -0.5, None, ALU.mult)
                ins.then_inc(dve_W.sem, 1)
                dve.wait_ge(pe_W.sem, pe_W.at(0, "b2"))
                dve.tensor_copy(B2[:, :, :].rearrange("p (k j) e -> p k (j e)", k=3), psS[:, :, 0:2 * D]).then_inc(dve_W.sem, 1)
                dve.wait_ge(pe_W.sem, pe_W.at(0, "m1"))
                for k in range(2):
                    ins = dve.tensor_copy(M1f[:, k * HID // 2:(k + 1) * HID // 2], (psA, psB)[k][0:SK, 0:HID // 2])
                ins.then_inc(dve_W.sem, 1)
                dve.wait_ge(dve_W.sem, dve_W.at(0, "m1"))
                for t, f, to, n in (("M", M1f, M1S, HID), ("R", WS, RS, D)):
                    part, rest = M1h[:, 0:n], M1r[:, 0:n]
                    dve.tensor_copy(part, f[:, :]).then_inc(dve_W.sem, 1)
                    dve.wait_ge(dve_W.sem, dve_W.at(0, "h" + t))
                    dve.tensor_tensor(rest, f[:, :], part, ALU.subtract).then_inc(dve_W.sem, 1)
                    dve.tensor_scalar(to[:, :], part, kc("mh", SK), None, ALU.mult).then_inc(dve_W.sem, 1)
                    dve.wait_ge(dve_W.sem, dve_W.at(0, "ah" + t))
                    dve.tensor_copy(part, rest).then_inc(dve_W.sem, 1)
                    dve.wait_ge(dve_W.sem, dve_W.at(0, "m" + t))
                    dve.tensor_tensor(rest, rest, part, ALU.subtract).then_inc(dve_W.sem, 1)
                    dve.scalar_tensor_tensor(out=to[:, :], in0=part, scalar=kc("mm", SK), in1=to[:, :],
                                               op0=ALU.mult, op1=ALU.add).then_inc(dve_W.sem, 1)
                    dve.wait_ge(dve_W.sem, dve_W.at(0, "am" + t))
                    dve.tensor_copy(part, rest).then_inc(dve_W.sem, 1)
                    dve.wait_ge(dve_W.sem, dve_W.at(0, "l" + t))
                    dve.scalar_tensor_tensor(out=to[:, :], in0=part, scalar=kc("ml", SK), in1=to[:, :],
                                               op0=ALU.mult, op1=ALU.add).then_inc(dve_W.sem, 1)
                    dve.wait_ge(dve_W.sem, dve_W.at(0, "al" + t))

            def sum_tile(g, u, k):
                dve.wait_ge(pool_L.sem, pool_L.at(g, f"x{k}"))
                if k == 0:
                    if exists(g - 2):
                        dve.wait_ge(sums_out[u % 2], landed(g - 2, u % 2))
                v = X[:, (XT * u + k) % NX, :].rearrange("p (q r j l) -> p q j r l", q=TQ, r=QR, j=N)
                dve.tensor_reduce(R[:, u % 2, k * TQ * N:(k + 1) * TQ * N].rearrange("p (q j) -> p q j", q=TQ),
                                  v[:, :, :, 0:2, :], AX.XY, ALU.add).then_inc(dve_L.sem, 1)

            def rsqrt(steps, g, t, x, half, a, b, y):
                dve.tensor_scalar(half, x, -0.5, None, ALU.mult).then_inc(steps.sem, 1)
                dve.tensor_scalar(y.bitcast(i32), x.bitcast(i32), -0.5, float(0x5F3759DF), ALU.mult, ALU.add).then_inc(steps.sem, 1)
                for k in range(3):
                    dve.wait_ge(steps.sem, steps.at(g, f"{t}y{k - 1}" if k else t + "g0"))
                    dve.tensor_tensor(a, y, y, ALU.mult).then_inc(steps.sem, 1)
                    dve.wait_ge(steps.sem, steps.at(g, f"{t}a{k}"))
                    dve.tensor_tensor(b, a, half, ALU.mult).then_inc(steps.sem, 1)
                    dve.wait_ge(steps.sem, steps.at(g, f"{t}b{k}"))
                    dve.scalar_tensor_tensor(out=y, in0=b, scalar=1.5, in1=y, op0=ALU.add, op1=ALU.mult).then_inc(steps.sem, 1)

            def stage_A(g, u, part):
                r = u % 2
                f = F[r]
                p = f[:, :, PR:FR].rearrange("p k (b c) -> p k b c", b=GB)
                aux = f[:, :, FR + BC:FC].rearrange("p k (b c) -> p k b c", b=GB)

                def by_c(t):
                    return t[:, :].rearrange("p (k b) -> p k b", k=2).unsqueeze(3).broadcast_to([HALF, 2, GB, C])

                def kb(t):
                    return t[:, :].rearrange("p (k b) -> p k b", k=2)

                if part == "norm":
                    dve.wait_ge(pe_A.sem, pe_A.at(g, "tm"))
                    if exists(g - 2):
                        dve.wait_ge(pe_S.sem, pe_S.at(g - 2, "g"))
                    dve.tensor_copy(f[:, :, PR:FC], psB[0:HALF, 0:2 * TMC].rearrange("p (k c) -> p k c", k=2)).then_inc(dve_A.sem, 1)
                    dve.wait_ge(dve_A.sem, dve_A.at(g, "cp"))
                    dve.tensor_tensor(prod[:, :, :], f[:, :, PR:FR], f[:, :, FR:FR + BC], ALU.mult).then_inc(dve_A.sem, 1)
                    dve.wait_ge(dve_A.sem, dve_A.at(g, "pr"))
                    dve.tensor_reduce(sc["var"][:, :], prod[:, :, :].rearrange("p k (b c) -> p (k b) c", c=C), AX.X, ALU.add).then_inc(dve_A.sem, 1)
                    dve.wait_ge(dve_A.sem, dve_A.at(g, "var"))
                    dve.tensor_scalar(sc["ve"][:, :], sc["var"][:, :], EPS, None, ALU.add).then_inc(dve_A.sem, 1)
                    dve.wait_ge(dve_A.sem, dve_A.at(g, "ve"))
                    rsqrt(dve_A, g, "r", sc["ve"][:, :], sc["hv"][:, :], sc["ya"][:, :], sc["yb"][:, :], sc["rstd"][:, :])
                    dve.wait_ge(dve_A.sem, dve_A.at(g, "ry2"))
                    dve.tensor_tensor(f[:, :, 0:BC].rearrange("p k (b c) -> p k b c", b=GB), p, by_c(sc["rstd"]), ALU.mult).then_inc(dve_A.sem, 1)
                    dve.tensor_tensor(kb(sc["lr"]), aux[:, :, :, 1], kb(sc["rstd"]), ALU.mult).then_inc(dve_A.sem, 1)
                    dve.wait_ge(dve_A.sem, dve_A.at(g, "lr"))
                    dve.tensor_tensor(kb(sc["L"]), kb(sc["lr"]), aux[:, :, :, 2], ALU.add).then_inc(dve_A.sem, 1)
                    dve.wait_ge(dve_A.sem, dve_A.at(g, "L"))
                    dve.tensor_scalar(Dm[:, 1, :], sc["L"][:, :], 0.0, None, ALU.min).then_inc(dve_A.sem, 1)
                    dve.tensor_scalar(Dm[:, 0, :], sc["L"][:, :], -1.0, 0.0, ALU.mult, ALU.min).then_inc(dve_A.sem, 1)
                elif part == "norm2":
                    dve.tensor_scalar(sc["t1"][:, :], sc["rstd"][:, :], 1.0, None, ALU.add).then_inc(dve_A.sem, 1)
                    dve.wait_ge(dve_A.sem, dve_A.at(g, "t1"))
                    dve.tensor_tensor(sc["t2"][:, :], sc["t1"][:, :], sc["t1"][:, :], ALU.mult).then_inc(dve_A.sem, 1)
                    dve.wait_ge(dve_A.sem, dve_A.at(g, "t2"))
                    dve.tensor_tensor(sc["s2"][:, :], sc["t2"][:, :], sc["var"][:, :], ALU.mult).then_inc(dve_A.sem, 1)
                    dve.wait_ge(dve_A.sem, dve_A.at(g, "s2"))
                    dve.tensor_scalar(sc["s3"][:, :], sc["s2"][:, :], EPS, None, ALU.add).then_inc(dve_A.sem, 1)
                    dve.wait_ge(dve_A.sem, dve_A.at(g, "s3"))
                    rsqrt(dve_A, g, "q", sc["s3"][:, :], sc["hv2"][:, :], sc["ya"][:, :], sc["yb"][:, :], sc["r2"][:, :])
                    dve.wait_ge(dve_A.sem, dve_A.at(g, "qy2"))
                    dve.tensor_tensor(sc["al"][:, :], sc["t1"][:, :], sc["r2"][:, :], ALU.mult).then_inc(dve_A.sem, 1)
                elif part == "sel":
                    dve.wait_ge(act_A.sem, act_A.at(g, "e"))
                    dve.tensor_tensor(sc["den"][:, :], Ex2[:, 0, :], Ex2[:, 1, :], ALU.add).then_inc(dve_A.sem, 1)
                    dve.wait_ge(dve_A.sem, dve_A.at(g, "den"))
                    dve.reciprocal(sc["rden"][:, :], sc["den"][:, :]).then_inc(dve_A.sem, 1)
                    dve.wait_ge(dve_A.sem, dve_A.at(g, "rden"))
                    dve.tensor_tensor(selT[:, :], Ex2[:, 1, :], sc["rden"][:, :], ALU.mult).then_inc(dve_A.sem, 1)
                elif part == "top":
                    dve.wait_ge(pe_A.sem, pe_A.at(g, "sl"))
                    dve.tensor_copy(sel[:, 0:T], psA[0:GB, 0:T]).then_inc(dve_A.sem, 1)
                    dve.wait_ge(dve_A.sem, dve_A.at(g, "row"))
                    by_itself(dve)
                    dve.max(m8a[:, :], sel[:, :]).then_inc(dve_A.sem, 1)
                    dve.wait_ge(dve_A.sem, dve_A.at(g, "m8a"))
                    by_itself(dve)
                    dve.match_replace(sl1[:, :], m8a[:, :], sel[:, :], -1.0).then_inc(dve_A.sem, 1)
                    dve.wait_ge(dve_A.sem, dve_A.at(g, "mr1"))
                    by_itself(dve)
                    dve.max(m8b[:, :], sl1[:, :]).then_inc(dve_A.sem, 1)
                    dve.wait_ge(dve_A.sem, dve_A.at(g, "m8b"))
                    dve.memset(m8b[:, KSEL - 8:8], -7.0).then_inc(dve_A.sem, 1)
                    dve.wait_ge(dve_A.sem, dve_A.at(g, "fx"))
                    by_itself(dve)
                    dve.match_replace(sl2[:, :], m8b[:, :], sl1[:, :], -1.0).then_inc(dve_A.sem, 1)
                    dve.wait_ge(dve_A.sem, dve_A.at(g, "mr2"))
                    dve.tensor_scalar(mask[:, :], sl2[:, 0:T], 0.0, None, ALU.is_lt).then_inc(dve_A.sem, 1)
                    dve.wait_ge(dve_A.sem, dve_A.at(g, "mk"))
                    dve.tensor_tensor_scan(cum[:, :], kc("ones", GB), mask[:, :], 0.0, ALU.mult, ALU.add).then_inc(dve_A.sem, 1)
                    dve.wait_ge(dve_A.sem, dve_A.at(g, "cs"))
                    dve.tensor_tensor(srow[:, :], cum[:, :], mask[:, :], ALU.mult).then_inc(dve_A.sem, 1)
                elif part == "slots":
                    dve.wait_ge(pe_A.sem, pe_A.at(g, "st"))
                    col = psA[0:HALF, 400:400 + 2 * GB]
                    if exists(g - 2):
                        dve.wait_ge(pe_S.sem, pe_S.at(g - 2, "ga"))
                    for d in range(2):
                        dve.tensor_tensor(Sg[r][:, :, d, :].rearrange("p k (b s) -> p k b s", b=GB),
                                            col.rearrange("p (k b) -> p k b", k=2).unsqueeze(3).broadcast_to([HALF, 2, GB, KSEL]),
                                            kc("iota14", HALF).unsqueeze(1).unsqueeze(1).broadcast_to([HALF, 2, GB, KSEL]),
                                            ALU.is_equal).then_inc(dve_A.sem, 1)
                    dve.tensor_scalar(keep[:, :], col, 0.0, None, ALU.is_equal).then_inc(dve_A.sem, 1)
                    dve.scalar_tensor_tensor(out=ST[u][:, :, :], in0=psA[0:SLOTS, 0:T].unsqueeze(1).broadcast_to([SLOTS, GB, T]),
                                               scalar=kc("r1", SLOTS), in1=kc("bmt", SLOTS).unsqueeze(2).broadcast_to([SLOTS, GB, T]),
                                               op0=ALU.is_equal, op1=ALU.mult).then_inc(dve_A.sem, 1)
                elif part == "parts":
                    dve.wait_ge(dve_A.sem, dve_A.at(g, "kp"))
                    dve.tensor_tensor(sc["kw"][:, :], sc["al"][:, :], keep[:, :], ALU.mult).then_inc(dve_A.sem, 1)
                    dve.tensor_tensor(sc["ky"][:, :], sc["t1"][:, :], keep[:, :], ALU.mult).then_inc(dve_A.sem, 1)
                    v = v26[:, :, :].rearrange("p (k b s) c -> p s k b c", k=2, b=GB)
                    dve.wait_ge(dve_A.sem, dve_A.at(g, "ky"))
                    dve.tensor_tensor(v[:, 0, :, :, 0:C], p, by_c(sc["kw"]), ALU.mult).then_inc(dve_A.sem, 1)
                    dve.tensor_tensor(v[:, 1, :, :, 0:C], p, by_c(sc["ky"]), ALU.mult).then_inc(dve_A.sem, 1)
                    dve.tensor_copy(v[:, 0, :, :, C], kb(keep)).then_inc(dve_A.sem, 1)
                    dve.tensor_tensor(v[:, 1, :, :, C], aux[:, :, :, 0], kb(keep), ALU.mult).then_inc(dve_A.sem, 1)
                    if exists(g - 1):
                        dve.wait_ge(pe_A.sem, pe_A.at(g - 1, "tr2"))
                    dve.wait_ge(dve_A.sem, dve_A.at(g, "mean"))

                    def part_of(src, n0, n1):
                        return dve.tensor_copy(SP[:, :, n0:n1, :],
                                               src[:, :, :].unsqueeze(2).broadcast_to([HALF, 4 * GB, n1 - n0, W1]))

                    part_of(v26, 0, 3).then_inc(dve_A.sem, 1)
                    dve.wait_ge(dve_A.sem, dve_A.at(g, "H"))
                    dve.tensor_tensor(d1[:, :, :], v26[:, :, :], SP[:, :, 0, :], ALU.subtract).then_inc(dve_A.sem, 1)
                    dve.wait_ge(dve_A.sem, dve_A.at(g, "d1"))
                    part_of(d1, 3, 6).then_inc(dve_A.sem, 1)
                    dve.wait_ge(dve_A.sem, dve_A.at(g, "M"))
                    dve.tensor_tensor(d2[:, :, :], d1[:, :, :], SP[:, :, 3, :], ALU.subtract).then_inc(dve_A.sem, 1)
                    dve.wait_ge(dve_A.sem, dve_A.at(g, "d2"))
                    part_of(d2, 6, 8).then_inc(dve_A.sem, 1)
                else:
                    dve.wait_ge(pe_A.sem, pe_A.at(g, "tr1"))
                    if exists(g - 2):
                        dve.wait_ge(pe_F1.sem, pe_F1.at(g - 2, f"n{2 * HT - 1}"))
                    dve.tensor_copy(Stk1[r][:, :], psA[:, :].bitcast(bf16)[0:SK, 0:GT]).then_inc(dve_A.sem, 1)

            def stage_S(g, u, part):


                r = u % 2
                if part == "ga":
                    dve.wait_ge(pe_S.sem, pe_S.at(g, "ga"))
                    dve.tensor_tensor(ZY[:, :], psS[0:FR, 0, 0:SLOTS], kc("bmzy", FR), ALU.mult).then_inc(dve_S.sem, 1)
                    dve.tensor_scalar(RM[:, :], kc("iota", ROWS), psS[0:ROWS, 0, ZR:ZR + 1], NEG, ALU.is_gt, ALU.mult).then_inc(dve_S.sem, 1)
                elif part == "u":
                    dve.wait_ge(pe_S.sem, pe_S.at(g, "u"))
                    for k in range(2):
                        dve.tensor_tensor(UB[:, :, k, :], psS[0:ZR, 1 + k, 0:HP * SLOTS].rearrange("p (j s) -> p j s", j=HP),
                                            kc("bm2", ZR).unsqueeze(1).broadcast_to([ZR, HP, SLOTS]), ALU.mult).then_inc(dve_S.sem, 1)
                elif part == "sc":
                    dve.wait_ge(pe_S.sem, pe_S.at(g, "sc"))
                    dve.wait_ge(dve_S.sem, dve_S.at(g, "rm"))
                    dve.tensor_tensor(Sm[:, :, :].rearrange("p (k j) t -> p k j t", k=3),
                                        psS[0:ROWS, :, 0:2 * T].rearrange("p k (j t) -> p k j t", j=2),
                                        RM[:, :].unsqueeze(1).unsqueeze(1).broadcast_to([ROWS, 3, 2, T]), ALU.add).then_inc(dve_S.sem, 1)
                    dve.wait_ge(dve_S.sem, dve_S.at(g, "sm"))
                    dve.tensor_reduce(mx[:, :], Sm[:, :, :], AX.X, ALU.max).then_inc(dve_S.sem, 1)
                    dve.wait_ge(dve_S.sem, dve_S.at(g, "mx"))
                    dve.tensor_scalar(nm[:, :], mx[:, :], -1.0, None, ALU.mult).then_inc(dve_S.sem, 1)
                elif part == "g":
                    dve.wait_ge(act_S.sem, act_S.at(g, "e5"))
                    dve.reciprocal(rinv[:, :], rsum[:, :]).then_inc(dve_S.sem, 1)
                    dve.wait_ge(pe_S.sem, pe_S.at(g, "g"))
                    dve.wait_ge(dve_S.sem, dve_S.at(g, "ri"))
                    dve.tensor_tensor(GN[:, :, :], psS[0:ROWS, 0, 0:HP * ZR].rearrange("p (j c) -> p j c", j=HP),
                                        rinv[:, :].unsqueeze(2).broadcast_to([ROWS, HP, ZR]), ALU.mult).then_inc(dve_S.sem, 1)
                elif part == "gt":
                    dve.wait_ge(pe_S.sem, pe_S.at(g, "gt"))
                    for k in range(2):
                        dve.tensor_tensor(G2[ZR * k:ZR * k + ZR, :, :].rearrange("p (i j) s -> p i j s", i=2),
                                            psS[0:ZR, 1:3, 0:3 * ROWS].rearrange("p i (j s) -> p i j s", j=3)[:, :, :, SLOTS * k:SLOTS * (k + 1)],
                                            kc("bm2", ZR).unsqueeze(1).unsqueeze(1).broadcast_to([ZR, 2, 3, SLOTS]), ALU.mult).then_inc(dve_S.sem, 1)
                elif part == "at":
                    dve.wait_ge(pe_S.sem, pe_S.at(g, "at"))
                    dve.tensor_scalar(dmin[:, :], psS[0:SLOTS, 0, 2 * D:2 * D + 2], 0.0, None, ALU.min).then_inc(dve_S.sem, 1)
                    dve.tensor_tensor(AO[:, :], psS[0:SLOTS, 0, 0:D], OB[:, :], ALU.add).then_inc(dve_S.sem, 1)
                elif part == "norm":
                    dve.wait_ge(act_S.sem, act_S.at(g, "se"))
                    dve.tensor_tensor(dden[:, :], dexp[:, 0:1], dexp[:, 1:2], ALU.add).then_inc(dve_S.sem, 1)
                    dve.wait_ge(dve_S.sem, dve_S.at(g, "dn"))
                    dve.reciprocal(rdden[:, :], dden[:, :]).then_inc(dve_S.sem, 1)
                    dve.wait_ge(dve_S.sem, dve_S.at(g, "rn"))
                    dve.tensor_tensor(dsel[:, :], dexp[:, 1:2], rdden[:, :], ALU.mult).then_inc(dve_S.sem, 1)
                    dve.wait_ge(dve_S.sem, dve_S.at(g, "sv"))
                    dve.scalar_tensor_tensor(out=h1[:, :], in0=AO[:, :], scalar=dsel[:, 0:1], in1=psS[0:SLOTS, 0, D:2 * D],
                                               op0=ALU.mult, op1=ALU.add).then_inc(dve_S.sem, 1)
                    dve.wait_ge(dve_S.sem, dve_S.at(g, "h1"))
                    dve.bn_stats(bst[:, :], h1[:, :]).then_inc(dve_S.sem, 1)
                    dve.wait_ge(dve_S.sem, dve_S.at(g, "bs"))
                    by_itself(dve)
                    dve.bn_aggr(mv[:, :], bst[:, :]).then_inc(dve_S.sem, 1)
                    dve.wait_ge(dve_S.sem, dve_S.at(g, "ba"))
                    dve.tensor_scalar(vrs[:, :], mv[:, 1:2], EPS, None, ALU.add).then_inc(dve_S.sem, 1)
                    dve.wait_ge(dve_S.sem, dve_S.at(g, "vr"))
                    rsqrt(dve_S, g, "r", vrs[:, :], hvs[:, :], yas[:, :], ybs[:, :], rst[:, :])
                    dve.wait_ge(dve_S.sem, dve_S.at(g, "ry2"))
                    dve.tensor_scalar(xh[:, :], h1[:, :], mv[:, 0:1], rst[:, 0:1], ALU.subtract, ALU.mult).then_inc(dve_S.sem, 1)
                elif part == "xt":
                    dve.wait_ge(pe_S.sem, pe_S.at(g, "xt"))
                    dve.tensor_copy(XH[0:DH, :, :], psS[0:DH, 1, 0:2 * SLOTS].rearrange("p (k s) -> p k s", k=2)).then_inc(dve_S.sem, 1)
                else:
                    dve.wait_ge(pe_S.sem, pe_S.at(g, "f2"))
                    dve.tensor_tensor(OS[r][:, :], psS[0:SLOTS, 0, 0:D], h1[:, :], ALU.add).then_inc(dve_S.sem, 1)

            plan_A = {3: ["norm"], 5: ["norm2", "sel"], 6: ["top"], 9: ["slots", "parts"], 11: ["k1"]}
            plan_S = {0: "ga", 1: "u", 2: "sc", 5: "g", 6: "gt", 7: "at", 8: "norm", 10: "xt", 11: "f2"}
            plan_L = {1: 0, 2: 1, 4: 2, 6: 3, 8: 4, 10: 5, 11: 6}

            def body(p, u, q):
                for s in range(2 * HT):
                    if s in plan_S and active(p, 2):
                        stage_S(p - 2, (u - 2) % 4, plan_S[s])
                    if s in plan_L and active(p, 0):
                        sum_tile(p, u, plan_L[s])
                    for part in plan_A.get(s, []):
                        if active(p, 1):
                            stage_A(p - 1, (u - 1) % 4, part)

            weights()
            periods(nc.vector, body)


def kernel(x, L0_tok_channel_weights, L0_attn_Wqkv_w, L0_attn_Wqkv_b, L0_attn_sel_w, L0_attn_sel_b, L0_attn_out_w,
           L0_attn_out_b, L0_attn_temperature, L0_ffn_in_weight, L0_ffn_in_bias, L0_ffn_out_weight):
    import concourse.bacc as bacc
    from concourse.bass_utils import run_bass_kernel_spmd as run

    e48, e13r = np.zeros((1, FR), np.float32), np.zeros((1, SK), np.float32)
    e48[0, Z1] = 1
    e13r[0, C::W1] = 1
    arrays = {
        "x": x, "cw": L0_tok_channel_weights, "wqkv": L0_attn_Wqkv_w, "bqkv": np.reshape(L0_attn_Wqkv_b, (1, -1)),
        "selw": L0_attn_sel_w, "selb": np.reshape(L0_attn_sel_b, (1, -1)), "ow": L0_attn_out_w,
        "ob": np.reshape(L0_attn_out_b, (1, -1)), "temp": np.reshape(L0_attn_temperature, (1, 1)),
        "w1t": np.transpose(L0_ffn_in_weight), "b1": np.reshape(L0_ffn_in_bias, (1, -1)), "w2": L0_ffn_out_weight,
        "consts": constants(), "e48": e48, "e13r": e13r,
    }
    arrays = {f"in_{k}": np.ascontiguousarray(v) for k, v in arrays.items()}
    nc = bacc.Bacc("TRN2", target_bir_lowering=False, num_devices=1)
    args = [nc.dram_tensor(k, v.shape, mybir.dt.from_np(v.dtype), kind="ExternalInput").ap() for k, v in arrays.items()]
    args.append(nc.dram_tensor("out_0", (B, T, D), mybir.dt.float32, kind="ExternalOutput").ap())
    program(nc, *args)
    return run(nc, [arrays], core_ids=[0]).results[0]["out_0"]
```

```python
import numpy as np
import concourse.bass as bass
from concourse import mybir
from contextlib import ExitStack

B, C, IMG, PATCH, D, HEADS, HID = 64, 12, 224, 16, 192, 12, 768
N = IMG // PATCH
T = N * N
HD = D // HEADS
KSEL = int(np.ceil(np.sqrt(T)))
GB = 4
LAST = 4
NG = B // GB
BC = GB * C
SLOTS = GB * KSEL
HALF = T // 2
GT = GB * T
Z1 = BC
NW_IN = 1 + 2 * GB + 8 + 12
ZR = 64
PR = ZR
FR = PR + BC
AUX = 3
PF = BC + 1
TMC = 2 * BC + GB * AUX
FC = PR + TMC
W1 = C + 1
PAIRS = 8
PART_OF = [0, 0, 0, 1, 1, 1, 2, 2]
WPART_OF = [0, 1, 2, 0, 1, 2, 0, 1]
SK = PAIRS * W1
DH = D // 2
HP = HEADS // 2
ROWS = 2 * SLOTS
HT = HID // 128
FT = 7
FP = T // FT
OT = GB * FP
QR = 4
QB = QR * IMG
NQ = GB * C * IMG // QR // 128
TQ = 3
XT = NQ // TQ
NX = 4
NR = 4 * GB + 1
AT_F1 = [4, 5, 7, 8, 9, 10, 11, 12, 13, 21, 22, 23]
IN_F2 = [3, 5, 0, 2, 3, 0, 3, 4, 4, 5, 4, 3, 5, 0, 2, 5, 4, 4, 0, 0, 0, 0, 0, 0]
PLAN = len(IN_F2)
EPS = 1e-5
NEG = -10000.0

COLS = {}
_at = 0
for _name, _n in [("ident", 128), ("same", BC), ("bm2", SLOTS), ("bmzy", SLOTS), ("e4", SLOTS), ("bmt", GB),
                  ("r1", 1), ("iota14", KSEL), ("iota", T), ("tpos", 2), ("e13", 1), ("mh", 1),
                  ("mm", 1), ("ml", 1), ("bsel", GB), ("ones", T), ("f0", T)]:
    COLS[_name] = (_at, _at + _n)
    _at += _n
NCOLS = _at


def constants():
    k = np.zeros((128, NCOLS), np.float32)

    def col(name):
        a, b = COLS[name]
        return k[:, a:b]

    col("ident")[:] = np.eye(128)
    for b in range(GB):
        z, p = slice(b * C, b * C + C), slice(PR + b * C, PR + b * C + C)
        s = slice(b * KSEL, b * KSEL + KSEL)
        col("same")[z, z] = 1
        col("bm2")[z, s] = 1
        col("bmzy")[z, s] = 1
        col("bmzy")[p, s] = 1
        col("e4")[b, s] = 1
        col("bmt")[s, b] = 1
        col("r1")[s, 0] = np.arange(1, KSEL + 1)
        col("bsel")[z, b] = 1
    col("bm2")[Z1] = 1
    col("bmzy")[Z1] = 1
    col("iota14")[:] = np.arange(1, KSEL + 1)
    col("iota")[:] = np.arange(T)
    col("tpos")[:, 0] = np.arange(128)
    col("tpos")[:, 1] = HALF + np.arange(128)
    for n in range(PAIRS):
        col("e13")[n * W1 + C] = 1
        col(["mh", "mm", "ml"][WPART_OF[n]])[n * W1:n * W1 + W1] = 1
    col("ones")[:] = 1
    col("f0")[Z1] = 1
    return k


class Steps:

    def __init__(self, sem, names):
        self.sem, self.names = sem, names.split()

    def at(self, group, name):
        return group * len(self.names) + (self.names.index(name) + 1)


def program(nc, x, cw, wqkv, bqkv, selw, selb, ow, ob, temp, w1t, b1, w2, consts, e48, e13r, out):
    f32, bf16, i32 = mybir.dt.float32, mybir.dt.bfloat16, mybir.dt.int32
    ALU, ACT, AX = mybir.AluOpType, mybir.ActivationFunctionType, mybir.AxisListType

    xg = x.rearrange("(g b) c h w -> g (b c h w)", b=GB).rearrange("g (p q) -> g p q", p=128)
    og = out.rearrange("(g b) (t i) e -> g (b t) (i e)", b=GB, i=FT)
    scratch = nc.dram_tensor("patch_sums", (NG, 128, NQ * N), f32, kind="Internal").ap()
    sums_in = scratch.rearrange("g p q -> g (p q)").rearrange("g (r q) -> g r q", r=BC)

    with ExitStack() as ctx:
        def sb(name, shape, dt=f32):
            return ctx.enter_context(nc.sbuf_tensor(name, shape, dt))

        def ps(name):
            return ctx.enter_context(nc.psum_tensor(name, [128, 512], f32))

        def sem(name):
            return ctx.enter_context(nc.semaphore(name))

        K = sb("K", [128, NCOLS])

        def kc(name, rows=128):
            a, b = COLS[name]
            return K[0:rows, a:b]

        WR, BW, WcR = sb("WR", [FR, D]), sb("BW", [FR, D]), sb("WcR", [FR, D])
        WS, WcS = sb("WS", [SK, D]), sb("WcS", [SK, D])
        mean_r, mean_s = sb("mean_r", [FR, 1]), sb("mean_s", [SK, 1])
        WT4, WST = sb("WT4", [DH + 1, 2, FR]), sb("WST", [DH + 1, 2, SK])
        Wsel = sb("Wsel", [DH + 1, 2, 2])
        W1T = sb("W1T", [DH + 1, 2, HID])
        W2 = sb("W2", [128, HT, D])
        OB = sb("OB", [ZR, D])
        temp_sb = sb("temp_sb", [ZR, 1])
        A4 = sb("A4", [ZR, HEADS, ZR])
        B2 = sb("B2", [128, HP, D])
        TMR = sb("TMR", [PF, TMC])
        selM2 = sb("selM2", [ZR, 2])
        sel_raw, sel_d = sb("sel_raw", [ZR, 2]), sb("sel_d", [ZR, 1])
        M1S, RS = sb("M1S", [SK, HID], bf16), sb("RS", [SK, D], bf16)
        identb = sb("identb", [128, 128], bf16)

        X = sb("X", [128, NX, TQ * QB])
        R = sb("R", [128, 2, NQ * N])
        Praw = sb("Praw", [BC, 2, NQ * 128 * N // BC])
        Pt = sb("Pt", [BC, 2, T])
        P = [sb(f"P{i}", [PF, T]) for i in range(2)]
        FM = [sb(f"FM{i}", [ZR, T]) for i in range(2)]
        prod = sb("prod", [HALF, 2, BC])
        sc = {n: sb(n, [HALF, 2 * GB]) for n in ("var", "lr", "L", "t1", "t2", "s2", "al", "den", "rden", "kw", "ky")}
        rx, ry, rh, ra, rb = (sb(n, [HALF, NR]) for n in ("rx", "ry", "rh", "ra", "rb"))
        NORM1, NORM2, NORMC = slice(0, 2 * GB), slice(2 * GB, 4 * GB), slice(4 * GB, NR)
        TS = sb("TS", [HALF, 2, 1 + GB])
        Dm, Ex2 = sb("Dm", [HALF, 2, 2 * GB]), sb("Ex2", [HALF, 2, 2 * GB])
        sl1, sl2 = sb("sl1", [GB, T + 4]), sb("sl2", [GB, T + 4])
        m8a, m8b = sb("m8a", [GB, 8]), sb("m8b", [GB, 8])
        mask, cum, srow = sb("mask", [GB, T]), sb("cum", [GB, T]), sb("srow", [GB, T])
        Sg = sb("Sg", [HALF, 2, 2, SLOTS])
        keep = sb("keep", [HALF, 2 * GB])
        ST = [sb(f"ST{i}", [SLOTS, GB, T]) for i in range(4)]
        F = [sb(f"F{i}", [HALF, 2, FC]) for i in range(2)]
        v26, d1, d2 = (sb(n, [HALF, 4 * GB, W1]) for n in ("v26", "d1", "d2"))
        SP = sb("SP", [HALF, 4 * GB, PAIRS, W1], bf16)
        Stk1 = [sb(f"Stk1_{i}", [SK, GT], bf16) for i in range(2)]
        Stk2 = [sb(f"Stk2_{i}", [SK, GT], bf16) for i in range(4)]
        act_sb = [sb(f"act{i}", [128, HT, GT]) for i in range(2)]
        spare = [t[:, :, :].rearrange("p h t -> p (h t)") for t in act_sb]
        Wqkv = spare[0][0:DH + 1, 0:6 * D].rearrange("p (k n) -> p k n", k=2)
        Wo = spare[0][0:HD, 6 * D:(6 + HEADS) * D].rearrange("p (h e) -> p h e", h=HEADS)
        MqT, MkT, MvT = (spare[1][0:HD, n * HEADS * ZR:(n + 1) * HEADS * ZR].rearrange("p (h c) -> p h c", h=HEADS) for n in range(3))
        M1f, M1r = (spare[1][0:SK, n * HID:(n + 1) * HID] for n in (3, 4))
        M1h = spare[1][0:SK, 5 * HID:5 * HID + HID // 2].bitcast(bf16)
        ZY = sb("ZY", [FR, SLOTS])
        RM = sb("RM", [ROWS, T])
        UB = sb("UB", [ZR, HP, 2, SLOTS])
        Sm = sb("Sm", [ROWS, HP, T])
        mx, nm, rsum, rinv = (sb(n, [ROWS, HP]) for n in ("mx", "nm", "rsum", "rinv"))
        ET = sb("ET", [HALF, 2 * HP, ROWS])
        GN = sb("GN", [ROWS, HP, ZR])
        G2 = sb("G2", [128, HP, SLOTS])
        dsm, dsel = sb("dsm", [SLOTS, GB]), sb("dsel", [SLOTS, 1])
        res, h1, xh = (sb(n, [SLOTS, D]) for n in ("res", "h1", "xh"))
        bst, mv = sb("bst", [SLOTS, 6]), sb("mv", [SLOTS, 2])
        XH = sb("XH", [DH + 1, 2, SLOTS])
        actS = sb("actS", [128, HT, SLOTS])
        OS = [sb(f"OS{i}", [SLOTS, D]) for i in range(2)]
        obuf = [sb(f"obuf{i}", [OT, FT, D]) for i in range(2)]

        psF, psA, psC = ps("psF"), ps("psA"), ps("psC")
        psO = [ps("psO0"), ps("psO1")]
        psS = ctx.enter_context(nc.psum_tensor("psS", [128, 3, 512], f32))

        w_in, w_zero = sem("weights_loaded"), sem("weights_zeroed")
        x_in = [sem(f"x_loaded{k}") for k in range(NX)]
        sums_out = [sem(f"sums_stored{k}") for k in range(2)]
        sums_back = [sem(f"sums_loaded{k}") for k in range(2)]
        y_out = [sem(f"out_stored{k}") for k in range(2)]
        passed = sem("waits_passed")
        tiles = [f"x{k}" for k in range(XT)]
        pool_L = Steps(sem("pool_halved_x"), " ".join(tiles))
        dve_L = Steps(sem("dve_summed_x"), " ".join(tiles))
        pool_P = Steps(sem("pool_token_sums"), "q01 q23 p")
        pe_A = Steps(sem("pe_tokens"), "tm zt sl st")
        dve_A = Steps(sem("dve_tokens"), "cp pr var ve z lr L D1 D0 den rden sel m8a mr1 m8b fx mr2 mk cs sr S S2 kp ST t1 t2 s2 s3")
        act_A = Steps(sem("act_tokens"), "e fm")
        dve_R = Steps(sem("dve_rsqrt"), "h g " + " ".join(f"{n}{k}" for k in range(3) for n in "aby"))
        dve_K = Steps(sem("dve_stacks"), "al ky kw y w one mean d1 d2")
        act_K = Steps(sem("act_stacks"), "H M L k1 k2")
        pe_K = Steps(sem("pe_stacks"), "tr1 tr2")
        pe_G = Steps(sem("pe_queries"), "ga u rs")
        act_G = Steps(sem("act_queries"), "rs")
        dve_G = Steps(sem("dve_queries"), "zy rm dm ds ub0 ub1")
        pe_S = Steps(sem("pe_attention"), "sc et g gt at")
        dve_S = Steps(sem("dve_attention"), "sm mx nm ri gn g0 g1 h1 bs ba vr")
        act_S = Steps(sem("act_attention"), "e0 e1 e2 e3 e4 e5 t0 t1 t2")
        pe_C = Steps(sem("pe_chosen_ffn"), "xt f1 f2")
        dve_C = Steps(sem("dve_chosen_ffn"), "xh os")
        act_C = Steps(sem("act_chosen_ffn"), "XH ge")
        ffn = [f"n{k}" for k in range(2 * HT)]
        outs = [f"o{k}" for k in range(FT)]
        pe_F1 = Steps(sem("pe_ffn1"), " ".join(ffn))
        act_F1 = Steps(sem("act_gelu"), " ".join(ffn))
        pe_F2 = Steps(sem("pe_ffn2"), " ".join(outs))
        act_F2 = Steps(sem("act_out"), " ".join(outs))
        pe_W = Steps(sem("pe_weights"), "wt ws c sel q k v a4 b2 m1")
        splits = "h r1 ah m r2 am l al"
        dve_W = Steps(sem("dve_weights"), "wr0 ws0 wt0 ini idb mr mr2 wcr bw0 bw1 ms ms2 wcs rf wt ws cf cf2 raw sd sd2 s1 s0 tp tz tmm tmd tmb q k v a4 b2 ob m1 "
                      + " ".join(f"{n}{t}" for t in "MR" for n in splits.split()))
        block = ctx.enter_context(nc.Block())

        def periods(engine, body, first):
            for p in range(first):
                body(p, p % 4, p // 4)
            with engine.Fori(0, 3) as i:
                for k in range(first, first + 4):
                    body(i * 4 + k, k % 4, i + k // 4)
            for p in range(first + 12, NG + LAST):
                body(p, p % 4, p // 4)

        def by_itself(engine):
            engine.sem_inc(passed, 1)

        def active(p, lag):
            return not isinstance(p, int) or 0 <= p - lag < NG

        def exists(group):
            return not isinstance(group, int) or group >= 0

        def follows(group):
            return not isinstance(group, int) or group < NG

        def landed(group, par):
            return (group - par) * 8 + 16

        def tile_of(ap, i):
            return ap.rearrange("p (m i) -> p i m", i=FT)[:, i, :]

        @block.sync
        def _(sp):
            def load_x(p, u, k):
                sp.dma_start(X[:, (XT * u + k) % NX, :], xg[bass.ds(p, 1), :, k * TQ * QB:(k + 1) * TQ * QB]
                             .rearrange("o p q -> (o p) q")).then_inc(x_in[(XT * u + k) % NX], 16)

            load_x(0, 0, 0)
            load_x(0, 0, 1)
            sp.dma_start(K[:, :], consts).then_inc(w_in, 16)
            sp.wait_ge(dve_W.sem, dve_W.at(0, "wt0"))
            n = 1
            for b in range(GB):
                sp.dma_start(WR[b * C:b * C + C, :], cw).then_inc(w_in, 16)
                sp.dma_start(WR[PR + b * C:PR + b * C + C, :], cw).then_inc(w_in, 16)
                n += 2
            for k in range(PAIRS):
                sp.dma_start(WS[k * W1:k * W1 + C, :], cw).then_inc(w_in, 16)
                n += 1
            load_x(0, 0, 2)
            for dst, src in [
                    (Wqkv[0:DH, :, :], wqkv.rearrange("(k d) n -> d k n", k=2)), (Wqkv[DH:DH + 1, 0, :], bqkv),
                    (Wsel[0:DH, :, :], selw.rearrange("(k d) n -> d k n", k=2)), (Wsel[DH:DH + 1, 0, :], selb),
                    (Wo[:, :, :], ow.rearrange("(h d) e -> d h e", h=HEADS)),
                    (W1T[0:DH, :, :], w1t.rearrange("(k d) n -> d k n", k=2)), (W1T[DH:DH + 1, 0, :], b1),
                    (W2[:, :, :], w2.rearrange("(h p) e -> p h e", h=HT)),
                    (OB[:, :], ob.to_broadcast([ZR, D])),
                    (temp_sb[:, :], temp.to_broadcast([ZR, 1])),
                    (WT4[DH:DH + 1, 0, :], e48), (WST[DH:DH + 1, 0, :], e13r)]:
                sp.dma_start(dst, src).then_inc(w_in, 16)
                n += 1
            assert n == NW_IN, n

            load_x(0, 0, 3)

            def body(p, u, q):
                for k in range(XT):
                    if k == 3 and active(p, 1):
                        sp.wait_ge(dve_L.sem, dve_L.at(p - 1, f"x{XT - 1}"))
                        sp.dma_start(scratch[bass.ds(p - 1, 1)].rearrange("o p q -> (o p) q"),
                                     R[:, (u - 1) % 2, :]).then_inc(sums_out[(u - 1) % 2], 16)
                    if k == 4 and active(p, 1):
                        g, r = p - 1, (u - 1) % 2
                        sp.wait_ge(sums_out[r], landed(g, r))
                        if exists(g - 2):
                            sp.wait_ge(pool_P.sem, pool_P.at(g - 2, "q23"))
                        sp.dma_start(Praw[:, r, :], sums_in[bass.ds(g, 1)].rearrange("o p q -> (o p) q")
                                     ).then_inc(sums_back[r], 16)
                    if active(p, 0) and (k >= NX or not isinstance(p, int) or p):
                        sp.wait_ge(dve_L.sem, dve_L.at(p if k >= NX else p - 1, f"x{(k - NX) % XT}"))
                        load_x(p, u, k)

            periods(nc.sync, body, 4)
            for r in range(2):
                sp.wait_ge(sums_out[r], landed(NG - 2 + r, r))
                sp.wait_ge(y_out[r], landed(NG - 2 + r, r))

        @block.gpsimd
        def _(pool):
            def body(p, u, q):
                for k in range(XT):
                    if active(p, 0):
                        b = (XT * u + k) % NX
                        pool.wait_ge(x_in[b], (q * XT + ((XT * u + k) // NX + 1)) * 16)
                        v = X[:, b, :].rearrange("p (q r w) -> p q r w", q=TQ, r=QR)
                        if k == 5 and active(p, 1):
                            pool.wait_ge(pool_P.sem, pool_P.at(p - 1, "p"))
                        pool.tensor_tensor(v[:, :, 0:2, :], v[:, :, 0:2, :], v[:, :, 2:4, :], ALU.add).then_inc(pool_L.sem, 1)
                    if k == 4 and active(p, 0):
                        pool.wait_ge(pool_L.sem, pool_L.at(p, f"x{k}"))
                    if k == 4 and active(p, 1):
                        sum_quarters(p - 1, (u - 1) % 2)

            def sum_quarters(g, r):
                pool.wait_ge(sums_back[r], landed(g, r))
                raw = Praw[:, r, :].rearrange("p (i q j) -> p q i j", i=N, q=4)
                t = Pt[:, :, :].rearrange("p k (i j) -> p k i j", i=N)
                pool.tensor_tensor(t[:, 0], raw[:, 0], raw[:, 1], ALU.add).then_inc(pool_P.sem, 1)
                pool.tensor_tensor(t[:, 1], raw[:, 2], raw[:, 3], ALU.add).then_inc(pool_P.sem, 1)
                pool.wait_ge(pool_P.sem, pool_P.at(g, "q23"))
                if exists(g - 2):
                    pool.wait_ge(pe_A.sem, pe_A.at(g - 2, "tm"))
                pool.wait_ge(dve_W.sem, dve_W.at(0, "ini"))
                pool.tensor_tensor(P[r][0:BC, :], Pt[:, 0, :], Pt[:, 1, :], ALU.add).then_inc(pool_P.sem, 1)

            periods(nc.gpsimd, body, 4)

        @block.tensor
        def _(pe):
            def weights():
                pe.wait_ge(dve_W.sem, dve_W.at(0, "wcs"))
                for k in range(2):
                    mm = pe.transpose(psA[0:DH, k * FR:k * FR + FR], WcR[:, k * DH:k * DH + DH], kc("ident")[0:FR, 0:FR])
                mm.then_inc(pe_W.sem, 1)
                for k in range(2):
                    mm = pe.transpose(psC[0:DH, k * SK:k * SK + SK], WcS[:, k * DH:k * DH + DH], kc("ident")[0:SK, 0:SK])
                mm.then_inc(pe_W.sem, 1)
                pe.wait_ge(dve_W.sem, dve_W.at(0, "ws"))
                for k in range(2):
                    mm = pe.matmul(psO[0][0:BC, 0:BC], WT4[0:DH, k, 0:BC], WT4[0:DH, k, 0:BC], start=(k == 0), stop=(k == 1))
                mm.then_inc(pe_W.sem, 1)

                def bias_first(k):
                    return slice(0, DH + 1) if k == 0 else slice(0, DH)

                for k in range(2):
                    mm = pe.matmul(psF[0:ZR, 0:2], WT4[bias_first(k), k, 0:ZR], Wsel[bias_first(k), k, :],
                                   start=(k == 0), stop=(k == 1))
                mm.then_inc(pe_W.sem, 1)
                pe.wait_ge(dve_W.sem, dve_W.at(0, "raw"))
                banks = [(psS[:, 0], psS[:, 1]), (psS[:, 2], psA[:, :]), (psC[:, :], psO[1][:, :])]
                for m in range(3):
                    for h in range(HEADS):
                        to = banks[m][h // HP][0:HD, (h % HP) * ZR:(h % HP) * ZR + ZR]
                        for k in range(2):
                            mm = pe.matmul(to, Wqkv[bias_first(k), k, m * D + h * HD:m * D + h * HD + HD],
                                           WT4[bias_first(k), k, 0:ZR], start=(k == 0), stop=(k == 1))
                    mm.then_inc(pe_W.sem, 1)
                pe.wait_ge(dve_W.sem, dve_W.at(0, "v"))
                for h in range(HEADS):
                    mm = pe.matmul((psA if h < HP else psC)[0:ZR, (h % HP) * ZR:(h % HP) * ZR + ZR],
                                   MqT[:, h, :], MkT[:, h, :], start=True, stop=True)
                mm.then_inc(pe_W.sem, 1)
                for h in range(HEADS):
                    j = h % HP
                    r = ZR * (h // HP)
                    mm = pe.matmul(psS[r:r + ZR, j // 2, (j % 2) * D:(j % 2) * D + D], MvT[:, h, :], Wo[:, h, :],
                                   start=True, stop=True)
                mm.then_inc(pe_W.sem, 1)
                pe.wait_ge(dve_W.sem, dve_W.at(0, "b2"))
                for n in range(2):
                    for k in range(2):
                        mm = pe.matmul((psA, psC)[n][0:SK, 0:HID // 2], WST[bias_first(k), k, :],
                                       W1T[bias_first(k), k, n * HID // 2:(n + 1) * HID // 2], start=(k == 0), stop=(k == 1))
                mm.then_inc(pe_W.sem, 1)

            def step_A(g, u, name):
                r = u % 2
                if name == "tm":
                    pe.wait_ge(pool_P.sem, pool_P.at(g, "p"))
                    if exists(g - 2):
                        pe.wait_ge(act_K.sem, act_K.at(g - 2, "k2"))
                    for k in range(2):
                        mm = pe.matmul(psA[0:HALF, k * TMC:(k + 1) * TMC], P[r][:, k * HALF:(k + 1) * HALF], TMR[:, :],
                                       start=True, stop=True)
                elif name == "zt":
                    pe.wait_ge(dve_A.sem, dve_A.at(g, "z"))
                    by_itself(pe)
                    for k in range(2):
                        mm = pe.transpose(psA[0:ZR, k * HALF:(k + 1) * HALF], F[r][:, k, 0:ZR], kc("ident")[0:HALF, 0:HALF])
                elif name == "sl":
                    pe.wait_ge(dve_A.sem, dve_A.at(g, "sel"))
                    pe.wait_ge(act_A.sem, act_A.at(g, "fm"))
                    for k in range(2):
                        mm = pe.transpose(psA[0:GB, k * HALF:(k + 1) * HALF], TS[:, k, 1:1 + GB], kc("ident")[0:HALF, 0:HALF])
                else:
                    pe.wait_ge(dve_A.sem, dve_A.at(g, "sr"))
                    for k in range(2):
                        pe.matmul(psA[0:HALF, 400 + k * GB:400 + (k + 1) * GB], srow[:, k * HALF:(k + 1) * HALF],
                                  kc("ident")[0:GB, 0:GB], start=True, stop=True)
                    mm = pe.matmul(psA[0:SLOTS, 0:T], kc("e4", GB), srow[:, :], start=True, stop=True)
                mm.then_inc(pe_A.sem, 1)

            def step_K(g, u, name):
                k = int(name[2]) - 1
                pe.wait_ge(act_K.sem, act_K.at(g, "k1" if k else "L"))
                if not k and follows(g + 1):
                    pe.wait_ge(dve_A.sem, dve_A.at(g + 1, "ST"))
                to = psA[:, :].bitcast(bf16)
                for n in range(2 * GB):
                    c0 = (n % GB) * T + (n // GB) * HALF
                    mm = pe.transpose(to[0:SK, c0:c0 + HALF], SP[:, 2 * n + k, :, :].rearrange("p n c -> p (n c)"),
                                      identb[0:HALF, 0:HALF])
                mm.then_inc(pe_K.sem, 1)

            def step_G(g, u, name):
                r = u % 2
                if name == "ga":
                    pe.wait_ge(dve_A.sem, dve_A.at(g, "S2"))
                    if exists(g - 1):
                        pe.wait_ge(dve_S.sem, dve_S.at(g - 1, "h1"))
                    for k in range(2):
                        pe.matmul(psS[0:FR, 0, 0:SLOTS], F[r][:, k, 0:FR], Sg[:, k, 0, :], start=(k == 0), stop=(k == 1))
                    for k in range(2):
                        mm = pe.matmul(psS[0:ROWS, 0, ZR:ZR + 1 + GB], Sg[:, k, :, :].rearrange("p d s -> p (d s)"),
                                       TS[:, k, :], start=(k == 0), stop=(k == 1))
                else:
                    pe.wait_ge(dve_G.sem, dve_G.at(g, "zy"))
                    by_itself(pe)
                    for h in range(HEADS):
                        mm = pe.matmul(psS[0:ZR, 1 + h // HP, (h % HP) * SLOTS:(h % HP + 1) * SLOTS], A4[:, h, :],
                                       ZY[0:ZR, :], start=True, stop=True)
                    mm.then_inc(pe_G.sem, 1)
                    pe.wait_ge(dve_G.sem, dve_G.at(g, "dm"))
                    mm = pe.matmul(psS[0:SLOTS, 0, D:2 * D], ZY[:, :], BW[:, :], start=True, stop=True)
                mm.then_inc(pe_G.sem, 1)

            def step_S(g, u, name):
                r = u % 2
                if name == "sc":
                    pe.wait_ge(act_A.sem, act_A.at(g, "fm"))
                    pe.wait_ge(dve_G.sem, dve_G.at(g, "ub1"))
                    pe.wait_ge(act_G.sem, act_G.at(g, "rs"))
                    for j in range(HP):
                        mm = pe.matmul(psS[0:ROWS, j // 2, (j % 2) * T:(j % 2 + 1) * T],
                                       UB[:, j, :, :].rearrange("p k s -> p (k s)"), FM[r][:, :], start=True, stop=True)
                elif name == "et":
                    pe.wait_ge(act_S.sem, act_S.at(g, "e5"))
                    for n in range(2 * HP):
                        k, j = n // HP, n % HP
                        mm = pe.transpose(psS[0:HALF, n // 4, (n % 4) * ROWS:(n % 4 + 1) * ROWS],
                                          Sm[:, j, k * HALF:(k + 1) * HALF], kc("ident")[0:ROWS, 0:ROWS])
                elif name == "g":
                    pe.wait_ge(act_S.sem, act_S.at(g, "t2"))
                    for j in range(HP):
                        for k in range(2):
                            mm = pe.matmul(psS[0:ROWS, 0, j * ZR:(j + 1) * ZR], ET[:, k * HP + j, :], F[r][:, k, 0:ZR],
                                           start=(k == 0), stop=(k == 1))
                elif name == "gt":
                    pe.wait_ge(dve_S.sem, dve_S.at(g, "gn"))
                    by_itself(pe)
                    for j in range(HP):
                        mm = pe.transpose(psS[0:ZR, 1 + j // 3, (j % 3) * ROWS:(j % 3 + 1) * ROWS],
                                          GN[:, j, :], kc("ident")[0:ROWS, 0:ROWS])
                else:
                    pe.wait_ge(dve_S.sem, dve_S.at(g, "g1"))
                    for j in range(HP):
                        mm = pe.matmul(psS[0:SLOTS, 0, 0:D], G2[:, j, :], B2[:, j, :], start=(j == 0), stop=(j == HP - 1))
                mm.then_inc(pe_S.sem, 1)

            def step_C(g, u, name):
                if name == "xt":
                    pe.wait_ge(dve_C.sem, dve_C.at(g, "xh"))
                    by_itself(pe)
                    for k in range(2):
                        mm = pe.transpose(psC[0:DH, k * SLOTS:(k + 1) * SLOTS], xh[:, k * DH:(k + 1) * DH],
                                          kc("ident")[0:SLOTS, 0:SLOTS])
                elif name == "f1":
                    pe.wait_ge(act_C.sem, act_C.at(g, "XH"))
                    for h in range(HT):
                        for k in range(2):
                            rows = slice(0, DH + 1) if k == 0 else slice(0, DH)
                            mm = pe.matmul(psC[:, h * SLOTS:(h + 1) * SLOTS], W1T[rows, k, h * 128:(h + 1) * 128],
                                           XH[rows, k, :], start=(k == 0), stop=(k == 1))
                else:
                    pe.wait_ge(act_C.sem, act_C.at(g, "ge"))
                    for h in range(HT):
                        mm = pe.matmul(psC[0:SLOTS, 0:D], actS[:, h, :], W2[:, h, :], start=(h == 0), stop=(h == HT - 1))
                mm.then_inc(pe_C.sem, 1)

            def step_F1(g, u, n):
                if n == 0:
                    pe.wait_ge(act_K.sem, act_K.at(g, "k1"))
                if exists(g if n else g - 1):
                    pe.wait_ge(act_F1.sem, act_F1.at(g if n else g - 1, f"n{(n - 1) % (2 * HT)}"))
                pe.matmul(psF[:, 0:GT // 2], M1S[:, (n // 2) * 128:(n // 2 + 1) * 128],
                          Stk1[u % 2][:, (n % 2) * (GT // 2):(n % 2 + 1) * (GT // 2)], start=True, stop=True).then_inc(pe_F1.sem, 1)

            def step_F2(g, u, n):
                i, m = n // 8, n % 8
                to = psO[(i + u) % 2][0:OT, 0:D]
                if m == 0:
                    if i == 0:
                        pe.wait_ge(act_F1.sem, act_F1.at(g, f"n{2 * HT - 1}"))
                    if exists(g if i >= 2 else g - 1):
                        pe.wait_ge(act_F2.sem, act_F2.at(g if i >= 2 else g - 1, f"o{(i - 2) % FT}"))
                if m < HT:
                    pe.matmul(to, tile_of(act_sb[u % 2][:, m, :], i), W2[:, m, :], start=(m == 0), stop=False)
                elif m == HT:
                    if i == 0:
                        pe.wait_ge(act_K.sem, act_K.at(g, "k2"))
                    pe.matmul(to, tile_of(Stk2[u][:, :], i), RS[:, :], start=False, stop=False)
                else:
                    if i == 0:
                        pe.wait_ge(dve_C.sem, dve_C.at(g, "os"))
                    pe.matmul(to, tile_of(ST[u][:, :, :].rearrange("p b t -> p (b t)"), i), OS[u % 2][:, :],
                              start=False, stop=True).then_inc(pe_F2.sem, 1)

            plan = {0: ["S gt 3"], 2: ["S at 3"], 3: ["K tr1 3"], 4: ["G ga 2"], 5: ["G u 2"], 6: ["K tr2 3"], 11: ["A tm 1"],
                    13: ["S sc 2"], 16: ["A zt 1", "C xt 3"], 18: ["A sl 1"], 20: ["S et 2", "C f1 3"], 22: ["S g 2", "A st 1"],
                    23: ["C f2 3"]}
            stages = {"A": step_A, "G": step_G, "K": step_K, "S": step_S, "C": step_C}

            def body(p, u, q):
                done = 0
                for s in range(PLAN):
                    for what in plan.get(s, []):
                        stage, step, lag = what.split()
                        if active(p, int(lag)):
                            stages[stage](p - int(lag), (u - int(lag)) % 4, step)
                    if s in AT_F1 and active(p, 3):
                        step_F1(p - 3, (u - 3) % 4, AT_F1.index(s))
                    for n in range(done, done + IN_F2[s]):
                        if active(p, 4):
                            step_F2(p - 4, (u - 4) % 4, n)
                    done += IN_F2[s]

            pe.wait_ge(w_in, NW_IN * 16)
            weights()
            pe.wait_ge(dve_W.sem, dve_W.at(0, "m1"))
            periods(nc.tensor, body, 5)

        @block.scalar
        def _(act):
            def step_A(g, u, name):
                if name == "e":
                    act.wait_ge(dve_A.sem, dve_A.at(g, "D0"))
                    act.activation(Ex2[:, :, :], Dm[:, :, :], ACT.Exp).then_inc(act_A.sem, 1)
                else:
                    act.wait_ge(pe_A.sem, pe_A.at(g, "zt"))
                    if exists(g - 2):
                        act.wait_ge(pe_S.sem, pe_S.at(g - 2, "sc"))
                    act.activation(FM[u % 2][:, :], psA[0:ZR, 0:T], ACT.Copy).then_inc(act_A.sem, 1)

            def step_K(g, u, name):
                if name in "HML":
                    act.wait_ge(dve_K.sem, dve_K.at(g, {"H": "mean", "M": "d1", "L": "d2"}[name]))
                    if name == "H" and exists(g - 1):
                        act.wait_ge(pe_K.sem, pe_K.at(g - 1, "tr2"))
                    src, n0, n1 = {"H": (v26, 0, 3), "M": (d1, 3, 6), "L": (d2, 6, 8)}[name]
                    act.activation(SP[:, :, n0:n1, :], src[:, :, :].unsqueeze(2).broadcast_to([HALF, 4 * GB, n1 - n0, W1]),
                                   ACT.Copy).then_inc(act_K.sem, 1)
                elif name == "k1":
                    act.wait_ge(pe_K.sem, pe_K.at(g, "tr1"))
                    if exists(g - 2):
                        act.wait_ge(pe_F1.sem, pe_F1.at(g - 2, f"n{2 * HT - 1}"))
                    act.activation(Stk1[u % 2][:, :], psA[:, :].bitcast(bf16)[0:SK, 0:GT], ACT.Copy).then_inc(act_K.sem, 1)
                else:
                    act.wait_ge(pe_K.sem, pe_K.at(g, "tr2"))
                    act.activation(Stk2[u][:, :], psA[:, :].bitcast(bf16)[0:SK, 0:GT], ACT.Copy).then_inc(act_K.sem, 1)

            def step_G(g, u, name):
                act.wait_ge(pe_G.sem, pe_G.at(g, "rs"))
                act.activation(res[:, :], psS[0:SLOTS, 0, D:2 * D], ACT.Copy).then_inc(act_G.sem, 1)

            def step_S(g, u, name):
                if name == "exp":
                    act.wait_ge(dve_S.sem, dve_S.at(g, "nm"))
                    for j in range(HP):
                        act.activation(Sm[:, j, :], Sm[:, j, :], ACT.Exp, bias=nm[:, j:j + 1],
                                       accum_out=rsum[:, j:j + 1]).then_inc(act_S.sem, 1)
                else:
                    act.wait_ge(pe_S.sem, pe_S.at(g, "et"))
                    if exists(g - 1):
                        act.wait_ge(pe_S.sem, pe_S.at(g - 1, "g"))
                    for n in range(3):
                        act.activation(ET[:, 4 * n:4 * n + 4, :], psS[0:HALF, n, 0:4 * ROWS]
                                       .rearrange("p (k s) -> p k s", k=4), ACT.Copy).then_inc(act_S.sem, 1)

            def step_C(g, u, name):
                if name == "XH":
                    act.wait_ge(pe_C.sem, pe_C.at(g, "xt"))
                    act.activation(XH[0:DH, :, :], psC[0:DH, 0:2 * SLOTS].rearrange("p (k s) -> p k s", k=2),
                                   ACT.Copy).then_inc(act_C.sem, 1)
                else:
                    act.wait_ge(pe_C.sem, pe_C.at(g, "f1"))
                    act.activation(actS[:, :, :], psC[:, 0:HT * SLOTS].rearrange("p (h s) -> p h s", h=HT),
                                   ACT.Gelu).then_inc(act_C.sem, 1)

            def step_F1(g, u, n):
                act.wait_ge(pe_F1.sem, pe_F1.at(g, f"n{n}"))
                act.activation(act_sb[u % 2][:, n // 2, (n % 2) * (GT // 2):(n % 2 + 1) * (GT // 2)],
                               psF[:, 0:GT // 2], ACT.Gelu).then_inc(act_F1.sem, 1)

            def step_F2(g, u, i):
                act.wait_ge(pe_F2.sem, pe_F2.at(g, f"o{i}"))
                if i == 3:
                    if exists(g - 1):
                        act.wait_ge(y_out[(u - 1) % 2], landed(g - 1, (u - 1) % 2))
                act.activation(obuf[u % 2][:, i, :], psO[(i + u) % 2][0:OT, 0:D], ACT.Copy).then_inc(act_F2.sem, 1)
                if i == FT - 1:
                    act.wait_ge(act_F2.sem, act_F2.at(g, f"o{i}"))
                    act.dma_start(og[bass.ds(g, 1)].rearrange("o p q -> (o p) q"),
                                  obuf[u % 2][:, :, :].rearrange("p i e -> p (i e)")).then_inc(y_out[u % 2], 16)

            plan = {0: ["K L 3"], 3: ["K k1 3"], 5: ["G rs 2"], 6: ["K k2 3"], 15: ["A e 1"], 16: ["A fm 1", "C XH 3"], 17: ["S exp 2"],
                    19: ["K H 2"], 20: ["S t 2"], 21: ["C ge 3"], 22: ["K M 2"]}
            stages = {"A": step_A, "G": step_G, "K": step_K, "S": step_S, "C": step_C}

            def body(p, u, q):
                done = 0
                for s in range(PLAN):
                    for what in plan.get(s, []):
                        stage, step, lag = what.split()
                        if active(p, int(lag)):
                            stages[stage](p - int(lag), (u - int(lag)) % 4, step)
                    if s in AT_F1 and active(p, 3):
                        step_F1(p - 3, (u - 3) % 4, AT_F1.index(s))
                    for i in range(done // 8, (done + IN_F2[s]) // 8):
                        if active(p, 4):
                            step_F2(p - 4, (u - 4) % 4, i)
                    done += IN_F2[s]

            periods(nc.scalar, body, 5)

        @block.vector
        def _(dve):
            def weights_zeroed():
                dve.memset(WR[:, :], 0.0).then_inc(dve_W.sem, 1)
                dve.memset(WS[:, :], 0.0).then_inc(dve_W.sem, 1)
                dve.memset(XH[:, :, :], 1.0).then_inc(dve_W.sem, 1)

            def weights_first():
                dve.wait_ge(w_in, NW_IN * 16)
                for t in P:
                    dve.tensor_copy(t[:, :], kc("f0", PF))
                for t in F:
                    dve.memset(t[:, :, 0:Z1], 0.0)
                    dve.memset(t[:, :, Z1 + 1:PR], 0.0)
                    dve.memset(t[:, :, Z1:Z1 + 1], 1.0)
                dve.memset(rx[:, :], 1.0)
                dve.memset(sl1[:, :], -7.0)
                dve.tensor_copy(TS[:, :, 0], kc("tpos", HALF))
                dve.memset(m8b[:, :], -7.0).then_inc(dve_W.sem, 1)
                dve.tensor_copy(identb[:, :], kc("ident")).then_inc(dve_W.sem, 1)
                dve.tensor_reduce(mean_r[:, :], WR[:, :], AX.X, ALU.add).then_inc(dve_W.sem, 1)
                dve.wait_ge(dve_W.sem, dve_W.at(0, "mr"))
                dve.tensor_scalar(mean_r[:, :], mean_r[:, :], 1.0 / D, None, ALU.mult).then_inc(dve_W.sem, 1)
                dve.wait_ge(dve_W.sem, dve_W.at(0, "mr2"))
                dve.tensor_scalar(WcR[:, :], WR[:, :], mean_r[:, 0:1], None, ALU.subtract).then_inc(dve_W.sem, 1)
                dve.wait_ge(dve_W.sem, dve_W.at(0, "wcr"))
                dve.tensor_copy(BW[0:ZR, :], WcR[0:ZR, :]).then_inc(dve_W.sem, 1)
                dve.tensor_copy(BW[PR:FR, :], WR[PR:FR, :]).then_inc(dve_W.sem, 1)
                dve.tensor_reduce(mean_s[:, :], WS[:, :], AX.X, ALU.add).then_inc(dve_W.sem, 1)
                dve.wait_ge(dve_W.sem, dve_W.at(0, "ms"))
                dve.tensor_scalar(mean_s[:, :], mean_s[:, :], 1.0 / D, None, ALU.mult).then_inc(dve_W.sem, 1)
                dve.wait_ge(dve_W.sem, dve_W.at(0, "ms2"))
                dve.tensor_scalar(WcS[:, :], WS[:, :], mean_s[:, 0:1], None, ALU.subtract).then_inc(dve_W.sem, 1)
                dve.wait_ge(dve_W.sem, dve_W.at(0, "wcs"))
                dve.tensor_scalar(WS[:, :], WcS[:, :], kc("e13", SK), None, ALU.add).then_inc(dve_W.sem, 1)
                dve.wait_ge(pe_W.sem, pe_W.at(0, "ws"))
                dve.tensor_copy(WT4[0:DH, :, :], psA[0:DH, 0:2 * FR].rearrange("p (k c) -> p k c", k=2)).then_inc(dve_W.sem, 1)
                dve.tensor_copy(WST[0:DH, :, :], psC[0:DH, 0:2 * SK].rearrange("p (k c) -> p k c", k=2)).then_inc(dve_W.sem, 1)
                dve.wait_ge(pe_W.sem, pe_W.at(0, "c"))
                dve.memset(TMR[:, :], 0.0).then_inc(dve_W.sem, 1)
                dve.wait_ge(dve_W.sem, dve_W.at(0, "cf"))
                dve.scalar_tensor_tensor(out=TMR[0:BC, BC:2 * BC], in0=psO[0][0:BC, 0:BC], scalar=1.0 / D, in1=kc("same", BC),
                                         op0=ALU.mult, op1=ALU.mult).then_inc(dve_W.sem, 1)
                dve.wait_ge(pe_W.sem, pe_W.at(0, "sel"))
                dve.tensor_copy(sel_raw[:, :], psF[0:ZR, 0:2]).then_inc(dve_W.sem, 1)
                dve.wait_ge(dve_W.sem, dve_W.at(0, "raw"))
                dve.tensor_tensor(sel_d[:, :], sel_raw[:, 1:2], sel_raw[:, 0:1], ALU.subtract).then_inc(dve_W.sem, 1)
                dve.wait_ge(dve_W.sem, dve_W.at(0, "sd"))
                dve.reciprocal(temp_sb[:, :], temp_sb[:, :]).then_inc(dve_W.sem, 1)
                dve.wait_ge(dve_W.sem, dve_W.at(0, "sd2"))
                dve.tensor_tensor(selM2[:, 1:2], sel_d[:, :], temp_sb[:, :], ALU.mult).then_inc(dve_W.sem, 1)
                dve.wait_ge(dve_W.sem, dve_W.at(0, "s1"))
                dve.tensor_scalar(selM2[:, 0:1], selM2[:, 1:2], -1.0, None, ALU.mult).then_inc(dve_W.sem, 1)
                dve.wait_ge(dve_W.sem, dve_W.at(0, "s0"))
                dve.tensor_copy(TMR[0:BC, 0:BC], kc("ident")[0:BC, 0:BC]).then_inc(dve_W.sem, 1)
                aux = TMR[:, 2 * BC:TMC].rearrange("p (b c) -> p b c", c=AUX)
                dve.tensor_copy(aux[:, :, 2], kc("f0", PF)[:, 0:GB]).then_inc(dve_W.sem, 1)
                dve.tensor_scalar(aux[0:BC, :, 0], kc("bsel", BC), mean_r[0:BC, 0:1], None, ALU.mult).then_inc(dve_W.sem, 1)
                dve.tensor_scalar(aux[0:BC, :, 1], kc("bsel", BC), selM2[0:BC, 1:2], None, ALU.mult).then_inc(dve_W.sem, 1)
                dve.wait_ge(dve_W.sem, dve_W.at(0, "tz"))
                dve.tensor_scalar(aux[:, :, 2], aux[:, :, 2], selM2[0:PF, 1:2], None, ALU.mult).then_inc(dve_W.sem, 1)

            def weights_heads(m):
                banks = [(psS[:, 0], psS[:, 1]), (psS[:, 2], psA[:, :]), (psC[:, :], psO[1][:, :])]
                name, to = [("q", MqT), ("k", MkT), ("v", MvT)][m]
                dve.wait_ge(pe_W.sem, pe_W.at(0, name))
                for k in range(2):
                    ins = dve.tensor_copy(to[:, k * HP:(k + 1) * HP, :],
                                          banks[m][k][0:HD, 0:HP * ZR].rearrange("p (h c) -> p h c", h=HP))
                ins.then_inc(dve_W.sem, 1)

            def weights_attention(part):
                if part == "a4":
                    dve.wait_ge(pe_W.sem, pe_W.at(0, "a4"))
                    for k in range(2):
                        ins = dve.tensor_scalar(A4[:, k * HP:(k + 1) * HP, :], (psA, psC)[k][0:ZR, 0:HP * ZR]
                                                .rearrange("p (h c) -> p h c", h=HP), float(HD) ** -0.5, None, ALU.mult)
                    ins.then_inc(dve_W.sem, 1)
                else:
                    dve.wait_ge(pe_W.sem, pe_W.at(0, "b2"))
                    dve.tensor_copy(B2[:, :, :].rearrange("p (k j) e -> p k (j e)", k=3), psS[:, :, 0:2 * D]).then_inc(dve_W.sem, 1)
                    dve.wait_ge(dve_W.sem, dve_W.at(0, "b2"))
                    dve.scalar_tensor_tensor(out=B2[0:ZR, 0, :], in0=OB[:, :], scalar=kc("f0", ZR)[:, 0:1], in1=B2[0:ZR, 0, :],
                                             op0=ALU.mult, op1=ALU.add).then_inc(dve_W.sem, 1)

            def weights_ffn():
                dve.wait_ge(pe_W.sem, pe_W.at(0, "m1"))
                for k in range(2):
                    ins = dve.tensor_copy(M1f[:, k * HID // 2:(k + 1) * HID // 2], (psA, psC)[k][0:SK, 0:HID // 2])
                ins.then_inc(dve_W.sem, 1)

            def weights_parts(t):
                f, to, n = {"M": (M1f, M1S, HID), "R": (WS, RS, D)}[t]
                part, rest = M1h[:, 0:n], M1r[:, 0:n]
                dve.wait_ge(dve_W.sem, dve_W.at(0, "m1"))
                dve.tensor_copy(part, f[:, :]).then_inc(dve_W.sem, 1)
                dve.wait_ge(dve_W.sem, dve_W.at(0, "h" + t))
                dve.tensor_tensor(rest, f[:, :], part, ALU.subtract).then_inc(dve_W.sem, 1)
                dve.tensor_scalar(to[:, :], part, kc("mh", SK), None, ALU.mult).then_inc(dve_W.sem, 1)
                dve.wait_ge(dve_W.sem, dve_W.at(0, "ah" + t))
                dve.tensor_copy(part, rest).then_inc(dve_W.sem, 1)
                dve.wait_ge(dve_W.sem, dve_W.at(0, "m" + t))
                dve.tensor_tensor(rest, rest, part, ALU.subtract).then_inc(dve_W.sem, 1)
                dve.scalar_tensor_tensor(out=to[:, :], in0=part, scalar=kc("mm", SK), in1=to[:, :],
                                           op0=ALU.mult, op1=ALU.add).then_inc(dve_W.sem, 1)
                dve.wait_ge(dve_W.sem, dve_W.at(0, "am" + t))
                dve.tensor_copy(part, rest).then_inc(dve_W.sem, 1)
                dve.wait_ge(dve_W.sem, dve_W.at(0, "l" + t))
                dve.scalar_tensor_tensor(out=to[:, :], in0=part, scalar=kc("ml", SK), in1=to[:, :],
                                           op0=ALU.mult, op1=ALU.add).then_inc(dve_W.sem, 1)
                dve.wait_ge(dve_W.sem, dve_W.at(0, "al" + t))

            def sum_tile(g, u, k):
                dve.wait_ge(pool_L.sem, pool_L.at(g, f"x{k}"))
                if k == 0:
                    if exists(g - 2):
                        dve.wait_ge(sums_out[u % 2], landed(g - 2, u % 2))
                v = X[:, (XT * u + k) % NX, :].rearrange("p (q r j l) -> p q j r l", q=TQ, r=QR, j=N)
                dve.tensor_reduce(R[:, u % 2, k * TQ * N:(k + 1) * TQ * N].rearrange("p (q j) -> p q j", q=TQ),
                                  v[:, :, :, 0:2, :], AX.XY, ALU.add).then_inc(dve_L.sem, 1)

            def rsqrt(p):
                g = p - 1
                if active(p, 1):
                    dve.wait_ge(dve_A.sem, dve_A.at(g, "ve"))
                elif active(p, 2):
                    dve.wait_ge(dve_A.sem, dve_A.at(g - 1, "s3"))
                if active(p, 3):
                    dve.wait_ge(dve_S.sem, dve_S.at(g - 2, "vr"))
                dve.tensor_scalar(rh[:, :], rx[:, :], -0.5, None, ALU.mult).then_inc(dve_R.sem, 1)
                dve.tensor_scalar(ry[:, :].bitcast(i32), rx[:, :].bitcast(i32), -0.5, float(0x5F3759DF),
                                  ALU.mult, ALU.add).then_inc(dve_R.sem, 1)
                for k in range(3):
                    dve.wait_ge(dve_R.sem, dve_R.at(g, f"y{k - 1}" if k else "g"))
                    dve.tensor_tensor(ra[:, :], ry[:, :], ry[:, :], ALU.mult).then_inc(dve_R.sem, 1)
                    dve.wait_ge(dve_R.sem, dve_R.at(g, f"a{k}"))
                    dve.tensor_tensor(rb[:, :], ra[:, :], rh[:, :], ALU.mult).then_inc(dve_R.sem, 1)
                    dve.wait_ge(dve_R.sem, dve_R.at(g, f"b{k}"))
                    dve.scalar_tensor_tensor(out=ry[:, :], in0=rb[:, :], scalar=1.5, in1=ry[:, :],
                                             op0=ALU.add, op1=ALU.mult).then_inc(dve_R.sem, 1)
                dve.wait_ge(dve_R.sem, dve_R.at(g, "y2"))

            def kb(t):
                return t.rearrange("p (k b) -> p k b", k=2)

            def by_c(t):
                return kb(t).unsqueeze(3).broadcast_to([HALF, 2, GB, C])

            def features(u):
                f = F[u % 2]
                return (f[:, :, PR:FR].rearrange("p k (b c) -> p k b c", b=GB),
                        f[:, :, FR + BC:FC].rearrange("p k (b c) -> p k b c", b=GB))

            def stage_A(g, u, part):
                f = F[u % 2]
                p, aux = features(u)
                if part == "var":
                    dve.wait_ge(pe_A.sem, pe_A.at(g, "tm"))
                    if exists(g - 2):
                        dve.wait_ge(pe_S.sem, pe_S.at(g - 2, "g"))
                    dve.tensor_copy(f[:, :, PR:FC], psA[0:HALF, 0:2 * TMC].rearrange("p (k c) -> p k c", k=2)).then_inc(dve_A.sem, 1)
                    dve.wait_ge(dve_A.sem, dve_A.at(g, "cp"))
                    dve.tensor_tensor(prod[:, :, :], f[:, :, PR:FR], f[:, :, FR:FR + BC], ALU.mult).then_inc(dve_A.sem, 1)
                    dve.wait_ge(dve_A.sem, dve_A.at(g, "pr"))
                    dve.tensor_reduce(sc["var"][:, :], prod[:, :, :].rearrange("p k (b c) -> p (k b) c", c=C), AX.X, ALU.add).then_inc(dve_A.sem, 1)
                    dve.wait_ge(dve_A.sem, dve_A.at(g, "var"))
                    dve.tensor_scalar(rx[:, NORM1], sc["var"][:, :], EPS, None, ALU.add).then_inc(dve_A.sem, 1)
                elif part == "z":
                    dve.tensor_tensor(f[:, :, 0:BC].rearrange("p k (b c) -> p k b c", b=GB), p, by_c(ry[:, NORM1]), ALU.mult).then_inc(dve_A.sem, 1)
                    dve.tensor_tensor(kb(sc["lr"][:, :]), kb(ry[:, NORM1]), aux[:, :, :, 1], ALU.mult).then_inc(dve_A.sem, 1)
                    dve.wait_ge(dve_A.sem, dve_A.at(g, "lr"))
                    dve.tensor_tensor(kb(sc["L"][:, :]), kb(sc["lr"][:, :]), aux[:, :, :, 2], ALU.add).then_inc(dve_A.sem, 1)
                    dve.wait_ge(dve_A.sem, dve_A.at(g, "L"))
                    dve.tensor_scalar(Dm[:, 1, :], sc["L"][:, :], 0.0, None, ALU.min).then_inc(dve_A.sem, 1)
                    dve.tensor_scalar(Dm[:, 0, :], sc["L"][:, :], -1.0, 0.0, ALU.mult, ALU.min).then_inc(dve_A.sem, 1)
                elif part == "var2":
                    dve.tensor_scalar(sc["t1"][:, :], ry[:, NORM1], 1.0, None, ALU.add).then_inc(dve_A.sem, 1)
                    dve.wait_ge(dve_A.sem, dve_A.at(g, "t1"))
                    dve.tensor_tensor(sc["t2"][:, :], sc["t1"][:, :], sc["t1"][:, :], ALU.mult).then_inc(dve_A.sem, 1)
                    dve.wait_ge(dve_A.sem, dve_A.at(g, "t2"))
                    dve.tensor_tensor(sc["s2"][:, :], sc["t2"][:, :], sc["var"][:, :], ALU.mult).then_inc(dve_A.sem, 1)
                    dve.wait_ge(dve_A.sem, dve_A.at(g, "s2"))
                    dve.tensor_scalar(rx[:, NORM2], sc["s2"][:, :], EPS, None, ALU.add).then_inc(dve_A.sem, 1)
                elif part == "sel":
                    dve.wait_ge(act_A.sem, act_A.at(g, "e"))
                    dve.tensor_tensor(sc["den"][:, :], Ex2[:, 0, :], Ex2[:, 1, :], ALU.add).then_inc(dve_A.sem, 1)
                    dve.wait_ge(dve_A.sem, dve_A.at(g, "den"))
                    dve.reciprocal(sc["rden"][:, :], sc["den"][:, :]).then_inc(dve_A.sem, 1)
                    dve.wait_ge(dve_A.sem, dve_A.at(g, "rden"))
                    dve.tensor_tensor(TS[:, :, 1:1 + GB], kb(Ex2[:, 1, :]), kb(sc["rden"][:, :]), ALU.mult).then_inc(dve_A.sem, 1)
                elif part == "top":
                    dve.wait_ge(pe_A.sem, pe_A.at(g, "sl"))
                    by_itself(dve)
                    dve.max(m8a[:, :], psA[0:GB, 0:T]).then_inc(dve_A.sem, 1)
                    dve.wait_ge(dve_A.sem, dve_A.at(g, "m8a"))
                    by_itself(dve)
                    dve.match_replace(sl1[:, 0:T], m8a[:, :], psA[0:GB, 0:T], -1.0).then_inc(dve_A.sem, 1)
                    dve.wait_ge(dve_A.sem, dve_A.at(g, "mr1"))
                    by_itself(dve)
                    dve.max(m8b[:, :], sl1[:, :]).then_inc(dve_A.sem, 1)
                    dve.wait_ge(dve_A.sem, dve_A.at(g, "m8b"))
                    dve.memset(m8b[:, KSEL - 8:8], -7.0).then_inc(dve_A.sem, 1)
                    dve.wait_ge(dve_A.sem, dve_A.at(g, "fx"))
                    by_itself(dve)
                    dve.match_replace(sl2[:, :], m8b[:, :], sl1[:, :], -1.0).then_inc(dve_A.sem, 1)
                    dve.wait_ge(dve_A.sem, dve_A.at(g, "mr2"))
                    dve.tensor_scalar(mask[:, :], sl2[:, 0:T], 0.0, None, ALU.is_lt).then_inc(dve_A.sem, 1)
                    dve.wait_ge(dve_A.sem, dve_A.at(g, "mk"))
                    dve.tensor_tensor_scan(cum[:, :], kc("ones", GB), mask[:, :], 0.0, ALU.mult, ALU.add).then_inc(dve_A.sem, 1)
                    dve.wait_ge(dve_A.sem, dve_A.at(g, "cs"))
                    dve.tensor_tensor(srow[:, :], cum[:, :], mask[:, :], ALU.mult).then_inc(dve_A.sem, 1)
                else:
                    dve.wait_ge(pe_A.sem, pe_A.at(g, "st"))
                    col = psA[0:HALF, 400:400 + 2 * GB]
                    for d in range(2):
                        dve.tensor_tensor(Sg[:, :, d, :].rearrange("p k (b s) -> p k b s", b=GB),
                                          kb(col).unsqueeze(3).broadcast_to([HALF, 2, GB, KSEL]),
                                          kc("iota14", HALF).unsqueeze(1).unsqueeze(1).broadcast_to([HALF, 2, GB, KSEL]),
                                          ALU.is_equal).then_inc(dve_A.sem, 1)
                    dve.tensor_scalar(keep[:, :], col, 0.0, None, ALU.is_equal).then_inc(dve_A.sem, 1)
                    dve.scalar_tensor_tensor(out=ST[u][:, :, :], in0=psA[0:SLOTS, 0:T].unsqueeze(1).broadcast_to([SLOTS, GB, T]),
                                             scalar=kc("r1", SLOTS), in1=kc("bmt", SLOTS).unsqueeze(2).broadcast_to([SLOTS, GB, T]),
                                             op0=ALU.is_equal, op1=ALU.mult).then_inc(dve_A.sem, 1)

            def stage_K(g, u, part):
                if part == "v":
                    p, aux = features(u)
                    dve.tensor_tensor(sc["al"][:, :], sc["t1"][:, :], ry[:, NORM2], ALU.mult).then_inc(dve_K.sem, 1)
                    dve.tensor_tensor(sc["ky"][:, :], sc["t1"][:, :], keep[:, :], ALU.mult).then_inc(dve_K.sem, 1)
                    dve.wait_ge(dve_K.sem, dve_K.at(g, "al"))
                    dve.tensor_tensor(sc["kw"][:, :], sc["al"][:, :], keep[:, :], ALU.mult).then_inc(dve_K.sem, 1)
                    v = v26[:, :, :].rearrange("p (k b s) c -> p s k b c", k=2, b=GB)
                    dve.wait_ge(dve_K.sem, dve_K.at(g, "ky"))
                    dve.tensor_tensor(v[:, 1, :, :, 0:C], p, by_c(sc["ky"][:, :]), ALU.mult).then_inc(dve_K.sem, 1)
                    dve.wait_ge(dve_K.sem, dve_K.at(g, "kw"))
                    dve.tensor_tensor(v[:, 0, :, :, 0:C], p, by_c(sc["kw"][:, :]), ALU.mult).then_inc(dve_K.sem, 1)
                    dve.tensor_copy(v[:, 0, :, :, C], kb(keep[:, :])).then_inc(dve_K.sem, 1)
                    dve.tensor_tensor(v[:, 1, :, :, C], aux[:, :, :, 0], kb(keep[:, :]), ALU.mult).then_inc(dve_K.sem, 1)
                elif part == "d1":
                    dve.wait_ge(act_K.sem, act_K.at(g, "H"))
                    dve.tensor_tensor(d1[:, :, :], v26[:, :, :], SP[:, :, 0, :], ALU.subtract).then_inc(dve_K.sem, 1)
                else:
                    dve.wait_ge(act_K.sem, act_K.at(g, "M"))
                    dve.tensor_tensor(d2[:, :, :], d1[:, :, :], SP[:, :, 3, :], ALU.subtract).then_inc(dve_K.sem, 1)

            def stage_G(g, u, part):
                if part == "ga":
                    dve.wait_ge(pe_G.sem, pe_G.at(g, "ga"))
                    dve.tensor_tensor(ZY[:, :], psS[0:FR, 0, 0:SLOTS], kc("bmzy", FR), ALU.mult).then_inc(dve_G.sem, 1)
                    dve.tensor_scalar(RM[:, :], kc("iota", ROWS), psS[0:ROWS, 0, ZR:ZR + 1], NEG, ALU.is_gt, ALU.mult).then_inc(dve_G.sem, 1)
                    dve.tensor_tensor(dsm[:, :], psS[0:SLOTS, 0, ZR + 1:ZR + 1 + GB], kc("bmt", SLOTS), ALU.mult).then_inc(dve_G.sem, 1)
                    dve.wait_ge(dve_G.sem, dve_G.at(g, "dm"))
                    dve.tensor_reduce(dsel[:, :], dsm[:, :], AX.X, ALU.add).then_inc(dve_G.sem, 1)
                else:
                    dve.wait_ge(pe_G.sem, pe_G.at(g, "u"))
                    for k in range(2):
                        dve.tensor_tensor(UB[:, :, k, :], psS[0:ZR, 1 + k, 0:HP * SLOTS].rearrange("p (j s) -> p j s", j=HP),
                                          kc("bm2", ZR).unsqueeze(1).broadcast_to([ZR, HP, SLOTS]), ALU.mult).then_inc(dve_G.sem, 1)

            def stage_S(g, u, part):
                if part == "sc":
                    dve.wait_ge(pe_S.sem, pe_S.at(g, "sc"))
                    dve.wait_ge(dve_G.sem, dve_G.at(g, "rm"))
                    dve.tensor_tensor(Sm[:, :, :].rearrange("p (k j) t -> p k j t", k=3),
                                      psS[0:ROWS, :, 0:2 * T].rearrange("p k (j t) -> p k j t", j=2),
                                      RM[:, :].unsqueeze(1).unsqueeze(1).broadcast_to([ROWS, 3, 2, T]), ALU.add).then_inc(dve_S.sem, 1)
                    dve.wait_ge(dve_S.sem, dve_S.at(g, "sm"))
                    dve.tensor_reduce(mx[:, :], Sm[:, :, :], AX.X, ALU.max).then_inc(dve_S.sem, 1)
                    dve.wait_ge(dve_S.sem, dve_S.at(g, "mx"))
                    dve.tensor_scalar(nm[:, :], mx[:, :], -1.0, None, ALU.mult).then_inc(dve_S.sem, 1)
                elif part == "g":
                    dve.wait_ge(act_S.sem, act_S.at(g, "e5"))
                    dve.reciprocal(rinv[:, :], rsum[:, :]).then_inc(dve_S.sem, 1)
                    dve.wait_ge(pe_S.sem, pe_S.at(g, "g"))
                    dve.wait_ge(dve_S.sem, dve_S.at(g, "ri"))
                    dve.tensor_tensor(GN[:, :, :], psS[0:ROWS, 0, 0:HP * ZR].rearrange("p (j c) -> p j c", j=HP),
                                      rinv[:, :].unsqueeze(2).broadcast_to([ROWS, HP, ZR]), ALU.mult).then_inc(dve_S.sem, 1)
                elif part == "gt":
                    dve.wait_ge(pe_S.sem, pe_S.at(g, "gt"))
                    for k in range(2):
                        dve.tensor_tensor(G2[ZR * k:ZR * k + ZR, :, :].rearrange("p (i j) s -> p i j s", i=2),
                                          psS[0:ZR, 1:3, 0:3 * ROWS].rearrange("p i (j s) -> p i j s", j=3)[:, :, :, SLOTS * k:SLOTS * (k + 1)],
                                          kc("bm2", ZR).unsqueeze(1).unsqueeze(1).broadcast_to([ZR, 2, 3, SLOTS]), ALU.mult).then_inc(dve_S.sem, 1)
                else:
                    dve.wait_ge(pe_S.sem, pe_S.at(g, "at"))
                    dve.wait_ge(act_G.sem, act_G.at(g, "rs"))
                    if exists(g - 1):
                        dve.wait_ge(dve_C.sem, dve_C.at(g - 1, "os"))
                    dve.scalar_tensor_tensor(out=h1[:, :], in0=psS[0:SLOTS, 0, 0:D], scalar=dsel[:, 0:1], in1=res[:, :],
                                             op0=ALU.mult, op1=ALU.add).then_inc(dve_S.sem, 1)
                    dve.wait_ge(dve_S.sem, dve_S.at(g, "h1"))
                    dve.bn_stats(bst[:, :], h1[:, :]).then_inc(dve_S.sem, 1)
                    dve.wait_ge(dve_S.sem, dve_S.at(g, "bs"))
                    by_itself(dve)
                    dve.bn_aggr(mv[:, :], bst[:, :]).then_inc(dve_S.sem, 1)
                    dve.wait_ge(dve_S.sem, dve_S.at(g, "ba"))
                    dve.tensor_scalar(rx[0:SLOTS, NORMC], mv[:, 1:2], EPS, None, ALU.add).then_inc(dve_S.sem, 1)

            def stage_C(g, u, part):
                if part == "xh":
                    dve.tensor_scalar(xh[:, :], h1[:, :], mv[:, 0:1], ry[0:SLOTS, NORMC], ALU.subtract, ALU.mult).then_inc(dve_C.sem, 1)
                else:
                    dve.wait_ge(pe_C.sem, pe_C.at(g, "f2"))
                    dve.tensor_tensor(OS[u % 2][:, :], psC[0:SLOTS, 0:D], h1[:, :], ALU.add).then_inc(dve_C.sem, 1)

            def prepare(tile):
                if tile == 2:
                    weights_first()
                elif 3 <= tile <= 5:
                    weights_heads(tile - 3)
                elif 6 <= tile <= 7:
                    weights_attention("a4" if tile == 6 else "b2")
                elif tile == 8:
                    weights_ffn()
                elif 9 <= tile <= 10:
                    weights_parts("M" if tile == 9 else "R")

            plan = ["S gt 3", "C os 4", "L 0", "S at 3", "G ga 2", "L 1", "L 2", "G u 2", "L 3", "L 4", "A var 1", "R", "A z 1",
                    "C xh 3", "S sc 2", "A sel 1", "K v 2", "L 5", "A top 1", "K d1 2", "L 6", "A slots 1", "S g 2", "K d2 2",
                    "A var2 1"]
            stages = {"A": stage_A, "K": stage_K, "G": stage_G, "S": stage_S, "C": stage_C}

            def body(p, u, q):
                for what in plan:
                    if what[0] == "L":
                        if isinstance(p, int) and p < 2:
                            prepare(XT * p + int(what[2:]))
                        if active(p, 0):
                            sum_tile(p, u, int(what[2:]))
                    elif what == "R":
                        if active(p, 1) or active(p, 2) or active(p, 3):
                            rsqrt(p)
                    else:
                        stage, step, lag = what.split()
                        if active(p, int(lag)):
                            stages[stage](p - int(lag), (u - int(lag)) % 4, step)

            weights_zeroed()
            periods(nc.vector, body, 4)


def kernel(x, L0_tok_channel_weights, L0_attn_Wqkv_w, L0_attn_Wqkv_b, L0_attn_sel_w, L0_attn_sel_b, L0_attn_out_w,
           L0_attn_out_b, L0_attn_temperature, L0_ffn_in_weight, L0_ffn_in_bias, L0_ffn_out_weight):
    import concourse.bacc as bacc
    from concourse.bass_utils import run_bass_kernel_spmd as run

    e48, e13r = np.zeros((1, FR), np.float32), np.zeros((1, SK), np.float32)
    e48[0, Z1] = 1
    e13r[0, C::W1] = 1
    arrays = {
        "x": x, "cw": L0_tok_channel_weights, "wqkv": L0_attn_Wqkv_w, "bqkv": np.reshape(L0_attn_Wqkv_b, (1, -1)),
        "selw": L0_attn_sel_w, "selb": np.reshape(L0_attn_sel_b, (1, -1)), "ow": L0_attn_out_w,
        "ob": np.reshape(L0_attn_out_b, (1, -1)), "temp": np.reshape(L0_attn_temperature, (1, 1)),
        "w1t": np.transpose(L0_ffn_in_weight), "b1": np.reshape(L0_ffn_in_bias, (1, -1)), "w2": L0_ffn_out_weight,
        "consts": constants(), "e48": e48, "e13r": e13r,
    }
    arrays = {f"in_{k}": np.ascontiguousarray(v) for k, v in arrays.items()}
    nc = bacc.Bacc("TRN2", target_bir_lowering=False, num_devices=1)
    args = [nc.dram_tensor(k, v.shape, mybir.dt.from_np(v.dtype), kind="ExternalInput").ap() for k, v in arrays.items()]
    args.append(nc.dram_tensor("out_0", (B, T, D), mybir.dt.float32, kind="ExternalOutput").ap())
    program(nc, *args)
    return run(nc, [arrays], core_ids=[0]).results[0]["out_0"]
```
